# Optimizing a Trainium2 kernel written in Bass

```python
import numpy as np
import jax
import jax.numpy as jnp

def _softmax(x, axis=-1):
    return jax.nn.softmax(x, axis=axis)

def _gelu(x):
    return jax.nn.gelu(x, approximate=True)

def _silu(x):
    return jax.nn.silu(x)

def _sigmoid(x):
    return jax.nn.sigmoid(x)

def _layernorm(x, axis=-1, eps=1e-05):
    m = jnp.mean(x, axis=axis, keepdims=True)
    v = jnp.var(x, axis=axis, keepdims=True)
    return (x - m) / jnp.sqrt(v + eps)

def _scatter_add(tgt, idx, src, axis=0):
    return tgt.at[idx].add(src)

def _segment_sum(src, seg, n):
    return jax.ops.segment_sum(src, seg, n)
kernel_name = 'mk_decoder_preln_d2_seqx_r4_3fa9d4'

def setup_inputs(seed: int=0):
    np.random.seed(seed)
    _w = jnp.asarray

    def _rec_inputs():
        import jax
        import jax.numpy as jnp
        _rk = jax.random.key(seed)
        x = -0.0002928 + 1 * jax.random.normal(jax.random.fold_in(_rk, 1), (32, 100, 256), jnp.float32)
        _lenS = 100 - jax.random.randint(jax.random.fold_in(_rk, 7), (32,), 0, max(1, 100 // 4) + 1, jnp.int32)
        _lenS2 = 361 - jax.random.randint(jax.random.fold_in(_rk, 8), (32,), 0, max(1, 361 // 4) + 1, jnp.int32)
        _ctx_512P = jax.random.normal(jax.random.fold_in(_rk, 11), (32, 16, 128), jnp.float32)
        _ctx_512c = jax.random.dirichlet(jax.random.fold_in(_rk, 511), 0.3 * jnp.ones((16,), jnp.float32), (32, 361))
        _ctx_512t = jnp.einsum('bsk,bkd->bsd', _ctx_512c, _ctx_512P)
        _ctx_512t = _ctx_512t * jax.lax.rsqrt(jnp.mean(jnp.square(_ctx_512t)) + 1e-12) * 0.953939
        ctx_512 = -0.000514642 + 1.00011 * (_ctx_512t + 0.3 * jax.random.normal(jax.random.fold_in(_rk, 611), (32, 361, 128), jnp.float32))
        return (x, ctx_512)
    x, ctx_512 = _rec_inputs()

    def _L0_attn_setup():
        import jax, jax.numpy as jnp
        import numpy as np
        B, S, D, H, A = (2, 512, 256, 16, 64)
        INIT_STD = 0.02
        key = jax.random.key(seed)
        ks = jax.random.split(key, 5)
        return {'residual': jax.random.normal(ks[0], (B, S, D), dtype=jnp.float32), 'Wq': jax.random.normal(ks[1], (H, D, A), dtype=jnp.float32) * INIT_STD, 'Wk': jax.random.normal(ks[2], (H, D, A), dtype=jnp.float32) * INIT_STD, 'Wv': jax.random.normal(ks[3], (H, D, A), dtype=jnp.float32) * INIT_STD, 'Wo': jax.random.normal(ks[4], (H, A, D), dtype=jnp.float32) * INIT_STD, 'bq': jnp.zeros((H, A), dtype=jnp.float32), 'bk': jnp.zeros((H, A), dtype=jnp.float32), 'bv': jnp.zeros((H, A), dtype=jnp.float32), 'bo': jnp.zeros((D,), dtype=jnp.float32)}
    _L0_attn_all = _L0_attn_setup()
    _L0_attn_in = {k: v for k, v in _L0_attn_all.items() if k in ('Wq', 'Wk', 'Wv', 'Wo', 'bq', 'bk', 'bv', 'bo')}
    del _L0_attn_all

    def _L0_xattn_setup():
        import jax, jax.numpy as jnp
        import numpy as np
        DIM = 256
        LATENT_DIM = 128
        NUM_HEADS = 16
        HEAD_DIM = DIM // NUM_HEADS
        SCALE = HEAD_DIM ** (-0.5)
        key = jax.random.key(seed)
        k1, k2, k3, k4, k5 = jax.random.split(key, 5)
        B, xN, zN = (2, 512, 512)
        x = jax.random.normal(k1, (B, xN, DIM), dtype=jnp.float32)
        z = jax.random.normal(k2, (B, zN, LATENT_DIM), dtype=jnp.float32)
        Wq = jax.random.normal(k3, (DIM, DIM), dtype=jnp.float32) * DIM ** (-0.5)
        Wkv = jax.random.normal(k4, (2 * DIM, LATENT_DIM), dtype=jnp.float32) * LATENT_DIM ** (-0.5)
        Wo = jax.random.normal(k5, (DIM, DIM), dtype=jnp.float32) * DIM ** (-0.5)
        return {'x': x, 'z': z, 'Wq': Wq, 'Wkv': Wkv, 'Wo': Wo}
    _L0_xattn_all = _L0_xattn_setup()
    _L0_xattn_in = {k: v for k, v in _L0_xattn_all.items() if k in ('Wq', 'Wkv', 'Wo')}
    del _L0_xattn_all

    def _L0_ffn_setup():
        import jax, jax.numpy as jnp
        import numpy as np
        B, S = (4, 128)
        H = 256
        I = 704
        E = 8
        K = 2
        IS = 352
        key = jax.random.key(seed)
        ks = jax.random.split(key, 8)

        def init(k, shape, fan_in):
            return (jax.random.normal(k, shape, jnp.float32) / np.sqrt(fan_in)).astype(jnp.float32)
        return {'hidden_states': jax.random.normal(ks[0], (B, S, H), jnp.float32), 'gate_w': init(ks[1], (H, E), H), 'Wg': init(ks[2], (E, H, I), H), 'Wu': init(ks[3], (E, H, I), H), 'Wd': init(ks[4], (E, I, H), I), 'Sg': init(ks[5], (H, IS), H), 'Su': init(ks[6], (H, IS), H), 'Sd': init(ks[7], (IS, H), IS)}
    _L0_ffn_all = _L0_ffn_setup()
    _L0_ffn_in = {k: v for k, v in _L0_ffn_all.items() if k in ('gate_w', 'Wg', 'Wu', 'Wd', 'Sg', 'Su', 'Sd')}
    del _L0_ffn_all

    def _L1_attn_setup():
        import jax, jax.numpy as jnp
        import numpy as np
        N_HEADS = 16
        D_EMBD = 256
        B, T = (2, 512)
        key = jax.random.key(seed)
        k1, k2, k3 = jax.random.split(key, 3)
        x = jax.random.normal(k1, (B, T, D_EMBD), dtype=jnp.float32)
        W1 = jax.random.normal(k2, (D_EMBD, 3 * D_EMBD), dtype=jnp.float32) / np.sqrt(D_EMBD)
        b1 = jnp.zeros((3 * D_EMBD,), dtype=jnp.float32)
        W2 = jax.random.normal(k3, (D_EMBD, D_EMBD), dtype=jnp.float32) / np.sqrt(D_EMBD)
        b2 = jnp.zeros((D_EMBD,), dtype=jnp.float32)
        return {'x': x, 'W1': W1, 'b1': b1, 'W2': W2, 'b2': b2}
    _L1_attn_all = _L1_attn_setup()
    _L1_attn_in = {k: v for k, v in _L1_attn_all.items() if k in ('W1', 'b1', 'W2', 'b2')}
    del _L1_attn_all

    def _L1_xattn_setup():
        import jax, jax.numpy as jnp
        import numpy as np
        NUM_HEADS = 16
        HEAD_DIM = 64
        Q_DIM = 256
        KV_DIM = 128
        INNER = NUM_HEADS * HEAD_DIM
        key = jax.random.key(seed)
        ks = jax.random.split(key, 7)
        B, N, M = (32, 128, 512)
        q = jax.random.normal(ks[0], (B, N, Q_DIM), dtype=jnp.float32)
        kv = jax.random.normal(ks[1], (B, M, KV_DIM), dtype=jnp.float32)
        Wq = jax.random.normal(ks[2], (Q_DIM, INNER), dtype=jnp.float32) / np.sqrt(Q_DIM)
        Wk = jax.random.normal(ks[3], (KV_DIM, INNER), dtype=jnp.float32) / np.sqrt(KV_DIM)
        Wv = jax.random.normal(ks[4], (KV_DIM, INNER), dtype=jnp.float32) / np.sqrt(KV_DIM)
        Wo = jax.random.normal(ks[5], (INNER, Q_DIM), dtype=jnp.float32) / np.sqrt(INNER)
        bo = jax.random.normal(ks[6], (Q_DIM,), dtype=jnp.float32) * 0.01
        return {'q': q, 'kv': kv, 'Wq': Wq, 'Wk': Wk, 'Wv': Wv, 'Wo': Wo, 'bo': bo}
    _L1_xattn_all = _L1_xattn_setup()
    _L1_xattn_in = {k: v for k, v in _L1_xattn_all.items() if k in ('Wq', 'Wk', 'Wv', 'Wo', 'bo')}
    del _L1_xattn_all

    def _L1_ffn_setup():
        import jax, jax.numpy as jnp
        import numpy as np
        E, K, NG, TG = (64, 8, 8, 4)
        CAP = 256
        SCALE = 2.5

        def _route(x_flat, gate_weight, e_bias):
            T = x_flat.shape[0]
            logits = x_flat.astype(jnp.float32) @ gate_weight.astype(jnp.float32).T
            scores = jax.nn.sigmoid(logits)
            sfc = scores + e_bias[None, :]
            group_scores = jax.lax.top_k(sfc.reshape(T, NG, E // NG), 2)[0].sum(-1)
            _, gidx = jax.lax.top_k(group_scores, TG)
            gmask = jnp.zeros((T, NG), jnp.float32).at[jnp.arange(T)[:, None], gidx].set(1.0)
            smask = jnp.repeat(gmask, E // NG, axis=1)
            tmp = jnp.where(smask > 0, sfc, 0.0)
            _, topk_idx = jax.lax.top_k(tmp, K)
            topk_w = jnp.take_along_axis(scores, topk_idx, axis=1)
            topk_w = topk_w / (topk_w.sum(-1, keepdims=True) + 1e-20)
            return (topk_idx, topk_w * SCALE)

        def _moe_forward(hidden_states, gate_weight, e_bias, w1, w2, w3, shared_gate, shared_up, shared_down):
            B, S, H = hidden_states.shape
            T = B * S
            x = hidden_states.reshape(T, H)
            topk_idx, topk_w = _route(x, gate_weight, e_bias)
            Sk = T * K
            flat_e = topk_idx.reshape(-1)
            order = jnp.argsort(flat_e)
            sorted_e = flat_e[order]
            counts = jax.ops.segment_sum(jnp.ones((Sk,), jnp.int32), flat_e, num_segments=E)
            offsets = jnp.cumsum(counts) - counts
            pos = jnp.arange(Sk) - offsets[sorted_e]
            tok_sorted = x[order // K]
            xe = jnp.zeros((E, CAP, H), x.dtype).at[sorted_e, pos].set(tok_sorted, mode='drop')
            h = jax.nn.silu(jnp.einsum('ech,efh->ecf', xe, w1)) * jnp.einsum('ech,efh->ecf', xe, w3)
            ye = jnp.einsum('ecf,ehf->ech', h, w2)
            pos_c = jnp.minimum(pos, CAP - 1)
            vals = ye[sorted_e, pos_c]
            vals = jnp.where((pos < CAP)[:, None], vals, 0.0)
            flat_w = topk_w.reshape(-1)[order].astype(vals.dtype)
            flat_t = (jnp.arange(Sk) // K)[order]
            out = jax.ops.segment_sum(vals * flat_w[:, None], flat_t, num_segments=T)
            shared = jax.nn.silu(x @ shared_gate.T) * (x @ shared_up.T) @ shared_down.T
            return (out + shared).reshape(B, S, H)
        key = jax.random.key(seed)
        ks = jax.random.split(key, 9)
        B, S, H, F = (1, 512, 256, 128)
        bound = 1.0 / 32.0
        return {'hidden_states': jax.random.normal(ks[0], (B, S, H), jnp.float32), 'gate_weight': jax.random.uniform(ks[1], (E, H), jnp.float32, -bound, bound), 'e_bias': jnp.zeros((E,), jnp.float32), 'w1': jax.random.normal(ks[2], (E, F, H), jnp.float32) * 0.02, 'w2': jax.random.normal(ks[3], (E, H, F), jnp.float32) * 0.02, 'w3': jax.random.normal(ks[4], (E, F, H), jnp.float32) * 0.02, 'shared_gate': jax.random.normal(ks[5], (2 * F, H), jnp.float32) * 0.02, 'shared_up': jax.random.normal(ks[6], (2 * F, H), jnp.float32) * 0.02, 'shared_down': jax.random.normal(ks[7], (H, 2 * F), jnp.float32) * 0.02}
    _L1_ffn_all = _L1_ffn_setup()
    _L1_ffn_in = {k: v for k, v in _L1_ffn_all.items() if k in ('gate_weight', 'e_bias', 'w1', 'w2', 'w3', 'shared_gate', 'shared_up', 'shared_down')}
    del _L1_ffn_all
    return {'x': x, 'ctx_512': ctx_512, 'L0_attn_Wq': _L0_attn_in['Wq'], 'L0_attn_Wk': _L0_attn_in['Wk'], 'L0_attn_Wv': _L0_attn_in['Wv'], 'L0_attn_Wo': _L0_attn_in['Wo'], 'L0_attn_bq': _L0_attn_in['bq'], 'L0_attn_bk': _L0_attn_in['bk'], 'L0_attn_bv': _L0_attn_in['bv'], 'L0_attn_bo': _L0_attn_in['bo'], 'L0_xattn_Wq': _L0_xattn_in['Wq'], 'L0_xattn_Wkv': _L0_xattn_in['Wkv'], 'L0_xattn_Wo': _L0_xattn_in['Wo'], 'L0_ffn_gate_w': _L0_ffn_in['gate_w'], 'L0_ffn_Wg': _L0_ffn_in['Wg'], 'L0_ffn_Wu': _L0_ffn_in['Wu'], 'L0_ffn_Wd': _L0_ffn_in['Wd'], 'L0_ffn_Sg': _L0_ffn_in['Sg'], 'L0_ffn_Su': _L0_ffn_in['Su'], 'L0_ffn_Sd': _L0_ffn_in['Sd'], 'L1_attn_W1': _L1_attn_in['W1'], 'L1_attn_b1': _L1_attn_in['b1'], 'L1_attn_W2': _L1_attn_in['W2'], 'L1_attn_b2': _L1_attn_in['b2'], 'L1_xattn_Wq': _L1_xattn_in['Wq'], 'L1_xattn_Wk': _L1_xattn_in['Wk'], 'L1_xattn_Wv': _L1_xattn_in['Wv'], 'L1_xattn_Wo': _L1_xattn_in['Wo'], 'L1_xattn_bo': _L1_xattn_in['bo'], 'L1_ffn_gate_weight': _L1_ffn_in['gate_weight'], 'L1_ffn_e_bias': _L1_ffn_in['e_bias'], 'L1_ffn_w1': _L1_ffn_in['w1'], 'L1_ffn_w2': _L1_ffn_in['w2'], 'L1_ffn_w3': _L1_ffn_in['w3'], 'L1_ffn_shared_gate': _L1_ffn_in['shared_gate'], 'L1_ffn_shared_up': _L1_ffn_in['shared_up'], 'L1_ffn_shared_down': _L1_ffn_in['shared_down']}

def reference(x, ctx_512, L0_attn_Wq, L0_attn_Wk, L0_attn_Wv, L0_attn_Wo, L0_attn_bq, L0_attn_bk, L0_attn_bv, L0_attn_bo, L0_xattn_Wq, L0_xattn_Wkv, L0_xattn_Wo, L0_ffn_gate_w, L0_ffn_Wg, L0_ffn_Wu, L0_ffn_Wd, L0_ffn_Sg, L0_ffn_Su, L0_ffn_Sd, L1_attn_W1, L1_attn_b1, L1_attn_W2, L1_attn_b2, L1_xattn_Wq, L1_xattn_Wk, L1_xattn_Wv, L1_xattn_Wo, L1_xattn_bo, L1_ffn_gate_weight, L1_ffn_e_bias, L1_ffn_w1, L1_ffn_w2, L1_ffn_w3, L1_ffn_shared_gate, L1_ffn_shared_up, L1_ffn_shared_down):
    import jax
    import jax.numpy as jnp

    def _L0_attn_ref(residual, Wq, Wk, Wv, Wo, bq, bk, bv, bo):
        import jax, jax.numpy as jnp
        import numpy as np
        B, S, D, H, A = (2, 512, 256, 16, 64)
        INIT_STD = 0.02
        q = jnp.einsum('bsd,hda->bhsa', residual, Wq) + bq[None, :, None, :]
        k = jnp.einsum('bsd,hda->bhsa', residual, Wk) + bk[None, :, None, :]
        v = jnp.einsum('bsd,hda->bhsa', residual, Wv) + bv[None, :, None, :]
        scale = 1.0 / jnp.sqrt(jnp.float32(q.shape[-1]))
        scores = jnp.einsum('bhsa,bhta->bhst', q, k) * scale
        s = scores.shape[-1]
        causal = jnp.tril(jnp.ones((s, s), dtype=bool))
        masked = jnp.where(causal, scores, jnp.float32(-100000.0))
        pattern = jax.nn.softmax(masked, axis=-1)
        z = jnp.einsum('bhst,bhta->bshа'.replace('а', 'a'), pattern, v)
        out = jnp.einsum('bsha,had->bsd', z, Wo) + bo
        return out

    def _L0_xattn_ref(x, z, Wq, Wkv, Wo):
        import jax, jax.numpy as jnp
        import numpy as np
        DIM = 256
        LATENT_DIM = 128
        NUM_HEADS = 16
        HEAD_DIM = DIM // NUM_HEADS
        SCALE = HEAD_DIM ** (-0.5)
        B, xN, _ = x.shape
        _, zN, _ = z.shape
        Q = (x @ Wq.T).reshape(B, xN, NUM_HEADS, HEAD_DIM)
        KV = (z @ Wkv.T).reshape(B, zN, 2, NUM_HEADS, HEAD_DIM)
        K = KV[:, :, 0]
        V = KV[:, :, 1]
        attn = jnp.einsum('bqhd,bkhd->bhqk', Q, K) * SCALE
        attn = jax.nn.softmax(attn, axis=-1)
        O = jnp.einsum('bhqk,bkhd->bqhd', attn, V).reshape(B, xN, DIM)
        return O @ Wo.T

    def _L0_ffn_ref(hidden_states, gate_w, Wg, Wu, Wd, Sg, Su, Sd):
        import jax, jax.numpy as jnp
        import numpy as np
        B, S = (4, 128)
        H = 256
        I = 704
        E = 8
        K = 2
        IS = 352
        b, s, h = hidden_states.shape
        x = hidden_states.reshape(-1, h)
        T = x.shape[0]
        logits = x @ gate_w
        top_v, top_i = jax.lax.top_k(logits, K)
        top_p = jax.nn.softmax(top_v, axis=-1)
        combine = jnp.zeros((T, E), x.dtype).at[jnp.arange(T)[:, None], top_i].add(top_p)
        g = jnp.einsum('th,ehi->tei', x, Wg)
        u = jnp.einsum('th,ehi->tei', x, Wu)
        d = jnp.einsum('tei,eih->teh', jax.nn.silu(g) * u, Wd)
        expert_out = jnp.einsum('te,teh->th', combine, d)
        shared = jax.nn.silu(x @ Sg) * (x @ Su) @ Sd
        return (expert_out + shared).reshape(b, s, h)

    def _L1_attn_ref(x, W1, b1, W2, b2):
        import jax, jax.numpy as jnp
        import numpy as np
        N_HEADS = 16
        D_EMBD = 256
        B, T = (2, 512)
        bs, t, d = x.shape
        h = N_HEADS
        kqv = x @ W1 + b1
        k, q, v = jnp.split(kqv, 3, axis=-1)

        def to_heads(z):
            return z.reshape(bs, t, h, d // h).transpose(0, 2, 1, 3)
        k, q, v = (to_heads(k), to_heads(q), to_heads(v))
        mask = jnp.tril(jnp.ones((t, t), dtype=bool))
        attn = jnp.where(mask, jnp.einsum('bhqd,bhkd->bhqk', q, k), 0.0)
        out = jnp.einsum('bhqk,bhkd->bhqd', attn, v)
        out = out.transpose(0, 2, 1, 3).reshape(bs, t, d)
        return out @ W2 + b2

    def _L1_xattn_ref(q, kv, Wq, Wk, Wv, Wo, bo):
        import jax, jax.numpy as jnp
        import numpy as np
        NUM_HEADS = 16
        HEAD_DIM = 64
        Q_DIM = 256
        KV_DIM = 128
        INNER = NUM_HEADS * HEAD_DIM
        B, N, _ = q.shape
        M = kv.shape[1]
        scale = HEAD_DIM ** (-0.5)
        qh = (q @ Wq).reshape(B, N, NUM_HEADS, HEAD_DIM).transpose(0, 2, 1, 3)
        kh = (kv @ Wk).reshape(B, M, NUM_HEADS, HEAD_DIM).transpose(0, 2, 1, 3)
        vh = (kv @ Wv).reshape(B, M, NUM_HEADS, HEAD_DIM).transpose(0, 2, 1, 3)
        scores = jnp.einsum('bhnd,bhmd->bhnm', qh, kh) * scale
        attn = jax.nn.softmax(scores, axis=-1)
        out = jnp.einsum('bhnm,bhmd->bhnd', attn, vh)
        out = out.transpose(0, 2, 1, 3).reshape(B, N, INNER)
        return out @ Wo + bo

    def _L1_ffn_ref(hidden_states, gate_weight, e_bias, w1, w2, w3, shared_gate, shared_up, shared_down):
        import jax, jax.numpy as jnp
        import numpy as np
        E, K, NG, TG = (64, 8, 8, 4)
        CAP = 256
        SCALE = 2.5

        def _route(x_flat, gate_weight, e_bias):
            T = x_flat.shape[0]
            logits = x_flat.astype(jnp.float32) @ gate_weight.astype(jnp.float32).T
            scores = jax.nn.sigmoid(logits)
            sfc = scores + e_bias[None, :]
            group_scores = jax.lax.top_k(sfc.reshape(T, NG, E // NG), 2)[0].sum(-1)
            _, gidx = jax.lax.top_k(group_scores, TG)
            gmask = jnp.zeros((T, NG), jnp.float32).at[jnp.arange(T)[:, None], gidx].set(1.0)
            smask = jnp.repeat(gmask, E // NG, axis=1)
            tmp = jnp.where(smask > 0, sfc, 0.0)
            _, topk_idx = jax.lax.top_k(tmp, K)
            topk_w = jnp.take_along_axis(scores, topk_idx, axis=1)
            topk_w = topk_w / (topk_w.sum(-1, keepdims=True) + 1e-20)
            return (topk_idx, topk_w * SCALE)

        def _moe_forward(hidden_states, gate_weight, e_bias, w1, w2, w3, shared_gate, shared_up, shared_down):
            B, S, H = hidden_states.shape
            T = B * S
            x = hidden_states.reshape(T, H)
            topk_idx, topk_w = _route(x, gate_weight, e_bias)
            Sk = T * K
            flat_e = topk_idx.reshape(-1)
            order = jnp.argsort(flat_e)
            sorted_e = flat_e[order]
            counts = jax.ops.segment_sum(jnp.ones((Sk,), jnp.int32), flat_e, num_segments=E)
            offsets = jnp.cumsum(counts) - counts
            pos = jnp.arange(Sk) - offsets[sorted_e]
            tok_sorted = x[order // K]
            xe = jnp.zeros((E, CAP, H), x.dtype).at[sorted_e, pos].set(tok_sorted, mode='drop')
            h = jax.nn.silu(jnp.einsum('ech,efh->ecf', xe, w1)) * jnp.einsum('ech,efh->ecf', xe, w3)
            ye = jnp.einsum('ecf,ehf->ech', h, w2)
            pos_c = jnp.minimum(pos, CAP - 1)
            vals = ye[sorted_e, pos_c]
            vals = jnp.where((pos < CAP)[:, None], vals, 0.0)
            flat_w = topk_w.reshape(-1)[order].astype(vals.dtype)
            flat_t = (jnp.arange(Sk) // K)[order]
            out = jax.ops.segment_sum(vals * flat_w[:, None], flat_t, num_segments=T)
            shared = jax.nn.silu(x @ shared_gate.T) * (x @ shared_up.T) @ shared_down.T
            return (out + shared).reshape(B, S, H)
        return _moe_forward(hidden_states, gate_weight, e_bias, w1, w2, w3, shared_gate, shared_up, shared_down)
    x = x + _L0_attn_ref(_layernorm(x, axis=-1), L0_attn_Wq, L0_attn_Wk, L0_attn_Wv, L0_attn_Wo, L0_attn_bq, L0_attn_bk, L0_attn_bv, L0_attn_bo)
    x = x + _L0_xattn_ref(_layernorm(x, axis=-1), ctx_512, L0_xattn_Wq, L0_xattn_Wkv, L0_xattn_Wo)
    x = x + _L0_ffn_ref(_layernorm(x, axis=-1), L0_ffn_gate_w, L0_ffn_Wg, L0_ffn_Wu, L0_ffn_Wd, L0_ffn_Sg, L0_ffn_Su, L0_ffn_Sd)
    x = x + _L1_attn_ref(_layernorm(x, axis=-1), L1_attn_W1, L1_attn_b1, L1_attn_W2, L1_attn_b2)
    x = x + _L1_xattn_ref(_layernorm(x, axis=-1), ctx_512, L1_xattn_Wq, L1_xattn_Wk, L1_xattn_Wv, L1_xattn_Wo, L1_xattn_bo)
    x = x + _L1_ffn_ref(_layernorm(x, axis=-1), L1_ffn_gate_weight, L1_ffn_e_bias, L1_ffn_w1, L1_ffn_w2, L1_ffn_w3, L1_ffn_shared_gate, L1_ffn_shared_up, L1_ffn_shared_down)
    return x

_drawn_inputs = setup_inputs


def setup_inputs(seed=0):
    import zlib

    import numpy as np

    out = dict(_drawn_inputs(seed))
    spreads = {'L0_attn_bq': (0.0, 0.744),
     'L0_attn_bk': (0.0, 2.0),
     'L0_attn_bv': (0.0, 0.1),
     'L0_attn_bo': (0.0, 0.1),
     'L1_attn_b1': (0.0, 0.1),
     'L1_attn_b2': (0.0, 0.8),
     'L1_ffn_e_bias': (0.0, 0.8)}
    factors = {'L0_attn_Wq': 4.344,
     'L0_attn_Wk': 3.543,
     'L1_xattn_Wq': 8.0,
     'L1_xattn_Wk': 8.0,
     'L1_xattn_Wv': 5.408,
     'L1_xattn_Wo': 5.413,
     'L1_xattn_bo': 200.0,
     'L1_ffn_gate_weight': 8.0,
     'L1_ffn_w1': 8.0,
     'L1_ffn_w2': 8.0,
     'L1_ffn_w3': 8.0,
     'L1_ffn_shared_gate': 8.0,
     'L1_ffn_shared_up': 8.0,
     'L1_ffn_shared_down': 8.0}
    for name, (base, spread) in spreads.items():
        noise = np.random.default_rng([zlib.crc32(name.encode()), seed]).standard_normal(out[name].shape)
        drawn = base * np.exp(spread * noise) if base else spread * noise
        out[name] = jnp.asarray(drawn.astype(out[name].dtype))
    for name, factor in factors.items():
        out[name] = (out[name] * factor).astype(out[name].dtype)
    return out
```

```python
from contextlib import ExitStack

import concourse.bass as bass
from concourse import mybir

F32 = mybir.dt.float32
I32 = mybir.dt.int32
U32 = mybir.dt.uint32
ALU = mybir.AluOpType
ACT = mybir.ActivationFunctionType
AX = mybir.AxisListType

LAST_STAGE = 6

B, S, D = 32, 100, 256
KC = D // 128
H = 16
CTX, CTXD = 361, 128
EPS = 1e-5
MASKED = -100000.0


class Shared:

    def __init__(self, nc, sem):
        self.nc, self.sem = nc, sem


class Banks:

    def __init__(self, k, first, n):
        self.PS, self.first, self.n, self.uses = k.PS, first, n, k.uses
        self.filled, self.moved = k.filled[first:first + n], k.moved[first:first + n]

    def plan(self, names):
        self.bank = {name: n % self.n for n, name in enumerate(names)}
        self.order = {name: n // self.n for n, name in enumerate(names)}
        self.per = [len(range(b, len(names), self.n)) for b in range(self.n)]
        assert len(self.bank) == len(names)
        self.base = self.uses[self.first:self.first + self.n]
        return self

    def done(self, turns):
        for b in range(self.n):
            self.uses[self.first + b] += turns * self.per[b]

    def at(self, name, p, *shape):
        n = 1
        for q in shape:
            n *= q
        flat = self.PS[0:p, self.first + self.bank[name], 0:n]
        if len(shape) == 2:
            return flat.rearrange("p (a b) -> p a b", a=shape[0])
        if len(shape) == 3:
            return flat.rearrange("p (a b c) -> p a b c", a=shape[0], b=shape[1])
        return flat

    def before(self, name, i):
        b = self.bank[name]
        return i * self.per[b] + (self.base[b] + self.order[name])

    def wait_free(self, pe, name, i, *moved):
        last = {self.bank[name]: self.order[name]}
        for m in moved:
            b = self.bank[m]
            last[b] = max(last.get(b, 0), self.order[m] + 1)
        for b, n in last.items():
            pe.wait_ge(self.moved[b], i * self.per[b] + (self.base[b] + n + 1))

    def fill_done(self, ins, name):
        ins.then_inc(self.filled[self.bank[name]], 1)

    def wait_full(self, eng, name, i):
        eng.wait_ge(self.filled[self.bank[name]], self.before(name, i) + 1)

    def move_done(self, ins, name):
        ins.then_inc(self.moved[self.bank[name]], 1)

    def wait_moved(self, eng, i, *names):
        last = {}
        for m in names:
            last[self.bank[m]] = max(last.get(self.bank[m], 0), self.order[m])
        for b, n in last.items():
            eng.wait_ge(self.moved[b], i * self.per[b] + (self.base[b] + n + 2))


def layer_norm(dve, ln, step, t, i, xs, stored=None):
    for u, x in enumerate(xs):
        step.done(dve.bn_stats(ln.stats[:, u, :], x))
    step.wait(dve, i)
    dve.sem_inc(ln.passed, 1)
    for u in range(len(xs)):
        step.done(dve.bn_aggr(ln.mv[:, u, :], ln.stats[:, u, :]))
    step.wait(dve, i)
    dve.tensor_scalar(ln.var[:], ln.mv[:, :, 1], EPS, None, ALU.add).then_inc(ln.var_ready, 1)
    dve.wait_ge(ln.rstd_ready, t + 1)
    if stored is not None:
        dve.wait_ge(stored, t * 16)
    for u, x in enumerate(xs):
        dve.tensor_scalar(ln.xn[:, u, :], x, ln.mv[:, u, 0:1], ln.rstd[:, u:u + 1],
                          ALU.subtract, ALU.mult).then_inc(ln.xn_ready, 1)


LN_STEPS = 4


def layer_norm_rstd(pool, ln, t):
    pool.wait_ge(ln.var_ready, t + 1)
    pool.tensor_tensor(ln.rstd[:], ln.var[:], ln.half[:], ALU.pow).then_inc(ln.rstd_ready, 1)


class Chain:

    def __init__(self, sem, per):
        self.sem, self.per, self.n = sem, per, 0

    def done(self, ins):
        self.n += 1
        ins.then_inc(self.sem, 1)

    def wait(self, eng, i):
        eng.wait_ge(self.sem, i * self.per + self.n)

    def link(self, eng, i, ins):
        self.done(ins)
        self.wait(eng, i)

    def end(self):
        assert self.n == self.per, (self.n, self.per)


class Norm:

    def __init__(self, sb, sem, name, half):
        self.half = half
        self.stats, self.mv = sb(name + "_stats", [S, 2, 6]), sb(name + "_mv", [S, 2, 2])
        self.var, self.rstd = sb(name + "_var", [S, 2]), sb(name + "_rstd", [S, 2])
        self.xn = sb(name + "_xn", [S, 2, D])
        self.var_ready, self.rstd_ready = sem(name + "_var_ready"), sem(name + "_rstd_ready")
        self.xn_ready, self.passed = sem(name + "_xn_ready"), sem(name + "_wait_passed")


def turn_norm(pe, k, ln, xb, t):
    xb.wait_free(pe, "xT", t)
    pe.wait_ge(ln.xn_ready, t * 2 + 2)
    for c in range(KC):
        for u in range(2):
            last = pe.transpose(xb.at("xT", 128, KC, 2, S)[:, c, u, :],
                                ln.xn[:, u, c * 128:(c + 1) * 128], k.ident[0:S, 0:S])
    xb.fill_done(last, "xT")


def self_attention(k, w):
    nc, X = k.nc, k.X
    A = 64
    T = H * A // 128
    TURNS = B // 2
    GH = 4
    G = H // GH
    with ExitStack() as ctx:
        def sb(name, shape):
            return ctx.enter_context(nc.sbuf_tensor(name, shape, F32))

        sem = k.sem
        wq, wk, wv = (sb(n, [128, KC, H * A]) for n in ("a_wq", "a_wk", "a_wv"))
        wo = sb("a_wo", [128, T, D])
        bq, bk = sb("a_bq", [128, T]), sb("a_bk", [128, T])
        bv, bo = sb("a_bv", [S, H, A]), sb("a_bo", [S, D])
        ln = Norm(sb, sem, "a", k.half)
        xT = sb("a_xT", [128, KC, 2, S])
        qT = sb("a_qT", [128, T, 2 * S])
        kT = sb("a_kT", [128, T, 2, 2 * S])
        v = sb("a_v", [S, 2, H, A + 1])
        sm = sb("a_sm", [S, 2, G, GH, S])
        mx = sb("a_mx", [S, 2, G, GH])
        pT = sb("a_pT", [S, 2, G, GH, S])
        den = sb("a_den", [S, 2, G, GH])
        o = sb("a_o", [S, 2, H * A])
        oT = sb("a_oT", [128, 2, T, S])
        loaded, prepared = sem("a_loaded"), sem("a_prepared")
        shifted, exped, bq_scaled = sem("a_shifted"), sem("a_exped"), sem("a_bq_scaled")
        chain = Chain(sem("a_dve_step"), LN_STEPS + 2 + 4 * G)
        banks, xb = Banks(k, 0, 7), Banks(k, 7, 1).plan(["xT"])
        names = ([f"q{j}" for j in range(T // 2)] + [f"k{j}" for j in range(T // 2)]
                 + [f"v{u}{c}" for u in range(2) for c in range(2)]
                 + [f"s{u}{g}" for u in range(2) for g in range(G)])
        for u in range(2):
            for g in range(G):
                names.append(f"p{u}{g}")
                if g:
                    names.append(f"o{u}{g - 1}")
            names.append(f"o{u}{G - 1}")
        names += [f"t{u}{c}" for u in range(2) for c in range(2)] + ["y0", "y1"]
        banks.plan(names)
        bank = banks.at

        with nc.Block() as block:
            @block.sync
            def _(sp):
                for t, src in ((wq, w["Wq"]), (wk, w["Wk"]), (wv, w["Wv"])):
                    sp.dma_start(t[:], src.rearrange("(c p) n -> p c n", p=128)).then_inc(loaded, 16)
                sp.dma_start(wo[:], w["Wo"].rearrange("(t p) n -> p t n", p=128)).then_inc(loaded, 16)
                for t, src in ((bq, w["bq"]), (bk, w["bk"])):
                    sp.dma_start(t[:], src).then_inc(loaded, 16)
                sp.dma_start(bv[:].rearrange("p h a -> p (h a)"), w["bv"].partition_broadcast(S)).then_inc(loaded, 16)
                sp.dma_start(bo[:], w["bo"].partition_broadcast(S)).then_inc(loaded, 16)

            LOADED = 8 * 16

            @block.gpsimd
            def _(pool):
                pool.memset(v[:, :, :, A:A + 1], 1.0).then_inc(prepared, 1)
                pool.wait_ge(prepared, 1)
                pool.memset(kT[:], 0.0).then_inc(prepared, 1)
                layer_norm_rstd(pool, ln, 0)
                with pool.Fori(0, TURNS) as i:
                    layer_norm_rstd(pool, ln, i + 1)

            @block.tensor
            def _(pe):
                pe.wait_ge(loaded, LOADED)
                pe.wait_ge(prepared, 2)
                turn_norm(pe, k, ln, xb, 0)
                with pe.Fori(0, TURNS) as i:
                    xb.wait_moved(pe, i, "xT")
                    for nm, wt in (("q", wq), ("k", wk)):
                        for j in range(T // 2):
                            name = f"{nm}{j}"
                            banks.wait_free(pe, name, i)
                            for t in range(2):
                                for c in range(KC):
                                    m = (2 * j + t) * 128
                                    last = pe.matmul(bank(name, 128, 2, 2 * S)[:, t, :], wt[:, c, m:m + 128],
                                                     xT[:, c].rearrange("p u s -> p (u s)"),
                                                     start=(c == 0), stop=(c == KC - 1))
                            banks.fill_done(last, name)
                    for u in range(2):
                        for half in range(2):
                            name = f"v{u}{half}"
                            banks.wait_free(pe, name, i)
                            for c in range(KC):
                                last = pe.matmul(bank(name, S, 512), xT[:, c, u, :],
                                                 wv[:, c, half * 512:(half + 1) * 512],
                                                 start=(c == 0), stop=(c == KC - 1))
                            banks.fill_done(last, name)
                    for u in range(2):
                        for g in range(G):
                            banks.wait_free(pe, f"s{u}{g}", i, f"q{g}", f"k{g}")
                            for t in range(GH // 2):
                                cols = slice(u * S, (u + 1) * S)
                                last = pe.matmul(bank(f"s{u}{g}", S, GH, S)[:, 2 * t:2 * t + 2, :],
                                                 qT[:, 2 * g + t, cols], kT[:, 2 * g + t, :, cols],
                                                 start=True, stop=True)
                            banks.fill_done(last, f"s{u}{g}")

                    def turn_probs(u, g):
                        name = f"p{u}{g}"
                        banks.wait_free(pe, name, i)
                        pe.wait_ge(exped, i * (2 * G) + (u * G + g + 1))
                        for n in range(GH):
                            last = pe.transpose(bank(name, S, GH, S)[:, n, :], sm[:, u, g, n, :],
                                                k.ident[0:S, 0:S])
                        banks.fill_done(last, name)

                    def weigh(u, g):
                        name = f"o{u}{g}"
                        banks.wait_free(pe, name, i, f"v{u}{g // 2}", f"p{u}{g}")
                        for n in range(GH):
                            last = pe.matmul(bank(name, S, GH, A + 1)[:, n, :], pT[:, u, g, n, :],
                                             v[:, u, g * GH + n, :], start=True, stop=True)
                        banks.fill_done(last, name)

                    for u in range(2):
                        for g in range(G):
                            turn_probs(u, g)
                            if g:
                                weigh(u, g - 1)
                        weigh(u, G - 1)
                    for u in range(2):
                        for half in range(2):
                            name = f"t{u}{half}"
                            banks.wait_free(pe, name, i, f"o{u}{2 * half}", f"o{u}{2 * half + 1}")
                            for t in range(4):
                                m = (half * 4 + t) * 128
                                last = pe.transpose(bank(name, 128, 4, S)[:, t, :], o[:, u, m:m + 128],
                                                    k.ident[0:S, 0:S])
                            banks.fill_done(last, name)
                    turn_norm(pe, k, ln, xb, i + 1)
                    for u in range(2):
                        name = f"y{u}"
                        banks.wait_free(pe, name, i, f"t{u}0", f"t{u}1")
                        for t in range(T):
                            last = pe.matmul(bank(name, S, D), oT[:, u, t, :], wo[:, t, :],
                                             start=(t == 0), stop=(t == T - 1))
                        banks.fill_done(last, name)

            @block.scalar
            def _(act):
                act.wait_ge(loaded, LOADED)
                act.wait_ge(prepared, 2)

                def move_norm(t):
                    xb.wait_full(act, "xT", t)
                    xb.move_done(act.activation(xT[:], xb.at("xT", 128, KC, 2, S), ACT.Copy), "xT")

                move_norm(0)
                with act.Fori(0, TURNS) as i:
                    for j in range(T // 2):
                        name = f"k{j}"
                        banks.wait_full(act, name, i)
                        for t in range(2):
                            for r in range(2):
                                rows = slice(r * A, (r + 1) * A)
                                last = act.activation(kT[rows, 2 * j + t, r, :], bank(name, 128, 2, 2 * S)[rows, t, :],
                                                      ACT.Identity, bias=bk[rows, 2 * j + t:2 * j + t + 1])
                        banks.move_done(last, name)
                    for u in range(2):
                        for g in range(G):
                            act.wait_ge(shifted, i * (2 * G) + (u * G + g + 1))
                            act.activation(sm[:, u, g], sm[:, u, g], ACT.Exp).then_inc(exped, 1)
                            banks.wait_full(act, f"p{u}{g}", i)
                            banks.move_done(act.activation(pT[:, u, g], bank(f"p{u}{g}", S, GH, S), ACT.Copy),
                                            f"p{u}{g}")
                    for u in range(2):
                        for half in range(2):
                            name = f"t{u}{half}"
                            banks.wait_full(act, name, i)
                            banks.move_done(act.activation(oT[:, u, half * 4:half * 4 + 4, :],
                                                           bank(name, 128, 4, S), ACT.Copy), name)
                    move_norm(i + 1)

            @block.vector
            def _(dve):
                dve.wait_ge(loaded, LOADED)
                dve.tensor_scalar(bq[:], bq[:], 0.125, None, ALU.mult).then_inc(bq_scaled, 1)
                dve.wait_ge(bq_scaled, 1)
                first = Chain(sem("a_dve_first"), LN_STEPS)
                layer_norm(dve, ln, first, 0, 0, [X[:, u, :] for u in range(2)])
                with dve.Fori(0, TURNS) as i:
                    for u in range(2):
                        chain.done(dve.tensor_tensor(X[:, 2 * i + u, :], X[:, 2 * i + u, :], bo[:], ALU.add))
                    for j in range(T // 2):
                        name = f"q{j}"
                        banks.wait_full(dve, name, i)
                        last = dve.scalar_tensor_tensor(
                            qT[:, 2 * j:2 * j + 2, :], bank(name, 128, 2, 2 * S), 0.125,
                            bq[:, 2 * j:2 * j + 2].unsqueeze(2).broadcast_to([128, 2, 2 * S]), ALU.mult, ALU.add)
                        banks.move_done(last, name)
                    for u in range(2):
                        for half in range(2):
                            name = f"v{u}{half}"
                            banks.wait_full(dve, name, i)
                            h = slice(half * 8, half * 8 + 8)
                            banks.move_done(dve.tensor_tensor(v[:, u, h, 0:A], bank(name, S, 8, A), bv[:, h, :],
                                                              ALU.add), name)
                    for u in range(2):
                        for g in range(G):
                            name = f"s{u}{g}"
                            banks.wait_full(dve, name, i)
                            banks.move_done(dve.tensor_tensor(
                                sm[:, u, g], bank(name, S, GH, S),
                                k.causal[:].unsqueeze(1).broadcast_to([S, GH, S]), ALU.min), name)
                            banks.wait_moved(dve, i, name)
                            chain.link(dve, i, dve.tensor_reduce(mx[:, u, g], sm[:, u, g], AX.X, ALU.max))
                            dve.tensor_tensor(sm[:, u, g], sm[:, u, g],
                                              mx[:, u, g].unsqueeze(2).broadcast_to([S, GH, S]),
                                              ALU.subtract).then_inc(shifted, 1)
                    layer_norm(dve, ln, chain, i + 1, i, [X[:, 2 * i + 2 + u, :] for u in range(2)])
                    for u in range(2):
                        for g in range(G):
                            name = f"o{u}{g}"
                            banks.wait_full(dve, name, i)
                            ps = bank(name, S, GH, A + 1)
                            chain.link(dve, i, dve.reciprocal(den[:, u, g], ps[:, :, A]))
                            banks.move_done(dve.tensor_tensor(
                                o[:, u, g * GH * A:(g + 1) * GH * A].rearrange("p (n a) -> p n a", a=A),
                                ps[:, :, 0:A], den[:, u, g].unsqueeze(2).broadcast_to([S, GH, A]), ALU.mult), name)
                    for u in range(2):
                        name = f"y{u}"
                        banks.wait_full(dve, name, i)
                        banks.move_done(dve.tensor_tensor(X[:, 2 * i + u, :], X[:, 2 * i + u, :],
                                                          bank(name, S, D), ALU.add), name)
                    chain.end()
        banks.done(TURNS)
        xb.done(TURNS + 1)


def cross_attention(k, w, name, A, scale):
    nc, X = k.nc, k.X
    HT = 128 // A
    T = H // HT
    TURNS = B // 2
    KEYS, CH = 121, 3
    HG = 4 if A == 64 else H
    VB = min(H * A, 512)
    NP, NT = 6, 4
    with ExitStack() as ctx:
        def sb(n, shape):
            return ctx.enter_context(nc.sbuf_tensor(f"{name}_{n}", shape, F32))

        def sem(n):
            return k.sem(f"{name}_{n}")

        wq, wk = sb("wq", [128, KC, T * 128]), sb("wk", [128, T * 128])
        wv, wo = sb("wv", [128, H * A]), sb("wo", [128, T, D])
        bo = sb("bo", [S, D])
        ln = Norm(lambda n, shape: ctx.enter_context(nc.sbuf_tensor(n, shape, F32)), k.sem, name, k.half)
        xT = sb("xT", [128, KC, 2, S])
        cT = sb("cT", [128, 2, KEYS * CH])
        qT = sb("qT", [128, T, HT, 2 * S])
        kT = sb("kT", [128, 2, T, CTX])
        v = sb("v", [KEYS, 2, CH, H, A + 1])
        nmx = sb("nmx", [S, 2, H])
        p = sb("p", [S, NP, KEYS * CH])
        pT = sb("pT", [KEYS, NT, CH, S])
        den = sb("den", [S, 2, H])
        o = sb("o", [S, 2, H, A])
        oT = sb("oT", [128, 2, T, S])
        loaded, prepared, ctx_loaded = sem("loaded"), sem("prepared"), sem("ctx_loaded")
        max_ready = sem("max_ready")

        heads = [(u, h) for u in range(2) for h in range(H)]
        steps = []
        for m in range(0, 2 * H + 6, 2):
            steps += [("s", *heads[n]) for n in (m, m + 1) if n < 2 * H]
            steps += [("p", *heads[n]) for n in (m - 4, m - 3) if 0 <= n < 2 * H]
            for n in (m - 6, m - 5):
                if 0 <= n:
                    steps.append(("o", *heads[n]))
            if m - 6 == H + 4:
                steps += [("t", 0, c) for c in range(0, T, 4)]
            if m - 6 == H + 8:
                steps.append(("y", 0, 0))
        steps += [("x", 0, 0)] + [("t", 1, c) for c in range(0, T, 4)] + [("y", 1, 0)]

        banks = Banks(k, 0, 5)
        banks.plan([f"q{j}" for j in range(T // 2)] + [f"k{u}{t}" for u in range(2) for t in range(T)]
                   + [f"v{u}{c}{n}" for u in range(2) for c in range(CH) for n in range(H * A // VB)]
                   + [f"{a}{u}.{h}" for a, u, h in steps if a in "spty"])
        ob = Banks(k, 5, 2).plan([f"o{u}.{g}" for u in range(2) for g in range(H // HG)])
        xb = Banks(k, 7, 1).plan(["xT"])
        bank = banks.at
        on_act = [n for n in range(2 * H) if n % 2]
        chain = Chain(sem("dve_step"), LN_STEPS + 2 * H // HG + (2 if w["bo"] is not None else 0))

        with nc.Block() as block:
            @block.sync
            def _(sp):
                sp.dma_start(wq[:], w["Wq"].rearrange("(c p) n -> p c n", p=128)).then_inc(loaded, 16)
                sp.dma_start(wk[:], w["Wk"]).then_inc(loaded, 16)
                sp.dma_start(wv[:], w["Wv"]).then_inc(loaded, 16)
                sp.dma_start(wo[:], w["Wo"].rearrange("(t p) n -> p t n", p=128)).then_inc(loaded, 16)
                if w["bo"] is not None:
                    sp.dma_start(bo[:], w["bo"].partition_broadcast(S)).then_inc(loaded, 16)
                sp.dma_start(cT[:], k.ctx_T[0:2].rearrange("b p n -> p b n")).then_inc(ctx_loaded, 16)
                with sp.Fori(0, TURNS - 1) as i:
                    banks.wait_full(sp, f"v1{CH - 1}{H * A // VB - 1}", i)
                    sp.dma_start(cT[:], k.ctx_T[bass.ds(2 * i + 2, 2)].rearrange("b p n -> p b n"))\
                      .then_inc(ctx_loaded, 16)

            LOADED = 64 if w["bo"] is None else 80

            @block.gpsimd
            def _(pool):
                pool.memset(v[:, :, :, :, A:A + 1], 1.0).then_inc(prepared, 1)
                pool.wait_ge(prepared, 1)
                pool.memset(p[:, :, CTX:KEYS * CH], 0.0).then_inc(prepared, 1)
                pool.wait_ge(prepared, 2)
                pool.memset(qT[:], 0.0).then_inc(prepared, 1)
                layer_norm_rstd(pool, ln, 0)
                with pool.Fori(0, TURNS) as i:
                    layer_norm_rstd(pool, ln, i + 1)

            @block.tensor
            def _(pe):
                pe.wait_ge(loaded, LOADED)
                pe.wait_ge(prepared, 3)
                turn_norm(pe, k, ln, xb, 0)
                with pe.Fori(0, TURNS) as i:
                    xb.wait_moved(pe, i, "xT")
                    for j in range(T // 2):
                        banks.wait_free(pe, f"q{j}", i)
                        for t in range(2):
                            for c in range(KC):
                                m = (2 * j + t) * 128
                                last = pe.matmul(bank(f"q{j}", 128, 2, 2 * S)[:, t, :], wq[:, c, m:m + 128],
                                                 xT[:, c].rearrange("p u s -> p (u s)"),
                                                 start=(c == 0), stop=(c == KC - 1))
                        banks.fill_done(last, f"q{j}")
                    for u in range(2):
                        for t in range(T):
                            banks.wait_free(pe, f"k{u}{t}", i)
                            if u == 0 and t == 0:
                                pe.wait_ge(ctx_loaded, i * 16 + 16)
                            last = pe.matmul(bank(f"k{u}{t}", 128, CTX), wk[:, t * 128:(t + 1) * 128],
                                             cT[:, u, 0:CTX], start=True, stop=True)
                            banks.fill_done(last, f"k{u}{t}")
                    for u in range(2):
                        for c in range(CH):
                            for n in range(H * A // VB):
                                banks.wait_free(pe, f"v{u}{c}{n}", i)
                                last = pe.matmul(bank(f"v{u}{c}{n}", KEYS, VB), cT[:, u, c * KEYS:(c + 1) * KEYS],
                                                 wv[:, n * VB:(n + 1) * VB], start=True, stop=True)
                                banks.fill_done(last, f"v{u}{c}{n}")
                    for kind, u, h in steps:
                        name, n = f"{kind}{u}.{h}", u * H + h
                        if kind == "s":
                            banks.wait_free(pe, name, i, f"q{h // HT // 2}", f"k{u}{h // HT}")
                            banks.fill_done(pe.matmul(
                                bank(name, S, CTX), qT[:, h // HT, h % HT, u * S:(u + 1) * S],
                                kT[:, u, h // HT, :], start=True, stop=True), name)
                        elif kind == "p":
                            banks.wait_free(pe, name, i, f"s{u}.{h}")
                            for c in range(CH):
                                last = pe.transpose(bank(name, KEYS, CH, S)[:, c, :],
                                                    p[:, n % NP, c * KEYS:(c + 1) * KEYS], k.ident[0:S, 0:S])
                            banks.fill_done(last, name)
                        elif kind == "o":
                            g = h // HG
                            if h % HG == 0:
                                ob.wait_free(pe, f"o{u}.{g}", i)
                            vs = [f"v{u}{c}{h * A // VB}" for c in range(CH)] if h % HG == 0 else []
                            banks.wait_moved(pe, i, f"p{u}.{h}", *vs)
                            for c in range(CH):
                                last = pe.matmul(ob.at(f"o{u}.{g}", S, HG, A + 1)[:, h % HG, :],
                                                 pT[:, n % NT, c, :], v[:, u, c, h, :],
                                                 start=(c == 0), stop=(c == CH - 1))
                            if h % HG == HG - 1:
                                ob.fill_done(last, f"o{u}.{g}")
                        elif kind == "x":
                            turn_norm(pe, k, ln, xb, i + 1)
                        elif kind == "t":
                            banks.wait_free(pe, name, i)
                            gs = sorted({(h + t) * (128 // A) // HG for t in range(min(4, T))})
                            ob.wait_moved(pe, i, *[f"o{u}.{g}" for g in gs])
                            for t in range(min(4, T)):
                                last = pe.transpose(bank(name, 128, min(4, T), S)[:, t, :],
                                                    o[:, u].rearrange("p h a -> p (h a)")[:, (h + t) * 128:(h + t + 1) * 128],
                                                    k.ident[0:S, 0:S])
                            banks.fill_done(last, name)
                        elif kind == "y":
                            banks.wait_free(pe, name, i, *[f"t{u}.{c}" for c in range(0, T, 4)])
                            for t in range(T):
                                last = pe.matmul(bank(name, S, D), oT[:, u, t, :], wo[:, t, :],
                                                 start=(t == 0), stop=(t == T - 1))
                            banks.fill_done(last, name)

            @block.scalar
            def _(act):
                def move_norm(t):
                    xb.wait_full(act, "xT", t)
                    xb.move_done(act.activation(xT[:], xb.at("xT", 128, KC, 2, S), ACT.Copy), "xT")

                def move(name, i, out, src, scale=1.0):
                    banks.wait_full(act, name, i)
                    banks.move_done(act.activation(out, src, ACT.Copy, scale=scale), name)

                move_norm(0)
                act.wait_ge(prepared, 3)
                with act.Fori(0, TURNS) as i:
                    if A == 64:
                        for j in range(T // 2):
                            banks.wait_full(act, f"q{j}", i)
                            for r in range(HT):
                                rows = slice(r * A, (r + 1) * A)
                                last = act.activation(qT[rows, 2 * j:2 * j + 2, r, :],
                                                      bank(f"q{j}", 128, 2, 2 * S)[rows], ACT.Copy, scale=scale)
                            banks.move_done(last, f"q{j}")
                    for u in range(2):
                        for t in range(0, T, 2):
                            move(f"k{u}{t}", i, kT[:, u, t, :], bank(f"k{u}{t}", 128, CTX))
                    for kind, u, h in steps:
                        name, n = f"{kind}{u}.{h}", u * H + h
                        if kind == "s":
                            act.wait_ge(max_ready, i * (2 * H) + (n + 1))
                            banks.move_done(act.activation(p[:, n % NP, 0:CTX], bank(name, S, CTX), ACT.Exp,
                                                           bias=nmx[:, u, h:h + 1]), name)
                        elif kind == "p" and n in on_act:
                            move(name, i, pT[:, n % NT], bank(name, KEYS, CH, S))
                        elif kind == "t":
                            move(name, i, oT[:, u, h:h + min(4, T), :], bank(name, 128, min(4, T), S))
                        elif kind == "x":
                            move_norm(i + 1)

            @block.vector
            def _(dve):
                first = Chain(sem("dve_first"), LN_STEPS)
                layer_norm(dve, ln, first, 0, 0, [X[:, u, :] for u in range(2)])
                if w["bo"] is not None:
                    dve.wait_ge(loaded, LOADED)
                dve.wait_ge(prepared, 3)
                with dve.Fori(0, TURNS) as i:
                    if w["bo"] is not None:
                        for u in range(2):
                            chain.done(dve.tensor_tensor(X[:, 2 * i + u, :], X[:, 2 * i + u, :], bo[:], ALU.add))
                    if A == 16:
                        banks.wait_full(dve, "q0", i)
                        for t in range(T):
                            last = dve.tensor_tensor(
                                qT[:, t], bank("q0", 128, 2, 2 * S)[:, t, :].unsqueeze(1).broadcast_to([128, HT, 2 * S]),
                                k.quarter_rows[:].unsqueeze(2).broadcast_to([128, HT, 2 * S]), ALU.mult)
                        banks.move_done(last, "q0")
                    for u in range(2):
                        for t in range(1, T, 2):
                            banks.wait_full(dve, f"k{u}{t}", i)
                            banks.move_done(dve.tensor_copy(kT[:, u, t, :], bank(f"k{u}{t}", 128, CTX)), f"k{u}{t}")
                    for u in range(2):
                        for c in range(CH):
                            for n in range(H * A // VB):
                                name = f"v{u}{c}{n}"
                                banks.wait_full(dve, name, i)
                                hs = slice(n * VB // A, (n + 1) * VB // A)
                                banks.move_done(dve.tensor_copy(v[:, u, c, hs, 0:A],
                                                                bank(name, KEYS, VB // A, A)), name)
                    for kind, u, h in steps:
                        name, n = f"{kind}{u}.{h}", u * H + h
                        if kind == "s":
                            banks.wait_full(dve, name, i)
                            dve.tensor_reduce(nmx[:, u, h:h + 1], bank(name, S, CTX), AX.X, ALU.max,
                                              negate=True).then_inc(max_ready, 1)
                        elif kind == "p" and n not in on_act:
                            banks.wait_full(dve, name, i)
                            banks.move_done(dve.tensor_copy(pT[:, n % NT], bank(name, KEYS, CH, S)), name)
                        elif kind == "o" and h % HG == HG - 1:
                            g = h // HG
                            ob.wait_full(dve, f"o{u}.{g}", i)
                            ps = ob.at(f"o{u}.{g}", S, HG, A + 1)
                            hs = slice(g * HG, (g + 1) * HG)
                            chain.link(dve, i, dve.reciprocal(den[:, u, hs], ps[:, :, A]))
                            ob.move_done(dve.tensor_tensor(
                                o[:, u, hs, :], ps[:, :, 0:A], den[:, u, hs].unsqueeze(2).broadcast_to([S, HG, A]),
                                ALU.mult), f"o{u}.{g}")
                        elif kind == "t" and u == 0 and h == 0:
                            layer_norm(dve, ln, chain, i + 1, i, [X[:, 2 * i + 2 + b, :] for b in range(2)])
                        elif kind == "y":
                            banks.wait_full(dve, name, i)
                            banks.move_done(dve.tensor_tensor(X[:, 2 * i + u, :], X[:, 2 * i + u, :],
                                                              bank(name, S, D), ALU.add), name)
                    chain.end()
        banks.done(TURNS)
        ob.done(TURNS)
        xb.done(TURNS + 1)


def linear_attention(k, w):
    nc, X = k.nc, k.X
    A, HT, GH = 16, 8, 4
    T = H // HT
    TURNS = B // 2
    with ExitStack() as ctx:
        def sb(n, shape):
            return ctx.enter_context(nc.sbuf_tensor(n, shape, F32))

        sem = k.sem
        wq, wk = sb("d_wq", [128, KC, T * 128]), sb("d_wk", [128, KC, T * 128])
        wv, wo = sb("d_wv", [128, KC, D]), sb("d_wo", [128, KC, D])
        bq, bk = sb("d_bq", [128, T]), sb("d_bk", [128, T])
        bv, bo = sb("d_bv", [S, D]), sb("d_bo", [S, D])
        ln = Norm(sb, sem, "d", k.half)
        xT = sb("d_xT", [128, KC, 2, S])
        qT, kT = sb("d_qT", [128, T, HT, 2 * S]), sb("d_kT", [128, T, 2 * S])
        v = sb("d_v", [S, 2, D])
        sT = sb("d_sT", [S, 2, H, S])
        o = sb("d_o", [S, 2, D])
        oT = sb("d_oT", [128, 2, KC, S])
        loaded = sem("d_loaded")
        chain = Chain(sem("d_dve_step"), LN_STEPS + 2)
        banks, xb = Banks(k, 0, 7), Banks(k, 7, 1).plan(["xT"])
        banks.plan(["q0", "k0", "v0", "v1"] + [f"s{u}{r}" for u in range(2) for r in range(H // GH)]
                   + ["o0", "o1", "t0", "t1", "y0", "y1"])
        bank = banks.at
        with nc.Block() as block:
            @block.sync
            def _(sp):
                for t, src in ((wq, w["Wq"]), (wk, w["Wk"]), (wv, w["Wv"]), (wo, w["Wo"])):
                    sp.dma_start(t[:], src.rearrange("(c p) n -> p c n", p=128)).then_inc(loaded, 16)
                for t, src in ((bq, w["bq"]), (bk, w["bk"])):
                    sp.dma_start(t[:], src).then_inc(loaded, 16)
                for t, src in ((bv, w["bv"]), (bo, w["bo"])):
                    sp.dma_start(t[:], src.partition_broadcast(S)).then_inc(loaded, 16)

            LOADED = 8 * 16

            @block.gpsimd
            def _(pool):
                layer_norm_rstd(pool, ln, 0)
                with pool.Fori(0, TURNS) as i:
                    layer_norm_rstd(pool, ln, i + 1)

            @block.tensor
            def _(pe):
                pe.wait_ge(loaded, LOADED)
                turn_norm(pe, k, ln, xb, 0)
                with pe.Fori(0, TURNS) as i:
                    xb.wait_moved(pe, i, "xT")
                    for nm, wt in (("q", wq), ("k", wk)):
                        for j in range(T // 2):
                            banks.wait_free(pe, f"{nm}{j}", i)
                            for t in range(2):
                                for c in range(KC):
                                    m = (2 * j + t) * 128
                                    last = pe.matmul(bank(f"{nm}{j}", 128, 2, 2 * S)[:, t, :], wt[:, c, m:m + 128],
                                                     xT[:, c].rearrange("p u s -> p (u s)"),
                                                     start=(c == 0), stop=(c == KC - 1))
                            banks.fill_done(last, f"{nm}{j}")
                    for u in range(2):
                        banks.wait_free(pe, f"v{u}", i)
                        for c in range(KC):
                            last = pe.matmul(bank(f"v{u}", S, D), xT[:, c, u, :], wv[:, c, :],
                                             start=(c == 0), stop=(c == KC - 1))
                        banks.fill_done(last, f"v{u}")
                    for u in range(2):
                        for r in range(H // GH):
                            banks.wait_free(pe, f"s{u}{r}", i, "q0", "k0")
                            t, h = r * GH // HT, r * GH % HT
                            cols = slice(u * S, (u + 1) * S)
                            banks.fill_done(pe.matmul(bank(f"s{u}{r}", S, GH, S), kT[:, t, cols],
                                                      qT[:, t, h:h + GH, cols], start=True, stop=True), f"s{u}{r}")
                    turn_norm(pe, k, ln, xb, i + 1)
                    for u in range(2):
                        banks.wait_free(pe, f"o{u}", i, f"v{u}", *[f"s{u}{r}" for r in range(H // GH)])
                        for h in range(H):
                            last = pe.matmul(bank(f"o{u}", S, H, A)[:, h, :], sT[:, u, h, :],
                                             v[:, u, h * A:(h + 1) * A], start=True, stop=True)
                        banks.fill_done(last, f"o{u}")
                    for u in range(2):
                        banks.wait_free(pe, f"t{u}", i, f"o{u}")
                        for t in range(KC):
                            last = pe.transpose(bank(f"t{u}", 128, KC, S)[:, t, :], o[:, u, t * 128:(t + 1) * 128],
                                                k.ident[0:S, 0:S])
                        banks.fill_done(last, f"t{u}")
                    for u in range(2):
                        banks.wait_free(pe, f"y{u}", i, f"t{u}")
                        for t in range(KC):
                            last = pe.matmul(bank(f"y{u}", S, D), oT[:, u, t, :], wo[:, t, :],
                                             start=(t == 0), stop=(t == KC - 1))
                        banks.fill_done(last, f"y{u}")

            @block.scalar
            def _(act):
                act.wait_ge(loaded, LOADED)

                def move_norm(t):
                    xb.wait_full(act, "xT", t)
                    xb.move_done(act.activation(xT[:], xb.at("xT", 128, KC, 2, S), ACT.Copy), "xT")

                move_norm(0)
                with act.Fori(0, TURNS) as i:
                    for j in range(T // 2):
                        banks.wait_full(act, f"k{j}", i)
                        for t in range(2):
                            last = act.activation(kT[:, 2 * j + t, :], bank(f"k{j}", 128, 2, 2 * S)[:, t, :],
                                                  ACT.Identity, bias=bk[:, 2 * j + t:2 * j + t + 1])
                        banks.move_done(last, f"k{j}")
                    move_norm(i + 1)
                    for u in range(2):
                        banks.wait_full(act, f"o{u}", i)
                        banks.move_done(act.activation(o[:, u, :], bank(f"o{u}", S, D), ACT.Copy), f"o{u}")
                    for u in range(2):
                        banks.wait_full(act, f"t{u}", i)
                        banks.move_done(act.activation(oT[:, u], bank(f"t{u}", 128, KC, S), ACT.Copy), f"t{u}")

            @block.vector
            def _(dve):
                dve.wait_ge(loaded, LOADED)
                first = Chain(sem("d_dve_first"), LN_STEPS)
                layer_norm(dve, ln, first, 0, 0, [X[:, u, :] for u in range(2)])
                with dve.Fori(0, TURNS) as i:
                    for u in range(2):
                        chain.done(dve.tensor_tensor(X[:, 2 * i + u, :], X[:, 2 * i + u, :], bo[:], ALU.add))
                    for j in range(T // 2):
                        banks.wait_full(dve, f"q{j}", i)
                        for t in range(2):
                            last = dve.scalar_tensor_tensor(
                                qT[:, t], bank(f"q{j}", 128, 2, 2 * S)[:, t, :].unsqueeze(1).broadcast_to([128, HT, 2 * S]),
                                bq[:, t:t + 1], k.one_rows[:].unsqueeze(2).broadcast_to([128, HT, 2 * S]),
                                ALU.add, ALU.mult)
                        banks.move_done(last, f"q{j}")
                    for u in range(2):
                        banks.wait_full(dve, f"v{u}", i)
                        banks.move_done(dve.tensor_tensor(v[:, u, :], bank(f"v{u}", S, D), bv[:], ALU.add), f"v{u}")
                    layer_norm(dve, ln, chain, i + 1, i, [X[:, 2 * i + 2 + u, :] for u in range(2)])
                    for u in range(2):
                        for r in range(H // GH):
                            banks.wait_full(dve, f"s{u}{r}", i)
                            banks.move_done(dve.tensor_tensor(
                                sT[:, u, r * GH:(r + 1) * GH], bank(f"s{u}{r}", S, GH, S),
                                k.keep[:].unsqueeze(1).broadcast_to([S, GH, S]), ALU.mult), f"s{u}{r}")
                    for u in range(2):
                        banks.wait_full(dve, f"y{u}", i)
                        banks.move_done(dve.tensor_tensor(X[:, 2 * i + u, :], X[:, 2 * i + u, :],
                                                          bank(f"y{u}", S, D), ALU.add), f"y{u}")
                    chain.end()
        banks.done(TURNS)
        xb.done(TURNS + 1)


class Ranking:

    def __init__(self, sb):
        self.above, self.equal = sb("above", [S, 2, 8, 8]), sb("equal", [S, 2, 8, 8])
        self.rank, self.sel = sb("rank", [S, 2, 8]), sb("sel", [S, 2, 8])


def chosen_by_rank(link, dve, k, r, score, count):
    wide = [S, 2, 8, 8]
    mine = score.unsqueeze(3).broadcast_to(wide)
    other = score.unsqueeze(2).broadcast_to(wide)
    link(dve.tensor_tensor(r.above[:], other, mine, ALU.is_gt))
    link(dve.tensor_tensor(r.equal[:], other, mine, ALU.is_equal))
    link(dve.tensor_tensor(r.equal[:], r.equal[:], k.ahead[:].unsqueeze(1).broadcast_to(wide), ALU.mult))
    link(dve.tensor_tensor(r.above[:], r.above[:], r.equal[:], ALU.add))
    link(dve.tensor_reduce(r.rank[:], r.above[:], AX.X, ALU.add))
    link(dve.tensor_scalar(r.sel[:], r.rank[:], float(count), None, ALU.is_lt))


RANK_STEPS = 6


class Dispatch:

    def __init__(self, k, sb, name, E, cap):
        nc = k.nc
        self.E, self.cap, self.rows = E, cap, E * cap
        self.xn = nc.dram_tensor(name + "_xn_rows", (B * S, D), F32).ap()
        self.token = nc.dram_tensor(name + "_token_of_row", (self.rows, 1), I32).ap()
        self.y = nc.dram_tensor(name + "_y_rows", (self.rows, D), F32).ap()
        self.row, self.weight = sb(name + "_row", [S, B, 8], I32), sb(name + "_weight", [S, B, 8], F32)


NO_TOKEN = 1 << 20
DROPPED = 32768.0


def route(k, w, name, E, xall, comb, dispatch=None):
    nc, X = k.nc, k.X
    TURNS = B // 2
    GROUPS, TOP, CAP, FACTOR = 8, 8, 256, 2.5
    with ExitStack() as ctx:
        def sb(n, shape):
            return ctx.enter_context(nc.sbuf_tensor(f"{name}_{n}", shape, F32))

        def sem(n):
            return k.sem(f"{name}_{n}")

        gate = sb("gate", [128, KC, E])
        ln = Norm(lambda n, shape: ctx.enter_context(nc.sbuf_tensor(n, shape, F32)), k.sem, name, k.half)
        xT = sb("xT", [128, KC, 2, S])
        logits = sb("logits", [S, 2, E])
        r = Ranking(sb)
        top, total = sb("top", [S, 2]), sb("total", [S, 2])
        expd = sb("expd", [S, 2, E])
        loaded, act_asked, act_done = sem("loaded"), sem("act_asked"), sem("act_done")
        names = ["l"]
        if E == 64:
            ebias = sb("ebias", [S, E])
            biased, masked, left = sb("biased", [S, 2, E]), sb("masked", [S, 2, E]), sb("left", [S, 2, E])
            best = sb("best", [S, 2, GROUPS, 8])
            gscore = sb("gscore", [S, 2, GROUPS])
            best8 = sb("best8", [S, 2, TOP])
            taken = sb("taken", [S, 2, E])
            before = sb("before", [S, 2, E])
            names.append("c")
            choices_ready = sem("choices_ready")
            passed, started = sem("passed"), sem("started")
            weight = sb("choice_weight", [S, 2, E])
            row1 = sb("row1", [128, E])
            late = sb("late", [S, 2, E])
            key = sb("key", [S, 2, E])
            key8 = sb("key8", [S, 2, TOP])
            match = sb("match", [S, 2, TOP, E])
            rows_now = ctx.enter_context(nc.sbuf_tensor(name + "_rows_now", [S, 2, TOP], I32))
            token_now = ctx.enter_context(nc.sbuf_tensor(name + "_token_now", [S, 2], I32))
            token_f = sb("token_f", [S, 2])
            no_token = ctx.enter_context(nc.sbuf_tensor(name + "_no_token", [128, 128], I32))
            constants, table_clear, stored = sem("constants"), sem("table_clear"), sem("xn_stored")
            rows_ready, sent, tokens_ready = sem("rows_ready"), sem("sent"), sem("tokens_ready")
            rows_free = sem("rows_free")
        banks, xb = Banks(k, 0, 7), Banks(k, 7, 1).plan(["xT"])
        banks.plan(names)
        steps = {8: LN_STEPS + RANK_STEPS + 5, 64: LN_STEPS + RANK_STEPS + 30}[E]
        chain = Chain(sem("dve_step"), steps)
        with nc.Block() as block:
            @block.sync
            def _(sp):
                sp.dma_start(gate[:], w["gate"].rearrange("(c p) n -> p c n", p=128)).then_inc(loaded, 16)
                if E == 64:
                    sp.dma_start(ebias[:], w["ebias"].partition_broadcast(S)).then_inc(loaded, 16)
                    sp.wait_ge(constants, 1)
                    sp.dma_start(dispatch.token.rearrange("(p n) o -> p (n o)", p=128), no_token[:])\
                      .then_inc(table_clear, 16)
                    rows_of = dispatch.xn.rearrange("(b s) d -> s b d", s=S)
                    with sp.Fori(0, TURNS) as i:
                        sp.wait_ge(ln.xn_ready, i * 2 + 2)
                        sp.dma_start(rows_of[:, bass.ds(i * 2, 2), :], ln.xn[:]).then_inc(stored, 16)
                    sp.wait_ge(stored, TURNS * 16)

            LOADED = 16 if E == 8 else 32

            @block.gpsimd
            def _(pool):
                if E == 64:
                    pool.memset(no_token[:], NO_TOKEN).then_inc(constants, 1)
                    pool.wait_ge(constants, 1)
                    pool.iota(row1[:], pattern=[[2, E]], base=1, channel_multiplier=0,
                              allow_small_or_imprecise_dtypes=True).then_inc(constants, 1)
                    pool.wait_ge(constants, 2)
                    pool.iota(token_f[:], pattern=[[S, 2]], base=0, channel_multiplier=1,
                              allow_small_or_imprecise_dtypes=True).then_inc(constants, 1)
                    pool.wait_ge(constants, 3)
                layer_norm_rstd(pool, ln, 0)
                if E == 64:
                    pool.sem_inc(rows_free, 1)
                    pool.wait_ge(table_clear, 16)
                with pool.Fori(0, TURNS) as i:
                    layer_norm_rstd(pool, ln, i + 1)
                    if E == 64:
                        pool.wait_ge(rows_ready, i + 1)
                        pool.sem_inc(started, 1)
                        for u in range(2):
                            for n in range(TOP):
                                pool.indirect_dma_start(
                                    out=dispatch.token, in_=token_now[:, u:u + 1], in_offset=None,
                                    out_offset=bass.IndirectOffsetOnAxis(
                                        ap=rows_now[:, u, n:n + 1].bitcast(U32), axis=0),
                                    bounds_check=dispatch.rows - 1, oob_is_err=False).then_inc(sent, 16)
                        pool.wait_ge(sent, i * (2 * TOP * 16) + 2 * TOP * 16)
                        pool.sem_inc(rows_free, 1)

            @block.tensor
            def _(pe):
                pe.wait_ge(loaded, LOADED)
                turn_norm(pe, k, ln, xb, 0)
                with pe.Fori(0, TURNS) as i:
                    banks.wait_free(pe, "l", i)
                    xb.wait_moved(pe, i, "xT")
                    for u in range(2):
                        for c in range(KC):
                            last = pe.matmul(banks.at("l", S, 2, E)[:, u, :], xT[:, c, u, :], gate[:, c, :],
                                             start=(c == 0), stop=(c == KC - 1))
                    banks.fill_done(last, "l")
                    turn_norm(pe, k, ln, xb, i + 1)
                    if E == 64:
                        banks.wait_free(pe, "c", i)
                        pe.wait_ge(choices_ready, i + 1)
                        for u in range(2):
                            pe.matmul(banks.at("c", S, 2, E)[:, u, :], k.earlier[:], taken[:, u, :],
                                      start=True, stop=False)
                            last = pe.matmul(banks.at("c", S, 2, E)[:, u, :], k.ones[:], before[:, u, :],
                                             start=False, stop=True)
                        banks.fill_done(last, "c")

            @block.scalar
            def _(act):
                def move_norm(t):
                    xb.wait_full(act, "xT", t)
                    act.activation(xT[:], xb.at("xT", 128, KC, 2, S), ACT.Copy)
                    xb.move_done(act.activation(xall[:, :, bass.ds(t * 2, 2), :], xb.at("xT", 128, KC, 2, S),
                                                ACT.Copy), "xT")

                move_norm(0)
                with act.Fori(0, TURNS) as i:
                    act.wait_ge(act_asked, i + 1)
                    act.activation(expd[:], logits[:], ACT.Exp if E == 8 else ACT.Sigmoid).then_inc(act_done, 1)
                    move_norm(i + 1)

            @block.vector
            def _(dve):
                first = Chain(sem("dve_first"), LN_STEPS)
                layer_norm(dve, ln, first, 0, 0, [X[:, u, :] for u in range(2)])
                if E == 64:
                    dve.wait_ge(loaded, LOADED)
                    dve.wait_ge(constants, 3)
                    first.link(dve, 0, dve.memset(before[:, 0, :], 0.0))
                with dve.Fori(0, TURNS) as i:
                    def link(ins):
                        chain.link(dve, i, ins)

                    if E == 8:
                        banks.wait_full(dve, "l", i)
                        banks.move_done(dve.tensor_copy(logits[:], banks.at("l", S, 2, E)), "l")
                        banks.wait_moved(dve, i, "l")
                        chosen_by_rank(link, dve, k, r, logits[:], 2)
                        link(dve.tensor_reduce(top[:], logits[:], AX.X, ALU.max))
                        dve.tensor_tensor(logits[:], logits[:], top[:].unsqueeze(2).broadcast_to([S, 2, E]),
                                          ALU.subtract).then_inc(act_asked, 1)
                        layer_norm(dve, ln, chain, i + 1, i, [X[:, 2 * i + 2 + u, :] for u in range(2)])
                        dve.wait_ge(act_done, i + 1)
                        link(dve.tensor_tensor(expd[:], expd[:], r.sel[:], ALU.mult))
                        link(dve.tensor_reduce(total[:], expd[:], AX.X, ALU.add))
                        link(dve.reciprocal(total[:], total[:]))
                        link(dve.tensor_tensor(comb[:, bass.ds(2 * i, 2), :], expd[:],
                                               total[:].unsqueeze(2).broadcast_to([S, 2, E]), ALU.mult))
                    else:
                        banks.wait_full(dve, "l", i)
                        banks.move_done(dve.tensor_copy(logits[:], banks.at("l", S, 2, E)), "l")
                        banks.wait_moved(dve, i, "l")
                        dve.sem_inc(act_asked, 1)
                        layer_norm(dve, ln, chain, i + 1, i, [X[:, 2 * i + 2 + u, :] for u in range(2)],
                                   stored)
                        dve.wait_ge(act_done, i + 1)
                        wide = [S, 2, E]
                        link(dve.tensor_tensor(biased[:], expd[:], ebias[:].unsqueeze(1).broadcast_to(wide), ALU.add))
                        dve.sem_inc(passed, 1)
                        for u in range(2):
                            for g in range(GROUPS):
                                last = dve.max(best[:, u, g, :], biased[:, u, g * 8:(g + 1) * 8])
                        link(last)
                        link(dve.tensor_tensor(gscore[:], best[:, :, :, 0], best[:, :, :, 1], ALU.add))
                        chosen_by_rank(link, dve, k, r, gscore[:], 4)
                        link(dve.tensor_tensor(
                            masked[:].rearrange("p u (g e) -> p u g e", g=GROUPS),
                            biased[:].rearrange("p u (g e) -> p u g e", g=GROUPS),
                            r.sel[:].unsqueeze(3).broadcast_to([S, 2, GROUPS, 8]), ALU.mult))
                        link(dve.tensor_scalar(masked[:], masked[:], 0.0, None, ALU.add))
                        dve.sem_inc(passed, 1)
                        for u in range(2):
                            last = dve.max(best8[:, u, :], masked[:, u, :])
                        link(last)
                        dve.sem_inc(passed, 1)
                        for u in range(2):
                            last = dve.match_replace(left[:, u, :], best8[:, u, :], masked[:, u, :], -3.0e38)
                        link(last)
                        link(dve.tensor_scalar(taken[:], left[:], -1.0e38, None, ALU.is_lt))
                        dve.tensor_tensor(before[:, 1, :], before[:, 0, :], taken[:, 0, :], ALU.add)\
                           .then_inc(choices_ready, 1)
                        link(dve.tensor_tensor(expd[:], expd[:], taken[:], ALU.mult))
                        link(dve.tensor_reduce(total[:], expd[:], AX.X, ALU.add))
                        link(dve.tensor_scalar(total[:], total[:], 1e-20, None, ALU.add))
                        link(dve.reciprocal(total[:], total[:]))
                        link(dve.tensor_tensor(expd[:], expd[:], total[:].unsqueeze(2).broadcast_to(wide), ALU.mult))
                        banks.wait_full(dve, "c", i)
                        place = banks.at("c", S, 2, E)
                        link(dve.tensor_scalar(left[:], place, float(CAP), None, ALU.is_lt))
                        link(dve.tensor_scalar(late[:], place, float(CAP), DROPPED, ALU.is_ge, ALU.mult))
                        link(dve.tensor_scalar(masked[:], place, 128.0, -float(dispatch.rows - 1), ALU.is_ge, ALU.mult))
                        banks.move_done(dve.tensor_scalar(key[:], place, float(CAP - 1), 128.0, ALU.min, ALU.mult), "c")
                        banks.wait_moved(dve, i, "c")
                        link(dve.tensor_tensor(key[:], key[:], row1[0:S].unsqueeze(1).broadcast_to(wide), ALU.add))
                        link(dve.tensor_tensor(late[:], late[:], masked[:], ALU.add))
                        link(dve.tensor_tensor(key[:], key[:], late[:], ALU.add))
                        link(dve.tensor_tensor(key[:], key[:], taken[:], ALU.mult))
                        link(dve.tensor_tensor(before[:, 0, :], before[:, 1, :], taken[:, 1, :], ALU.add))
                        link(dve.scalar_tensor_tensor(weight[:], expd[:], FACTOR, left[:], ALU.mult, ALU.mult))
                        dve.sem_inc(passed, 1)
                        for u in range(2):
                            last = dve.max(key8[:, u, :], key[:, u, :])
                        link(last)
                        dve.wait_ge(rows_free, i + 1)
                        dve.tensor_scalar(rows_now[:], key8[:], -1.0, None, ALU.add).then_inc(tokens_ready, 1)
                        dve.wait_ge(tokens_ready, i + 1)
                        dve.tensor_scalar(token_now[:], token_f[:], 0.0, None, ALU.add).then_inc(rows_ready, 1)
                        dve.wait_ge(rows_ready, i + 1)
                        link(dve.tensor_scalar(token_f[:], token_f[:], float(2 * S), None, ALU.add))
                        full = [S, 2, TOP, E]
                        link(dve.tensor_tensor(match[:], key[:].unsqueeze(2).broadcast_to(full),
                                               key8[:].unsqueeze(3).broadcast_to(full), ALU.is_equal))
                        link(dve.tensor_tensor(match[:], match[:], weight[:].unsqueeze(2).broadcast_to(full), ALU.mult))
                        chain.done(dve.tensor_reduce(dispatch.weight[:, bass.ds(2 * i, 2), :], match[:], AX.X, ALU.add))
                        link(dve.tensor_scalar(best8[:], key8[:], DROPPED, -DROPPED, ALU.is_gt, ALU.mult))
                        link(dve.tensor_tensor(best8[:], best8[:], key8[:], ALU.add))
                        link(dve.tensor_scalar(dispatch.row[:, bass.ds(2 * i, 2), :], best8[:], -1.0, None, ALU.add))
                    chain.end()
        banks.done(TURNS)
        xb.done(TURNS + 1)


def experts(k, w, name, E, width, xall, comb):
    nc, X = k.nc, k.X
    IT = -(-width // 128)
    I = IT * 128
    NB = 4
    GROUPS = B // NB
    BUFS = min(E, 2)
    with ExitStack() as ctx:
        def sb(n, shape):
            return ctx.enter_context(nc.sbuf_tensor(f"{name}_{n}", shape, F32))

        wg, wu = sb("wg", [128, BUFS, KC, I]), sb("wu", [128, BUFS, KC, I])
        wd = sb("wd", [128, BUFS, IT, D])
        gated = sb("gated", [128, IT, NB * S])
        h = sb("h", [128, IT, NB * S])
        loaded = [k.sem(f"{name}_loaded{n}") for n in range(BUFS)]
        silu_done = k.sem(f"{name}_silu_done")
        banks = Banks(k, 0, 8)
        names = [f"{a}{t}" for t in range(IT) for a in "gu"] + [f"y{n}" for n in range(NB // 2)]
        banks.plan(names)

        def loop(eng, body):
            if E == 1:
                with eng.Fori(0, GROUPS) as j:
                    body(j, j, 0, 0)
            else:
                with eng.Fori(0, E // 2) as pair:
                    for buf in range(2):
                        with eng.Fori(0, GROUPS) as j:
                            body(pair * (2 * GROUPS) + j + buf * GROUPS, j, buf, pair)

        with nc.Block() as block:
            @block.sync
            def _(sp):
                def load(e, buf):
                    sp.dma_start(wg[:, buf], w["G"][e].rearrange("(c p) n -> p c n", p=128)).then_inc(loaded[buf], 16)
                    sp.dma_start(wu[:, buf], w["U"][e].rearrange("(c p) n -> p c n", p=128)).then_inc(loaded[buf], 16)
                    sp.dma_start(wd[:, buf], w["D"][e].rearrange("(t p) n -> p t n", p=128)).then_inc(loaded[buf], 16)

                for buf in range(BUFS):
                    load(buf, buf)
                if E > 2:
                    with sp.Fori(0, E // 2 - 1) as pair:
                        for buf in range(2):
                            banks.wait_full(sp, names[-1], pair * (2 * GROUPS) + ((buf + 1) * GROUPS - 1))
                            load(pair * 2 + (2 + buf), buf)

            @block.tensor
            def _(pe):
                def body(turn, j, buf, pair):
                    xs = [xall[:, c, bass.ds(j * NB, NB), :].rearrange("p b s -> p (b s)") for c in range(KC)]
                    for t in range(IT):
                        for nm, wt in (("g", wg), ("u", wu)):
                            banks.wait_free(pe, f"{nm}{t}", turn)
                            if nm == "g" and t == 0:
                                pe.wait_ge(loaded[buf], pair * 48 + 48)
                            for c in range(KC):
                                last = pe.matmul(banks.at(f"{nm}{t}", 128, NB * S), wt[:, buf, c, t * 128:(t + 1) * 128],
                                                 xs[c], start=(c == 0), stop=(c == KC - 1))
                            banks.fill_done(last, f"{nm}{t}")
                    for n in range(NB // 2):
                        banks.wait_free(pe, f"y{n}", turn, *[f"u{t}" for t in range(IT)])
                        for b in range(2):
                            for t in range(IT):
                                s0 = (2 * n + b) * S
                                last = pe.matmul(banks.at(f"y{n}", S, 2, D)[:, b, :], h[:, t, s0:s0 + S],
                                                 wd[:, buf, t, :], start=(t == 0), stop=(t == IT - 1))
                        banks.fill_done(last, f"y{n}")

                loop(pe, body)

            @block.scalar
            def _(act):
                def body(turn, j, buf, pair):
                    for t in range(IT):
                        banks.wait_full(act, f"g{t}", turn)
                        banks.move_done(act.activation(gated[:, t, :], banks.at(f"g{t}", 128, NB * S), ACT.Silu),
                                        f"g{t}")

                loop(act, body)

            @block.vector
            def _(dve):
                def body(turn, j, buf, pair):
                    for t in range(IT):
                        banks.wait_moved(dve, turn, f"g{t}")
                        banks.wait_full(dve, f"u{t}", turn)
                        banks.move_done(dve.tensor_tensor(h[:, t, :], gated[:, t, :],
                                                          banks.at(f"u{t}", 128, NB * S), ALU.mult), f"u{t}")
                    for n in range(NB // 2):
                        banks.wait_full(dve, f"y{n}", turn)
                        for b in range(2):
                            at = j * NB + (2 * n + b)
                            y = banks.at(f"y{n}", S, 2, D)[:, b, :]
                            if comb is None:
                                last = dve.tensor_tensor(X[:, at, :], X[:, at, :], y, ALU.add)
                            else:
                                last = dve.scalar_tensor_tensor(X[:, at, :], y, comb[:, at, bass.ds(pair * 2 + buf, 1)],
                                                                X[:, at, :], ALU.mult, ALU.add)
                        banks.move_done(last, f"y{n}")

                loop(dve, body)
        banks.done(E * GROUPS)


def mixture(k, name, gate, shared, routed, E):
    with ExitStack() as ctx:
        xall = ctx.enter_context(k.nc.sbuf_tensor(name + "_xall", [128, KC, B + 2, S], F32))
        comb = ctx.enter_context(k.nc.sbuf_tensor(name + "_comb", [S, B, E], F32))
        route(k, gate, name + "_gate", E, xall, comb)
        experts(k, shared, name + "_shared", 1, shared["width"], xall, None)
        experts(k, routed, name + "_routed", E, routed["width"], xall, comb)


def gathered_experts(k, w, name, dispatch):
    nc = k.nc
    Q = 4
    TURNS = dispatch.E // Q
    NW = 2 * KC * 128 + D
    with ExitStack() as ctx:
        def sb(n, shape, dt=F32):
            return ctx.enter_context(nc.sbuf_tensor(f"{name}_{n}", shape, dt))

        def sem(n):
            return k.sem(f"{name}_{n}")

        wt = sb("w", [128, Q, NW])
        token = sb("token", [128, dispatch.E * 2], I32)
        token_now = sb("token_now", [128, Q, 2], I32)
        xg = sb("xg", [128, Q, 2, D])
        xT = sb("xT", [128, Q, KC, 256])
        gated, h = sb("gated", [128, Q, 256]), sb("h", [128, Q, 256])
        y = sb("y", [128, Q, 2, D])
        tokens_loaded, cleared, tokens_ready = sem("tokens_loaded"), sem("cleared"), sem("tokens_ready")
        w_loaded = [sem(f"w_loaded{q}") for q in range(Q)]
        gathered = [sem(f"gathered{q}") for q in range(Q)]
        y_stored = [sem(f"y_stored{q}") for q in range(Q)]
        silu_done, started = sem("silu_done"), sem("started")
        banks = Banks(k, 0, 8)
        names = [f"{a}{q}" for a in "xgy" for q in range(Q)]
        banks.plan(names)
        ident = k.ident
        y_rows = dispatch.y.rearrange("(p n) d -> p n d", p=128)
        with nc.Block() as block:
            @block.sync
            def _(sp):
                sp.dma_start(token[:], dispatch.token.rearrange("(p n) o -> p (n o)", p=128)).then_inc(tokens_loaded, 16)
                for q in range(Q):
                    sp.dma_start(wt[:, q], w["all"][q]).then_inc(w_loaded[q], 16)
                with sp.Fori(0, TURNS - 1) as i:
                    for q in range(Q):
                        banks.wait_full(sp, f"y{q}", i)
                        sp.dma_start(wt[:, q], w["all"][i * Q + (Q + q)]).then_inc(w_loaded[q], 16)

            @block.gpsimd
            def _(pool):
                pool.memset(xg[:], 0.0).then_inc(cleared, 1)
                pool.wait_ge(cleared, 1)
                pool.wait_ge(tokens_loaded, 16)
                with pool.Fori(0, TURNS) as i:
                    for q in range(Q):
                        banks.wait_full(pool, f"x{q}", i - 1)
                    pool.sem_inc(started, 1)
                    pool.tensor_copy(token_now[:].rearrange("p q h -> p (q h)"), token[:, bass.ds(i * (2 * Q), 2 * Q)])\
                        .then_inc(tokens_ready, 1)
                    pool.wait_ge(tokens_ready, i + 1)
                    pool.sem_inc(started, 1)
                    for q in range(Q):
                        for half in range(2):
                            pool.indirect_dma_start(
                                out=xg[:, q, half, :], out_offset=None, in_=dispatch.xn,
                                in_offset=bass.IndirectOffsetOnAxis(ap=token_now[:, q, half:half + 1].bitcast(U32), axis=0),
                                bounds_check=B * S - 1, oob_is_err=False).then_inc(gathered[q], 16)

            @block.tensor
            def _(pe):
                with pe.Fori(0, TURNS) as i:
                    for q in range(Q):
                        banks.wait_free(pe, f"x{q}", i)
                        pe.wait_ge(gathered[q], i * 32 + 32)
                        for c in range(KC):
                            for half in range(2):
                                last = pe.transpose(banks.at(f"x{q}", 128, KC, 2, 128)[:, c, half, :],
                                                    xg[:, q, half, c * 128:(c + 1) * 128], ident[:])
                        banks.fill_done(last, f"x{q}")
                    for q in range(Q):
                        banks.wait_free(pe, f"g{q}", i, f"x{q}")
                        pe.wait_ge(w_loaded[q], i * 16 + 16)
                        for m in range(2):
                            for c in range(KC):
                                at = (m * KC + c) * 128
                                last = pe.matmul(banks.at(f"g{q}", 128, 2, 256)[:, m, :], wt[:, q, at:at + 128],
                                                 xT[:, q, c, :], start=(c == 0), stop=(c == KC - 1))
                        banks.fill_done(last, f"g{q}")
                    for q in range(Q):
                        banks.wait_free(pe, f"y{q}", i, f"g{q}")
                        for half in range(2):
                            last = pe.matmul(banks.at(f"y{q}", 128, 2, D)[:, half, :],
                                             h[:, q, half * 128:(half + 1) * 128], wt[:, q, NW - D:NW],
                                             start=True, stop=True)
                        banks.fill_done(last, f"y{q}")

            @block.scalar
            def _(act):
                for q in range(Q):
                    act.sem_inc(y_stored[q], 16)
                with act.Fori(0, TURNS) as i:
                    for q in range(Q):
                        banks.wait_full(act, f"x{q}", i)
                        banks.move_done(act.activation(xT[:, q], banks.at(f"x{q}", 128, KC, 256), ACT.Copy), f"x{q}")
                    for q in range(Q):
                        banks.wait_full(act, f"g{q}", i)
                        act.activation(gated[:, q, :], banks.at(f"g{q}", 128, 2, 256)[:, 0, :], ACT.Silu)\
                           .then_inc(silu_done, 1)
                    for q in range(Q):
                        banks.wait_moved(act, i, f"y{q}")
                        act.dma_start(y_rows[:, bass.ds(i * (2 * Q) + 2 * q, 2), :], y[:, q]).then_inc(y_stored[q], 16)
                for q in range(Q):
                    act.wait_ge(y_stored[q], TURNS * 16 + 16)

            @block.vector
            def _(dve):
                with dve.Fori(0, TURNS) as i:
                    for q in range(Q):
                        dve.wait_ge(silu_done, i * Q + (q + 1))
                        banks.move_done(dve.tensor_tensor(h[:, q, :], gated[:, q, :],
                                                          banks.at(f"g{q}", 128, 2, 256)[:, 1, :], ALU.mult), f"g{q}")
                    for q in range(Q):
                        dve.wait_ge(y_stored[q], i * 16 + 16)
                        banks.wait_full(dve, f"y{q}", i)
                        banks.move_done(dve.tensor_copy(y[:, q], banks.at(f"y{q}", 128, 2, D)), f"y{q}")
        banks.done(TURNS)


def combine(k, name, dispatch):
    nc, X = k.nc, k.X
    TOP = 8
    TURNS = B // 2
    with ExitStack() as ctx:
        rows = ctx.enter_context(nc.sbuf_tensor(name + "_rows", [S, 2, TOP], I32))
        y = ctx.enter_context(nc.sbuf_tensor(name + "_y", [S, 2, TOP, D], F32))
        rows_ready, fetched = k.sem(name + "_rows_ready"), [k.sem(f"{name}_fetched{u}") for u in range(2)]
        added, started = k.sem(name + "_added"), k.sem(name + "_started")
        with nc.Block() as block:
            @block.gpsimd
            def _(pool):
                with pool.Fori(0, TURNS) as i:
                    for u in range(2):
                        pool.wait_ge(added, i * (2 * TOP) + (u * TOP + 1))
                        pool.sem_inc(started, 1)
                        pool.tensor_copy(rows[:, u], dispatch.row[:, 2 * i + u, :]).then_inc(rows_ready, 1)
                        pool.wait_ge(rows_ready, i * 2 + (u + 1))
                        pool.sem_inc(started, 1)
                        for n in range(TOP):
                            pool.indirect_dma_start(
                                out=y[:, u, n, :], out_offset=None, in_=dispatch.y,
                                in_offset=bass.IndirectOffsetOnAxis(ap=rows[:, u, n:n + 1].bitcast(U32), axis=0),
                                bounds_check=dispatch.rows - 1, oob_is_err=False).then_inc(fetched[u], 16)

            @block.vector
            def _(dve):
                dve.sem_inc(added, TOP + 1)
                with dve.Fori(0, TURNS) as i:
                    for u in range(2):
                        dve.wait_ge(fetched[u], i * (TOP * 16) + TOP * 16)
                        at = 2 * i + u
                        for n in range(TOP):
                            dve.scalar_tensor_tensor(X[:, at, :], y[:, u, n, :], dispatch.weight[:, at, n:n + 1],
                                                     X[:, at, :], ALU.mult, ALU.add).then_inc(added, 1)
                            dve.wait_ge(added, i * (2 * TOP) + (u * TOP + n + 2 + TOP))


def decoder(nc, w, x, ctx_T, out):
    with ExitStack() as ctx:
        def sem(name):
            return ctx.enter_context(nc.semaphore(name))

        k = Shared(nc, sem)
        k.X = ctx.enter_context(nc.sbuf_tensor("X", [S, B + 2, D], F32))
        k.ident = ctx.enter_context(nc.sbuf_tensor("ident", [128, 128], F32))
        k.causal = ctx.enter_context(nc.sbuf_tensor("causal", [S, S], F32))
        k.PS = ctx.enter_context(nc.psum_tensor("PS", [128, 8, 512], F32))
        k.filled, k.moved = [sem(f"bank{b}_filled") for b in range(8)], [sem(f"bank{b}_moved") for b in range(8)]
        k.uses = [0] * 8
        k.keep = ctx.enter_context(nc.sbuf_tensor("keep", [S, S], F32))
        k.earlier = ctx.enter_context(nc.sbuf_tensor("earlier", [S, S], F32))
        k.ones = ctx.enter_context(nc.sbuf_tensor("ones", [S, S], F32))
        k.ahead = ctx.enter_context(nc.sbuf_tensor("ahead", [S, 8, 8], F32))
        k.one_rows = ctx.enter_context(nc.sbuf_tensor("one_rows", [128, 8], F32))
        k.quarter_rows = ctx.enter_context(nc.sbuf_tensor("quarter_rows", [128, 8], F32))
        k.half = ctx.enter_context(nc.sbuf_tensor("minus_half", [S, 2], F32))
        x_loaded, made, stored = sem("x_loaded"), sem("constants_made"), sem("stored")

        with nc.Block() as block:
            @block.sync
            def _(sp):
                sp.dma_start(k.X[:, 0:B], x.rearrange("b s d -> s b d")).then_inc(x_loaded, 16)
                sp.wait_ge(x_loaded, 16)

            @block.gpsimd
            def _(pool):
                for moved in k.moved:
                    pool.sem_inc(moved, 1)
                pool.memset(k.X[:, B:B + 2], 0.0).then_inc(made, 1)
                pool.memset(k.half[:], -0.5).then_inc(made, 1)
                pool.memset(k.ident[:], 0.0).then_inc(made, 1)
                pool.memset(k.causal[:], 3.0e38).then_inc(made, 1)
                for t in (k.keep, k.earlier, k.ones, k.ahead):
                    pool.memset(t[:], 1.0).then_inc(made, 1)
                pool.wait_ge(made, 8)
                pool.memset(k.one_rows[:], 1.0).then_inc(made, 1)
                pool.memset(k.quarter_rows[:], 16 ** -0.5).then_inc(made, 1)
                pool.wait_ge(made, 10)
                for n, t in enumerate((k.one_rows, k.quarter_rows)):
                    pool.affine_select(out=t[:], in_=t[:], compare_op=ALU.is_ge, fill=0.0,
                                       base=0, pattern=[[-16, 8]], channel_multiplier=1).then_inc(made, 1)
                    pool.wait_ge(made, 11 + 2 * n)
                    pool.affine_select(out=t[:], in_=t[:], compare_op=ALU.is_ge, fill=0.0,
                                       base=15, pattern=[[16, 8]], channel_multiplier=-1).then_inc(made, 1)
                pool.affine_select(out=k.keep[:], in_=k.keep[:], compare_op=ALU.is_ge, fill=0.0,
                                   base=0, pattern=[[1, S]], channel_multiplier=-1).then_inc(made, 1)
                pool.affine_select(out=k.earlier[:], in_=k.earlier[:], compare_op=ALU.is_gt, fill=0.0,
                                   base=0, pattern=[[1, S]], channel_multiplier=-1).then_inc(made, 1)
                pool.affine_select(out=k.ahead[:], in_=k.ahead[:], compare_op=ALU.is_gt, fill=0.0,
                                   base=0, pattern=[[1, 8], [-1, 8]], channel_multiplier=0).then_inc(made, 1)
                pool.affine_select(out=k.ident[:], in_=k.ident[:], compare_op=ALU.not_equal, fill=1.0,
                                   base=0, pattern=[[-1, 128]], channel_multiplier=1).then_inc(made, 1)
                pool.affine_select(out=k.causal[:], in_=k.causal[:], compare_op=ALU.is_ge, fill=MASKED,
                                   base=0, pattern=[[-1, S]], channel_multiplier=1).then_inc(made, 1)
                pool.wait_ge(made, 19)

        k.ctx_T = ctx_T
        self_attention(k, w["L0_attn"])
        if LAST_STAGE >= 2:
            cross_attention(k, w["L0_xattn"], "b", 16, 16 ** -0.5)
        if LAST_STAGE >= 3:
            mixture(k, "c", w["L0_gate"], w["L0_shared"], w["L0_experts"], 8)
        if LAST_STAGE >= 4:
            linear_attention(k, w["L1_attn"])
        if LAST_STAGE >= 5:
            cross_attention(k, w["L1_xattn"], "e", 64, 64 ** -0.5)

        if LAST_STAGE >= 6:
            with ExitStack() as stage:
                def sb(n, shape, dt):
                    return stage.enter_context(nc.sbuf_tensor(n, shape, dt))

                dispatch = Dispatch(k, sb, "f", 64, 256)
                with nc.sbuf_tensor("f_xall", [128, KC, B + 2, S], F32) as xall:
                    route(k, w["L1_gate"], "f_gate", 64, xall, None, dispatch)
                    experts(k, w["L1_shared"], "f_shared", 1, 256, xall, None)
                gathered_experts(k, w["L1_experts"], "f_experts", dispatch)
                combine(k, "f_combine", dispatch)

        with nc.Block() as block:
            @block.sync
            def _(sp):
                sp.dma_start(out.rearrange("b s d -> s b d"), k.X[:, 0:B]).then_inc(stored, 16)
                sp.wait_ge(stored, 16)


def kernel(**inputs):
    import numpy as np
    import concourse.bacc as bacc
    from concourse.bass_utils import run_bass_kernel_spmd

    nc = bacc.Bacc("TRN2", target_bir_lowering=False, num_devices=1)
    arrays, w = {}, {}

    def give(name, a):
        a = np.ascontiguousarray(a)
        arrays["in_" + name] = a
        return nc.dram_tensor("in_" + name, a.shape, mybir.dt.from_np(a.dtype), kind="ExternalInput").ap()

    def heads_last(a):
        return np.transpose(a, (1, 0, 2)).reshape(a.shape[1], -1)

    def rows(a):
        return a.reshape(-1, 128).T

    I = {n: np.asarray(a) for n, a in inputs.items()}
    x = give("x", I["x"])
    ctx_T = give("ctx_T", np.pad(np.transpose(I["ctx_512"], (0, 2, 1)), ((0, 0), (0, 0), (0, 2))))
    w["L0_attn"] = dict(
        Wq=give("a_Wq", heads_last(I["L0_attn_Wq"])), Wk=give("a_Wk", heads_last(I["L0_attn_Wk"])),
        Wv=give("a_Wv", heads_last(I["L0_attn_Wv"])), Wo=give("a_Wo", I["L0_attn_Wo"].reshape(H * 64, D)),
        bq=give("a_bq", rows(I["L0_attn_bq"])), bk=give("a_bk", rows(I["L0_attn_bk"])),
        bv=give("a_bv", I["L0_attn_bv"].reshape(-1)), bo=give("a_bo", I["L0_attn_bo"]))
    w["L0_xattn"] = dict(
        Wq=give("b_Wq", I["L0_xattn_Wq"].T), Wk=give("b_Wk", I["L0_xattn_Wkv"][0:D].T),
        Wv=give("b_Wv", I["L0_xattn_Wkv"][D:2 * D].T), Wo=give("b_Wo", I["L0_xattn_Wo"].T), bo=None)
    w["L1_xattn"] = dict(
        bo=give("e_bo", I["L1_xattn_bo"]),
        **{n: give("e_" + n, I["L1_xattn_" + n]) for n in ("Wq", "Wk", "Wv", "Wo")})
    def columns(a, n):
        return np.pad(a, [(0, 0)] * (a.ndim - 1) + [(0, n - a.shape[-1])])

    def turned(a):
        return np.swapaxes(a, -1, -2)

    W1, b1 = I["L1_attn_W1"], I["L1_attn_b1"]
    w["L1_attn"] = dict(
        Wk=give("d_Wk", W1[:, 0:D]), Wq=give("d_Wq", W1[:, D:2 * D]),
        Wv=give("d_Wv", W1[:, 2 * D:]), Wo=give("d_Wo", I["L1_attn_W2"]),
        bk=give("d_bk", rows(b1[0:D])), bq=give("d_bq", rows(b1[D:2 * D])),
        bv=give("d_bv", b1[2 * D:]), bo=give("d_bo", I["L1_attn_b2"]))
    w["L0_gate"] = dict(gate=give("c_gate", I["L0_ffn_gate_w"]))
    w["L0_experts"] = dict(
        width=704, G=give("c_G", columns(I["L0_ffn_Wg"], 768)), U=give("c_U", columns(I["L0_ffn_Wu"], 768)),
        D=give("c_D", turned(columns(turned(I["L0_ffn_Wd"]), 768))))
    w["L0_shared"] = dict(
        width=352, G=give("c_SG", columns(I["L0_ffn_Sg"], 384)[None]), U=give("c_SU", columns(I["L0_ffn_Su"], 384)[None]),
        D=give("c_SD", turned(columns(turned(I["L0_ffn_Sd"]), 384))[None]))
    w["L1_gate"] = dict(gate=give("f_gate", I["L1_ffn_gate_weight"].T), ebias=give("f_ebias", I["L1_ffn_e_bias"]))
    def in_rows(a):
        return np.swapaxes(a.reshape(a.shape[0], -1, 128, a.shape[-1]), 1, 2).reshape(a.shape[0], 128, -1)

    w["L1_experts"] = dict(all=give("f_W", np.concatenate(
        [in_rows(turned(I["L1_ffn_w1"])), in_rows(turned(I["L1_ffn_w3"])), in_rows(turned(I["L1_ffn_w2"]))], axis=-1)))
    w["L1_shared"] = dict(
        width=256, G=give("f_SG", I["L1_ffn_shared_gate"].T[None]), U=give("f_SU", I["L1_ffn_shared_up"].T[None]),
        D=give("f_SD", I["L1_ffn_shared_down"].T[None]))
    out = nc.dram_tensor("out", (B, S, D), F32, kind="ExternalOutput").ap()
    decoder(nc, w, x, ctx_T, out)
    r = run_bass_kernel_spmd(nc, [arrays], core_ids=[0])
    return r.results[0]["out"]
```

```python
from contextlib import ExitStack

import concourse.bass as bass
from concourse import mybir

F32 = mybir.dt.float32
I32 = mybir.dt.int32
U32 = mybir.dt.uint32
ALU = mybir.AluOpType
ACT = mybir.ActivationFunctionType
AX = mybir.AxisListType

LAST_STAGE = 6

B, S, D = 32, 100, 256
KC = D // 128
H = 16
CTX, CTXD = 361, 128
EPS = 1e-5
MASKED = -100000.0


class Shared:

    def __init__(self, nc, sem):
        self.nc, self.sem = nc, sem


class Banks:

    def __init__(self, k, first, n):
        self.PS, self.first, self.n, self.uses = k.PS, first, n, k.uses
        self.filled, self.moved = k.filled[first:first + n], k.moved[first:first + n]

    def plan(self, names):
        self.bank = {name: n % self.n for n, name in enumerate(names)}
        self.order = {name: n // self.n for n, name in enumerate(names)}
        self.per = [len(range(b, len(names), self.n)) for b in range(self.n)]
        assert len(self.bank) == len(names)
        self.base = self.uses[self.first:self.first + self.n]
        return self

    def done(self, turns):
        for b in range(self.n):
            self.uses[self.first + b] += turns * self.per[b]

    def at(self, name, p, *shape):
        n = 1
        for q in shape:
            n *= q
        flat = self.PS[0:p, self.first + self.bank[name], 0:n]
        if len(shape) == 2:
            return flat.rearrange("p (a b) -> p a b", a=shape[0])
        if len(shape) == 3:
            return flat.rearrange("p (a b c) -> p a b c", a=shape[0], b=shape[1])
        return flat

    def before(self, name, i):
        b = self.bank[name]
        return i * self.per[b] + (self.base[b] + self.order[name])

    def wait_free(self, pe, name, i, *moved):
        last = {self.bank[name]: self.order[name]}
        for m in moved:
            b = self.bank[m]
            last[b] = max(last.get(b, 0), self.order[m] + 1)
        for b, n in last.items():
            pe.wait_ge(self.moved[b], i * self.per[b] + (self.base[b] + n + 1))

    def fill_done(self, ins, name):
        ins.then_inc(self.filled[self.bank[name]], 1)

    def wait_full(self, eng, name, i):
        eng.wait_ge(self.filled[self.bank[name]], self.before(name, i) + 1)

    def move_done(self, ins, name):
        ins.then_inc(self.moved[self.bank[name]], 1)

    def wait_moved(self, eng, i, *names):
        last = {}
        for m in names:
            last[self.bank[m]] = max(last.get(self.bank[m], 0), self.order[m])
        for b, n in last.items():
            eng.wait_ge(self.moved[b], i * self.per[b] + (self.base[b] + n + 2))


def layer_norm(dve, ln, step, t, i, xs, stored=None):
    for u, x in enumerate(xs):
        step.done(dve.bn_stats(ln.stats[:, u, :], x))
    step.wait(dve, i)
    dve.sem_inc(ln.passed, 1)
    for u in range(len(xs)):
        step.done(dve.bn_aggr(ln.mv[:, u, :], ln.stats[:, u, :]))
    step.wait(dve, i)
    dve.tensor_scalar(ln.var[:], ln.mv[:, :, 1], EPS, None, ALU.add).then_inc(ln.var_ready, 1)
    dve.wait_ge(ln.rstd_ready, t + 1)
    if stored is not None:
        dve.wait_ge(stored, t * 16)
    for u, x in enumerate(xs):
        dve.tensor_scalar(ln.xn[:, u, :], x, ln.mv[:, u, 0:1], ln.rstd[:, u:u + 1],
                          ALU.subtract, ALU.mult).then_inc(ln.xn_ready, 1)


LN_STEPS = 4


def layer_norm_rstd(pool, ln, t):
    pool.wait_ge(ln.var_ready, t + 1)
    pool.tensor_tensor(ln.rstd[:], ln.var[:], ln.half[:], ALU.pow).then_inc(ln.rstd_ready, 1)


class Chain:

    def __init__(self, sem, per):
        self.sem, self.per, self.n = sem, per, 0

    def done(self, ins):
        self.n += 1
        ins.then_inc(self.sem, 1)

    def wait(self, eng, i):
        eng.wait_ge(self.sem, i * self.per + self.n)

    def link(self, eng, i, ins):
        self.done(ins)
        self.wait(eng, i)

    def end(self):
        assert self.n == self.per, (self.n, self.per)


class Norm:

    def __init__(self, sb, sem, name, half):
        self.half = half
        self.stats, self.mv = sb(name + "_stats", [S, 2, 6]), sb(name + "_mv", [S, 2, 2])
        self.var, self.rstd = sb(name + "_var", [S, 2]), sb(name + "_rstd", [S, 2])
        self.xn = sb(name + "_xn", [S, 2, D])
        self.var_ready, self.rstd_ready = sem(name + "_var_ready"), sem(name + "_rstd_ready")
        self.xn_ready, self.passed = sem(name + "_xn_ready"), sem(name + "_wait_passed")


def turn_norm(pe, k, ln, xb, t):
    xb.wait_free(pe, "xT", t)
    pe.wait_ge(ln.xn_ready, t * 2 + 2)
    for c in range(KC):
        for u in range(2):
            last = pe.transpose(xb.at("xT", 128, KC, 2, S)[:, c, u, :],
                                ln.xn[:, u, c * 128:(c + 1) * 128], k.ident[0:S, 0:S])
    xb.fill_done(last, "xT")


def self_attention(k, w):
    nc, X = k.nc, k.X
    A = 64
    T = H * A // 128
    TURNS = B // 2
    GH = 4
    G = H // GH
    with ExitStack() as ctx:
        def sb(name, shape):
            return ctx.enter_context(nc.sbuf_tensor(name, shape, F32))

        sem = k.sem
        wq, wk, wv = (sb(n, [128, KC, H * A]) for n in ("a_wq", "a_wk", "a_wv"))
        wo = sb("a_wo", [128, T, D])
        bq, bk = sb("a_bq", [128, T]), sb("a_bk", [128, T])
        bv, bo = sb("a_bv", [S, H, A]), sb("a_bo", [S, D])
        ln = Norm(sb, sem, "a", k.half)
        xT = sb("a_xT", [128, KC, 2, S])
        qT = sb("a_qT", [128, T, 2 * S])
        kT = sb("a_kT", [128, T, 2, 2 * S])
        v = sb("a_v", [S, 2, H, A + 1])
        sm = sb("a_sm", [S, 2, G, GH, S])
        mx = sb("a_mx", [S, 2, G, GH])
        pT = sb("a_pT", [S, 2, G, GH, S])
        den = sb("a_den", [S, 2, G, GH])
        o = sb("a_o", [S, 2, H * A])
        oT = sb("a_oT", [128, 2, T, S])
        loaded, prepared = sem("a_loaded"), sem("a_prepared")
        shifted, exped, bq_scaled = sem("a_shifted"), sem("a_exped"), sem("a_bq_scaled")
        chain = Chain(sem("a_dve_step"), LN_STEPS + 2 + 4 * G)
        banks, xb = Banks(k, 0, 7), Banks(k, 7, 1).plan(["xT"])
        names = ([f"q{j}" for j in range(T // 2)] + [f"k{j}" for j in range(T // 2)]
                 + [f"v{u}{c}" for u in range(2) for c in range(2)]
                 + [f"s{u}{g}" for u in range(2) for g in range(G)])
        for u in range(2):
            for g in range(G):
                names.append(f"p{u}{g}")
                if g:
                    names.append(f"o{u}{g - 1}")
            names.append(f"o{u}{G - 1}")
        names += [f"t{u}{c}" for u in range(2) for c in range(2)] + ["y0", "y1"]
        banks.plan(names)
        bank = banks.at

        with nc.Block() as block:
            @block.sync
            def _(sp):
                for t, src in ((wq, w["Wq"]), (wk, w["Wk"]), (wv, w["Wv"])):
                    sp.dma_start(t[:], src.rearrange("(c p) n -> p c n", p=128)).then_inc(loaded, 16)
                sp.dma_start(wo[:], w["Wo"].rearrange("(t p) n -> p t n", p=128)).then_inc(loaded, 16)
                for t, src in ((bq, w["bq"]), (bk, w["bk"])):
                    sp.dma_start(t[:], src).then_inc(loaded, 16)
                sp.dma_start(bv[:].rearrange("p h a -> p (h a)"), w["bv"].partition_broadcast(S)).then_inc(loaded, 16)
                sp.dma_start(bo[:], w["bo"].partition_broadcast(S)).then_inc(loaded, 16)

            LOADED = 8 * 16

            @block.gpsimd
            def _(pool):
                pool.memset(v[:, :, :, A:A + 1], 1.0).then_inc(prepared, 1)
                pool.wait_ge(prepared, 1)
                pool.memset(kT[:], 0.0).then_inc(prepared, 1)
                layer_norm_rstd(pool, ln, 0)
                with pool.Fori(0, TURNS) as i:
                    layer_norm_rstd(pool, ln, i + 1)

            @block.tensor
            def _(pe):
                pe.wait_ge(loaded, LOADED)
                pe.wait_ge(prepared, 2)
                turn_norm(pe, k, ln, xb, 0)
                with pe.Fori(0, TURNS) as i:
                    xb.wait_moved(pe, i, "xT")
                    for nm, wt in (("q", wq), ("k", wk)):
                        for j in range(T // 2):
                            name = f"{nm}{j}"
                            banks.wait_free(pe, name, i)
                            for t in range(2):
                                for c in range(KC):
                                    m = (2 * j + t) * 128
                                    last = pe.matmul(bank(name, 128, 2, 2 * S)[:, t, :], wt[:, c, m:m + 128],
                                                     xT[:, c].rearrange("p u s -> p (u s)"),
                                                     start=(c == 0), stop=(c == KC - 1))
                            banks.fill_done(last, name)
                    for u in range(2):
                        for half in range(2):
                            name = f"v{u}{half}"
                            banks.wait_free(pe, name, i)
                            for c in range(KC):
                                last = pe.matmul(bank(name, S, 512), xT[:, c, u, :],
                                                 wv[:, c, half * 512:(half + 1) * 512],
                                                 start=(c == 0), stop=(c == KC - 1))
                            banks.fill_done(last, name)
                    for u in range(2):
                        for g in range(G):
                            banks.wait_free(pe, f"s{u}{g}", i, f"q{g}", f"k{g}")
                            for t in range(GH // 2):
                                cols = slice(u * S, (u + 1) * S)
                                last = pe.matmul(bank(f"s{u}{g}", S, GH, S)[:, 2 * t:2 * t + 2, :],
                                                 qT[:, 2 * g + t, cols], kT[:, 2 * g + t, :, cols],
                                                 start=True, stop=True)
                            banks.fill_done(last, f"s{u}{g}")

                    def turn_probs(u, g):
                        name = f"p{u}{g}"
                        banks.wait_free(pe, name, i)
                        pe.wait_ge(exped, i * (2 * G) + (u * G + g + 1))
                        for n in range(GH):
                            last = pe.transpose(bank(name, S, GH, S)[:, n, :], sm[:, u, g, n, :],
                                                k.ident[0:S, 0:S])
                        banks.fill_done(last, name)

                    def weigh(u, g):
                        name = f"o{u}{g}"
                        banks.wait_free(pe, name, i, f"v{u}{g // 2}", f"p{u}{g}")
                        for n in range(GH):
                            last = pe.matmul(bank(name, S, GH, A + 1)[:, n, :], pT[:, u, g, n, :],
                                             v[:, u, g * GH + n, :], start=True, stop=True)
                        banks.fill_done(last, name)

                    for u in range(2):
                        for g in range(G):
                            turn_probs(u, g)
                            if g:
                                weigh(u, g - 1)
                        weigh(u, G - 1)
                    for u in range(2):
                        for half in range(2):
                            name = f"t{u}{half}"
                            banks.wait_free(pe, name, i, f"o{u}{2 * half}", f"o{u}{2 * half + 1}")
                            for t in range(4):
                                m = (half * 4 + t) * 128
                                last = pe.transpose(bank(name, 128, 4, S)[:, t, :], o[:, u, m:m + 128],
                                                    k.ident[0:S, 0:S])
                            banks.fill_done(last, name)
                    turn_norm(pe, k, ln, xb, i + 1)
                    for u in range(2):
                        name = f"y{u}"
                        banks.wait_free(pe, name, i, f"t{u}0", f"t{u}1")
                        for t in range(T):
                            last = pe.matmul(bank(name, S, D), oT[:, u, t, :], wo[:, t, :],
                                             start=(t == 0), stop=(t == T - 1))
                        banks.fill_done(last, name)

            @block.scalar
            def _(act):
                act.wait_ge(loaded, LOADED)
                act.wait_ge(prepared, 2)

                def move_norm(t):
                    xb.wait_full(act, "xT", t)
                    xb.move_done(act.activation(xT[:], xb.at("xT", 128, KC, 2, S), ACT.Copy), "xT")

                move_norm(0)
                with act.Fori(0, TURNS) as i:
                    for j in range(T // 2):
                        name = f"k{j}"
                        banks.wait_full(act, name, i)
                        for t in range(2):
                            for r in range(2):
                                rows = slice(r * A, (r + 1) * A)
                                last = act.activation(kT[rows, 2 * j + t, r, :], bank(name, 128, 2, 2 * S)[rows, t, :],
                                                      ACT.Identity, bias=bk[rows, 2 * j + t:2 * j + t + 1])
                        banks.move_done(last, name)
                    for u in range(2):
                        for g in range(G):
                            act.wait_ge(shifted, i * (2 * G) + (u * G + g + 1))
                            act.activation(sm[:, u, g], sm[:, u, g], ACT.Exp).then_inc(exped, 1)
                            banks.wait_full(act, f"p{u}{g}", i)
                            banks.move_done(act.activation(pT[:, u, g], bank(f"p{u}{g}", S, GH, S), ACT.Copy),
                                            f"p{u}{g}")
                    for u in range(2):
                        for half in range(2):
                            name = f"t{u}{half}"
                            banks.wait_full(act, name, i)
                            banks.move_done(act.activation(oT[:, u, half * 4:half * 4 + 4, :],
                                                           bank(name, 128, 4, S), ACT.Copy), name)
                    move_norm(i + 1)

            @block.vector
            def _(dve):
                dve.wait_ge(loaded, LOADED)
                dve.tensor_scalar(bq[:], bq[:], 0.125, None, ALU.mult).then_inc(bq_scaled, 1)
                dve.wait_ge(bq_scaled, 1)
                first = Chain(sem("a_dve_first"), LN_STEPS)
                layer_norm(dve, ln, first, 0, 0, [X[:, u, :] for u in range(2)])
                with dve.Fori(0, TURNS) as i:
                    for u in range(2):
                        chain.done(dve.tensor_tensor(X[:, 2 * i + u, :], X[:, 2 * i + u, :], bo[:], ALU.add))
                    for j in range(T // 2):
                        name = f"q{j}"
                        banks.wait_full(dve, name, i)
                        last = dve.scalar_tensor_tensor(
                            qT[:, 2 * j:2 * j + 2, :], bank(name, 128, 2, 2 * S), 0.125,
                            bq[:, 2 * j:2 * j + 2].unsqueeze(2).broadcast_to([128, 2, 2 * S]), ALU.mult, ALU.add)
                        banks.move_done(last, name)
                    for u in range(2):
                        for half in range(2):
                            name = f"v{u}{half}"
                            banks.wait_full(dve, name, i)
                            h = slice(half * 8, half * 8 + 8)
                            banks.move_done(dve.tensor_tensor(v[:, u, h, 0:A], bank(name, S, 8, A), bv[:, h, :],
                                                              ALU.add), name)
                    for u in range(2):
                        for g in range(G):
                            name = f"s{u}{g}"
                            banks.wait_full(dve, name, i)
                            banks.move_done(dve.tensor_tensor(
                                sm[:, u, g], bank(name, S, GH, S),
                                k.causal[:].unsqueeze(1).broadcast_to([S, GH, S]), ALU.min), name)
                            banks.wait_moved(dve, i, name)
                            chain.link(dve, i, dve.tensor_reduce(mx[:, u, g], sm[:, u, g], AX.X, ALU.max))
                            dve.tensor_tensor(sm[:, u, g], sm[:, u, g],
                                              mx[:, u, g].unsqueeze(2).broadcast_to([S, GH, S]),
                                              ALU.subtract).then_inc(shifted, 1)
                    layer_norm(dve, ln, chain, i + 1, i, [X[:, 2 * i + 2 + u, :] for u in range(2)])
                    for u in range(2):
                        for g in range(G):
                            name = f"o{u}{g}"
                            banks.wait_full(dve, name, i)
                            ps = bank(name, S, GH, A + 1)
                            chain.link(dve, i, dve.reciprocal(den[:, u, g], ps[:, :, A]))
                            banks.move_done(dve.tensor_tensor(
                                o[:, u, g * GH * A:(g + 1) * GH * A].rearrange("p (n a) -> p n a", a=A),
                                ps[:, :, 0:A], den[:, u, g].unsqueeze(2).broadcast_to([S, GH, A]), ALU.mult), name)
                    for u in range(2):
                        name = f"y{u}"
                        banks.wait_full(dve, name, i)
                        banks.move_done(dve.tensor_tensor(X[:, 2 * i + u, :], X[:, 2 * i + u, :],
                                                          bank(name, S, D), ALU.add), name)
                    chain.end()
        banks.done(TURNS)
        xb.done(TURNS + 1)


def cross_attention(k, w, name, A, scale):
    nc, X = k.nc, k.X
    HT = 128 // A
    T = H // HT
    TURNS = B // 2
    KEYS, CH = 121, 3
    HG = 4 if A == 64 else H
    VB = min(H * A, 512)
    NP, NT = 6, 4
    with ExitStack() as ctx:
        def sb(n, shape):
            return ctx.enter_context(nc.sbuf_tensor(f"{name}_{n}", shape, F32))

        def sem(n):
            return k.sem(f"{name}_{n}")

        wq, wk = sb("wq", [128, KC, T * 128]), sb("wk", [128, T * 128])
        wv, wo = sb("wv", [128, H * A]), sb("wo", [128, T, D])
        bo = sb("bo", [S, D])
        ln = Norm(lambda n, shape: ctx.enter_context(nc.sbuf_tensor(n, shape, F32)), k.sem, name, k.half)
        xT = sb("xT", [128, KC, 2, S])
        cT = sb("cT", [128, 2, KEYS * CH])
        qT = sb("qT", [128, T, HT, 2 * S])
        kT = sb("kT", [128, 2, T, CTX])
        v = sb("v", [KEYS, 2, CH, H, A + 1])
        nmx = sb("nmx", [S, 2, H])
        p = sb("p", [S, NP, KEYS * CH])
        pT = sb("pT", [KEYS, NT, CH, S])
        den = sb("den", [S, 2, H])
        o = sb("o", [S, 2, H, A])
        oT = sb("oT", [128, 2, T, S])
        loaded, prepared, ctx_loaded = sem("loaded"), sem("prepared"), sem("ctx_loaded")
        max_ready = sem("max_ready")

        heads = [(u, h) for u in range(2) for h in range(H)]
        steps = []
        for m in range(0, 2 * H + 6, 2):
            steps += [("s", *heads[n]) for n in (m, m + 1) if n < 2 * H]
            steps += [("p", *heads[n]) for n in (m - 4, m - 3) if 0 <= n < 2 * H]
            for n in (m - 6, m - 5):
                if 0 <= n:
                    steps.append(("o", *heads[n]))
            if m - 6 == H + 4:
                steps += [("t", 0, c) for c in range(0, T, 4)]
            if m - 6 == H + 8:
                steps.append(("y", 0, 0))
        steps += [("x", 0, 0)] + [("t", 1, c) for c in range(0, T, 4)] + [("y", 1, 0)]

        banks = Banks(k, 0, 5)
        banks.plan([f"q{j}" for j in range(T // 2)] + [f"k{u}{t}" for u in range(2) for t in range(T)]
                   + [f"v{u}{c}{n}" for u in range(2) for c in range(CH) for n in range(H * A // VB)]
                   + [f"{a}{u}.{h}" for a, u, h in steps if a in "spty"])
        ob = Banks(k, 5, 2).plan([f"o{u}.{g}" for u in range(2) for g in range(H // HG)])
        xb = Banks(k, 7, 1).plan(["xT"])
        bank = banks.at
        on_act = [n for n in range(2 * H) if n % 2]
        chain = Chain(sem("dve_step"), LN_STEPS + 2 * H // HG + (2 if w["bo"] is not None else 0))

        with nc.Block() as block:
            @block.sync
            def _(sp):
                sp.dma_start(wq[:], w["Wq"].rearrange("(c p) n -> p c n", p=128)).then_inc(loaded, 16)
                sp.dma_start(wk[:], w["Wk"]).then_inc(loaded, 16)
                sp.dma_start(wv[:], w["Wv"]).then_inc(loaded, 16)
                sp.dma_start(wo[:], w["Wo"].rearrange("(t p) n -> p t n", p=128)).then_inc(loaded, 16)
                if w["bo"] is not None:
                    sp.dma_start(bo[:], w["bo"].partition_broadcast(S)).then_inc(loaded, 16)
                sp.dma_start(cT[:], k.ctx_T[0:2].rearrange("b p n -> p b n")).then_inc(ctx_loaded, 16)
                with sp.Fori(0, TURNS - 1) as i:
                    banks.wait_full(sp, f"v1{CH - 1}{H * A // VB - 1}", i)
                    sp.dma_start(cT[:], k.ctx_T[bass.ds(2 * i + 2, 2)].rearrange("b p n -> p b n"))\
                      .then_inc(ctx_loaded, 16)

            LOADED = 64 if w["bo"] is None else 80

            @block.gpsimd
            def _(pool):
                pool.memset(v[:, :, :, :, A:A + 1], 1.0).then_inc(prepared, 1)
                pool.wait_ge(prepared, 1)
                pool.memset(p[:, :, CTX:KEYS * CH], 0.0).then_inc(prepared, 1)
                pool.wait_ge(prepared, 2)
                pool.memset(qT[:], 0.0).then_inc(prepared, 1)
                layer_norm_rstd(pool, ln, 0)
                with pool.Fori(0, TURNS) as i:
                    layer_norm_rstd(pool, ln, i + 1)

            @block.tensor
            def _(pe):
                pe.wait_ge(loaded, LOADED)
                pe.wait_ge(prepared, 3)
                turn_norm(pe, k, ln, xb, 0)
                with pe.Fori(0, TURNS) as i:
                    xb.wait_moved(pe, i, "xT")
                    for j in range(T // 2):
                        banks.wait_free(pe, f"q{j}", i)
                        for t in range(2):
                            for c in range(KC):
                                m = (2 * j + t) * 128
                                last = pe.matmul(bank(f"q{j}", 128, 2, 2 * S)[:, t, :], wq[:, c, m:m + 128],
                                                 xT[:, c].rearrange("p u s -> p (u s)"),
                                                 start=(c == 0), stop=(c == KC - 1))
                        banks.fill_done(last, f"q{j}")
                    for u in range(2):
                        for t in range(T):
                            banks.wait_free(pe, f"k{u}{t}", i)
                            if u == 0 and t == 0:
                                pe.wait_ge(ctx_loaded, i * 16 + 16)
                            last = pe.matmul(bank(f"k{u}{t}", 128, CTX), wk[:, t * 128:(t + 1) * 128],
                                             cT[:, u, 0:CTX], start=True, stop=True)
                            banks.fill_done(last, f"k{u}{t}")
                    for u in range(2):
                        for c in range(CH):
                            for n in range(H * A // VB):
                                banks.wait_free(pe, f"v{u}{c}{n}", i)
                                last = pe.matmul(bank(f"v{u}{c}{n}", KEYS, VB), cT[:, u, c * KEYS:(c + 1) * KEYS],
                                                 wv[:, n * VB:(n + 1) * VB], start=True, stop=True)
                                banks.fill_done(last, f"v{u}{c}{n}")
                    for kind, u, h in steps:
                        name, n = f"{kind}{u}.{h}", u * H + h
                        if kind == "s":
                            banks.wait_free(pe, name, i, f"q{h // HT // 2}", f"k{u}{h // HT}")
                            banks.fill_done(pe.matmul(
                                bank(name, S, CTX), qT[:, h // HT, h % HT, u * S:(u + 1) * S],
                                kT[:, u, h // HT, :], start=True, stop=True), name)
                        elif kind == "p":
                            banks.wait_free(pe, name, i, f"s{u}.{h}")
                            for c in range(CH):
                                last = pe.transpose(bank(name, KEYS, CH, S)[:, c, :],
                                                    p[:, n % NP, c * KEYS:(c + 1) * KEYS], k.ident[0:S, 0:S])
                            banks.fill_done(last, name)
                        elif kind == "o":
                            g = h // HG
                            if h % HG == 0:
                                ob.wait_free(pe, f"o{u}.{g}", i)
                            vs = [f"v{u}{c}{h * A // VB}" for c in range(CH)] if h % HG == 0 else []
                            banks.wait_moved(pe, i, f"p{u}.{h}", *vs)
                            for c in range(CH):
                                last = pe.matmul(ob.at(f"o{u}.{g}", S, HG, A + 1)[:, h % HG, :],
                                                 pT[:, n % NT, c, :], v[:, u, c, h, :],
                                                 start=(c == 0), stop=(c == CH - 1))
                            if h % HG == HG - 1:
                                ob.fill_done(last, f"o{u}.{g}")
                        elif kind == "x":
                            turn_norm(pe, k, ln, xb, i + 1)
                        elif kind == "t":
                            banks.wait_free(pe, name, i)
                            gs = sorted({(h + t) * (128 // A) // HG for t in range(min(4, T))})
                            ob.wait_moved(pe, i, *[f"o{u}.{g}" for g in gs])
                            for t in range(min(4, T)):
                                last = pe.transpose(bank(name, 128, min(4, T), S)[:, t, :],
                                                    o[:, u].rearrange("p h a -> p (h a)")[:, (h + t) * 128:(h + t + 1) * 128],
                                                    k.ident[0:S, 0:S])
                            banks.fill_done(last, name)
                        elif kind == "y":
                            banks.wait_free(pe, name, i, *[f"t{u}.{c}" for c in range(0, T, 4)])
                            for t in range(T):
                                last = pe.matmul(bank(name, S, D), oT[:, u, t, :], wo[:, t, :],
                                                 start=(t == 0), stop=(t == T - 1))
                            banks.fill_done(last, name)

            @block.scalar
            def _(act):
                def move_norm(t):
                    xb.wait_full(act, "xT", t)
                    xb.move_done(act.activation(xT[:], xb.at("xT", 128, KC, 2, S), ACT.Copy), "xT")

                def move(name, i, out, src, scale=1.0):
                    banks.wait_full(act, name, i)
                    banks.move_done(act.activation(out, src, ACT.Copy, scale=scale), name)

                move_norm(0)
                act.wait_ge(prepared, 3)
                with act.Fori(0, TURNS) as i:
                    if A == 64:
                        for j in range(T // 2):
                            banks.wait_full(act, f"q{j}", i)
                            for r in range(HT):
                                rows = slice(r * A, (r + 1) * A)
                                last = act.activation(qT[rows, 2 * j:2 * j + 2, r, :],
                                                      bank(f"q{j}", 128, 2, 2 * S)[rows], ACT.Copy, scale=scale)
                            banks.move_done(last, f"q{j}")
                    for u in range(2):
                        for t in range(0, T, 2):
                            move(f"k{u}{t}", i, kT[:, u, t, :], bank(f"k{u}{t}", 128, CTX))
                    for kind, u, h in steps:
                        name, n = f"{kind}{u}.{h}", u * H + h
                        if kind == "s":
                            act.wait_ge(max_ready, i * (2 * H) + (n + 1))
                            banks.move_done(act.activation(p[:, n % NP, 0:CTX], bank(name, S, CTX), ACT.Exp,
                                                           bias=nmx[:, u, h:h + 1]), name)
                        elif kind == "p" and n in on_act:
                            move(name, i, pT[:, n % NT], bank(name, KEYS, CH, S))
                        elif kind == "t":
                            move(name, i, oT[:, u, h:h + min(4, T), :], bank(name, 128, min(4, T), S))
                        elif kind == "x":
                            move_norm(i + 1)

            @block.vector
            def _(dve):
                first = Chain(sem("dve_first"), LN_STEPS)
                layer_norm(dve, ln, first, 0, 0, [X[:, u, :] for u in range(2)])
                if w["bo"] is not None:
                    dve.wait_ge(loaded, LOADED)
                dve.wait_ge(prepared, 3)
                with dve.Fori(0, TURNS) as i:
                    if w["bo"] is not None:
                        for u in range(2):
                            chain.done(dve.tensor_tensor(X[:, 2 * i + u, :], X[:, 2 * i + u, :], bo[:], ALU.add))
                    if A == 16:
                        banks.wait_full(dve, "q0", i)
                        for t in range(T):
                            last = dve.tensor_tensor(
                                qT[:, t], bank("q0", 128, 2, 2 * S)[:, t, :].unsqueeze(1).broadcast_to([128, HT, 2 * S]),
                                k.quarter_rows[:].unsqueeze(2).broadcast_to([128, HT, 2 * S]), ALU.mult)
                        banks.move_done(last, "q0")
                    for u in range(2):
                        for t in range(1, T, 2):
                            banks.wait_full(dve, f"k{u}{t}", i)
                            banks.move_done(dve.tensor_copy(kT[:, u, t, :], bank(f"k{u}{t}", 128, CTX)), f"k{u}{t}")
                    for u in range(2):
                        for c in range(CH):
                            for n in range(H * A // VB):
                                name = f"v{u}{c}{n}"
                                banks.wait_full(dve, name, i)
                                hs = slice(n * VB // A, (n + 1) * VB // A)
                                banks.move_done(dve.tensor_copy(v[:, u, c, hs, 0:A],
                                                                bank(name, KEYS, VB // A, A)), name)
                    for kind, u, h in steps:
                        name, n = f"{kind}{u}.{h}", u * H + h
                        if kind == "s":
                            banks.wait_full(dve, name, i)
                            dve.tensor_reduce(nmx[:, u, h:h + 1], bank(name, S, CTX), AX.X, ALU.max,
                                              negate=True).then_inc(max_ready, 1)
                        elif kind == "p" and n not in on_act:
                            banks.wait_full(dve, name, i)
                            banks.move_done(dve.tensor_copy(pT[:, n % NT], bank(name, KEYS, CH, S)), name)
                        elif kind == "o" and h % HG == HG - 1:
                            g = h // HG
                            ob.wait_full(dve, f"o{u}.{g}", i)
                            ps = ob.at(f"o{u}.{g}", S, HG, A + 1)
                            hs = slice(g * HG, (g + 1) * HG)
                            chain.link(dve, i, dve.reciprocal(den[:, u, hs], ps[:, :, A]))
                            ob.move_done(dve.tensor_tensor(
                                o[:, u, hs, :], ps[:, :, 0:A], den[:, u, hs].unsqueeze(2).broadcast_to([S, HG, A]),
                                ALU.mult), f"o{u}.{g}")
                        elif kind == "t" and u == 0 and h == 0:
                            layer_norm(dve, ln, chain, i + 1, i, [X[:, 2 * i + 2 + b, :] for b in range(2)])
                        elif kind == "y":
                            banks.wait_full(dve, name, i)
                            banks.move_done(dve.tensor_tensor(X[:, 2 * i + u, :], X[:, 2 * i + u, :],
                                                              bank(name, S, D), ALU.add), name)
                    chain.end()
        banks.done(TURNS)
        ob.done(TURNS)
        xb.done(TURNS + 1)


def linear_attention(k, w):
    nc, X = k.nc, k.X
    A, HT, GH = 16, 8, 4
    T = H // HT
    TURNS = B // 2
    with ExitStack() as ctx:
        def sb(n, shape):
            return ctx.enter_context(nc.sbuf_tensor(n, shape, F32))

        sem = k.sem
        wq, wk = sb("d_wq", [128, KC, T * 128]), sb("d_wk", [128, KC, T * 128])
        wv, wo = sb("d_wv", [128, KC, D]), sb("d_wo", [128, KC, D])
        bq, bk = sb("d_bq", [128, T]), sb("d_bk", [128, T])
        bv, bo = sb("d_bv", [S, D]), sb("d_bo", [S, D])
        ln = Norm(sb, sem, "d", k.half)
        xT = sb("d_xT", [128, KC, 2, S])
        qT, kT = sb("d_qT", [128, T, HT, 2 * S]), sb("d_kT", [128, T, 2 * S])
        v = sb("d_v", [S, 2, D])
        sT = sb("d_sT", [S, 2, H, S])
        o = sb("d_o", [S, 2, D])
        oT = sb("d_oT", [128, 2, KC, S])
        loaded = sem("d_loaded")
        chain = Chain(sem("d_dve_step"), LN_STEPS + 2)
        banks, xb = Banks(k, 0, 7), Banks(k, 7, 1).plan(["xT"])
        banks.plan(["q0", "k0", "v0", "v1"] + [f"s{u}{r}" for u in range(2) for r in range(H // GH)]
                   + ["o0", "o1", "t0", "t1", "y0", "y1"])
        bank = banks.at
        with nc.Block() as block:
            @block.sync
            def _(sp):
                for t, src in ((wq, w["Wq"]), (wk, w["Wk"]), (wv, w["Wv"]), (wo, w["Wo"])):
                    sp.dma_start(t[:], src.rearrange("(c p) n -> p c n", p=128)).then_inc(loaded, 16)
                for t, src in ((bq, w["bq"]), (bk, w["bk"])):
                    sp.dma_start(t[:], src).then_inc(loaded, 16)
                for t, src in ((bv, w["bv"]), (bo, w["bo"])):
                    sp.dma_start(t[:], src.partition_broadcast(S)).then_inc(loaded, 16)

            LOADED = 8 * 16

            @block.gpsimd
            def _(pool):
                layer_norm_rstd(pool, ln, 0)
                with pool.Fori(0, TURNS) as i:
                    layer_norm_rstd(pool, ln, i + 1)

            @block.tensor
            def _(pe):
                pe.wait_ge(loaded, LOADED)
                turn_norm(pe, k, ln, xb, 0)
                with pe.Fori(0, TURNS) as i:
                    xb.wait_moved(pe, i, "xT")
                    for nm, wt in (("q", wq), ("k", wk)):
                        for j in range(T // 2):
                            banks.wait_free(pe, f"{nm}{j}", i)
                            for t in range(2):
                                for c in range(KC):
                                    m = (2 * j + t) * 128
                                    last = pe.matmul(bank(f"{nm}{j}", 128, 2, 2 * S)[:, t, :], wt[:, c, m:m + 128],
                                                     xT[:, c].rearrange("p u s -> p (u s)"),
                                                     start=(c == 0), stop=(c == KC - 1))
                            banks.fill_done(last, f"{nm}{j}")
                    for u in range(2):
                        banks.wait_free(pe, f"v{u}", i)
                        for c in range(KC):
                            last = pe.matmul(bank(f"v{u}", S, D), xT[:, c, u, :], wv[:, c, :],
                                             start=(c == 0), stop=(c == KC - 1))
                        banks.fill_done(last, f"v{u}")
                    for u in range(2):
                        for r in range(H // GH):
                            banks.wait_free(pe, f"s{u}{r}", i, "q0", "k0")
                            t, h = r * GH // HT, r * GH % HT
                            cols = slice(u * S, (u + 1) * S)
                            banks.fill_done(pe.matmul(bank(f"s{u}{r}", S, GH, S), kT[:, t, cols],
                                                      qT[:, t, h:h + GH, cols], start=True, stop=True), f"s{u}{r}")
                    turn_norm(pe, k, ln, xb, i + 1)
                    for u in range(2):
                        banks.wait_free(pe, f"o{u}", i, f"v{u}", *[f"s{u}{r}" for r in range(H // GH)])
                        for h in range(H):
                            last = pe.matmul(bank(f"o{u}", S, H, A)[:, h, :], sT[:, u, h, :],
                                             v[:, u, h * A:(h + 1) * A], start=True, stop=True)
                        banks.fill_done(last, f"o{u}")
                    for u in range(2):
                        banks.wait_free(pe, f"t{u}", i, f"o{u}")
                        for t in range(KC):
                            last = pe.transpose(bank(f"t{u}", 128, KC, S)[:, t, :], o[:, u, t * 128:(t + 1) * 128],
                                                k.ident[0:S, 0:S])
                        banks.fill_done(last, f"t{u}")
                    for u in range(2):
                        banks.wait_free(pe, f"y{u}", i, f"t{u}")
                        for t in range(KC):
                            last = pe.matmul(bank(f"y{u}", S, D), oT[:, u, t, :], wo[:, t, :],
                                             start=(t == 0), stop=(t == KC - 1))
                        banks.fill_done(last, f"y{u}")

            @block.scalar
            def _(act):
                act.wait_ge(loaded, LOADED)

                def move_norm(t):
                    xb.wait_full(act, "xT", t)
                    xb.move_done(act.activation(xT[:], xb.at("xT", 128, KC, 2, S), ACT.Copy), "xT")

                move_norm(0)
                with act.Fori(0, TURNS) as i:
                    for j in range(T // 2):
                        banks.wait_full(act, f"k{j}", i)
                        for t in range(2):
                            last = act.activation(kT[:, 2 * j + t, :], bank(f"k{j}", 128, 2, 2 * S)[:, t, :],
                                                  ACT.Identity, bias=bk[:, 2 * j + t:2 * j + t + 1])
                        banks.move_done(last, f"k{j}")
                    move_norm(i + 1)
                    for u in range(2):
                        banks.wait_full(act, f"o{u}", i)
                        banks.move_done(act.activation(o[:, u, :], bank(f"o{u}", S, D), ACT.Copy), f"o{u}")
                    for u in range(2):
                        banks.wait_full(act, f"t{u}", i)
                        banks.move_done(act.activation(oT[:, u], bank(f"t{u}", 128, KC, S), ACT.Copy), f"t{u}")

            @block.vector
            def _(dve):
                dve.wait_ge(loaded, LOADED)
                first = Chain(sem("d_dve_first"), LN_STEPS)
                layer_norm(dve, ln, first, 0, 0, [X[:, u, :] for u in range(2)])
                with dve.Fori(0, TURNS) as i:
                    for u in range(2):
                        chain.done(dve.tensor_tensor(X[:, 2 * i + u, :], X[:, 2 * i + u, :], bo[:], ALU.add))
                    for j in range(T // 2):
                        banks.wait_full(dve, f"q{j}", i)
                        for t in range(2):
                            last = dve.scalar_tensor_tensor(
                                qT[:, t], bank(f"q{j}", 128, 2, 2 * S)[:, t, :].unsqueeze(1).broadcast_to([128, HT, 2 * S]),
                                bq[:, t:t + 1], k.one_rows[:].unsqueeze(2).broadcast_to([128, HT, 2 * S]),
                                ALU.add, ALU.mult)
                        banks.move_done(last, f"q{j}")
                    for u in range(2):
                        banks.wait_full(dve, f"v{u}", i)
                        banks.move_done(dve.tensor_tensor(v[:, u, :], bank(f"v{u}", S, D), bv[:], ALU.add), f"v{u}")
                    layer_norm(dve, ln, chain, i + 1, i, [X[:, 2 * i + 2 + u, :] for u in range(2)])
                    for u in range(2):
                        for r in range(H // GH):
                            banks.wait_full(dve, f"s{u}{r}", i)
                            banks.move_done(dve.tensor_tensor(
                                sT[:, u, r * GH:(r + 1) * GH], bank(f"s{u}{r}", S, GH, S),
                                k.keep[:].unsqueeze(1).broadcast_to([S, GH, S]), ALU.mult), f"s{u}{r}")
                    for u in range(2):
                        banks.wait_full(dve, f"y{u}", i)
                        banks.move_done(dve.tensor_tensor(X[:, 2 * i + u, :], X[:, 2 * i + u, :],
                                                          bank(f"y{u}", S, D), ALU.add), f"y{u}")
                    chain.end()
        banks.done(TURNS)
        xb.done(TURNS + 1)


class Ranking:

    def __init__(self, sb):
        self.above, self.equal = sb("above", [S, 2, 8, 8]), sb("equal", [S, 2, 8, 8])
        self.rank, self.sel = sb("rank", [S, 2, 8]), sb("sel", [S, 2, 8])


def chosen_by_rank(link, dve, k, r, score, count):
    wide = [S, 2, 8, 8]
    mine = score.unsqueeze(3).broadcast_to(wide)
    other = score.unsqueeze(2).broadcast_to(wide)
    link(dve.tensor_tensor(r.above[:], other, mine, ALU.is_gt))
    link(dve.tensor_tensor(r.equal[:], other, mine, ALU.is_equal))
    link(dve.tensor_tensor(r.equal[:], r.equal[:], k.ahead[:].unsqueeze(1).broadcast_to(wide), ALU.mult))
    link(dve.tensor_tensor(r.above[:], r.above[:], r.equal[:], ALU.add))
    link(dve.tensor_reduce(r.rank[:], r.above[:], AX.X, ALU.add))
    link(dve.tensor_scalar(r.sel[:], r.rank[:], float(count), None, ALU.is_lt))


RANK_STEPS = 6


class Dispatch:

    def __init__(self, k, sb, name, rows, top, y_rows):
        nc = k.nc
        self.rows, self.top, self.y_rows = rows, top, y_rows
        self.xn = nc.dram_tensor(name + "_xn_rows", (B * S, D), F32).ap()
        self.token = nc.dram_tensor(name + "_token_of_row", (rows, 1), I32).ap()
        self.y = nc.dram_tensor(name + "_y_rows", (y_rows, D), F32).ap()
        self.row, self.weight = sb(name + "_row", [S, B, top], I32), sb(name + "_weight", [S, B, top], F32)


TILES = 2 * B * S // 128 + 7
NO_TOKEN = 1 << 20
DROPPED = 32768.0


def route(k, w, name, E, xall, dispatch):
    nc, X = k.nc, k.X
    TURNS = B // 2
    GROUPS, TOP, CAP, FACTOR = 8, 8, 256, 2.5
    with ExitStack() as ctx:
        def sb(n, shape):
            return ctx.enter_context(nc.sbuf_tensor(f"{name}_{n}", shape, F32))

        def sem(n):
            return k.sem(f"{name}_{n}")

        gate = sb("gate", [128, KC, E])
        ln = Norm(lambda n, shape: ctx.enter_context(nc.sbuf_tensor(n, shape, F32)), k.sem, name, k.half)
        xT = sb("xT", [128, KC, 2, S])
        logits = sb("logits", [S, 2, E])
        r = Ranking(sb)
        top, total = sb("top", [S, 2]), sb("total", [S, 2])
        expd = sb("expd", [S, 2, E])
        loaded, act_asked, act_done = sem("loaded"), sem("act_asked"), sem("act_done")
        before = sb("before", [S, 2, E])
        choices_ready = sem("choices_ready")
        constants, table_clear, stored = sem("constants"), sem("table_clear"), sem("xn_stored")
        table_parts = dispatch.rows // 128
        no_token = ctx.enter_context(nc.sbuf_tensor(name + "_no_token", [table_parts, 128], I32))
        if E == 8:
            places, chosen, comb = (sb(n, [S, B, E]) for n in ("places", "chosen", "comb"))
            keys, match = sb("keys", [S, B, E]), sb("match", [S, B, E])
            FULL = B * S // 128
            starts, spans = sb("starts", [S, FULL]), sb("spans", [S, E, FULL])
            counts, tiles, first_tile = sb("counts", [S, E]), sb("tiles", [S, E]), sb("first_tile", [S, E])
            firsts, ends, offset = sb("firsts", [S, E, E]), sb("ends", [S, E]), sb("offset", [S, E])
            tile_no, passed_by = sb("tile_no", [S, TILES + 2]), sb("passed_by", [S, TILES + 2, E])
            expert_f = sb("expert_f", [S, TILES + 2])
            high, low = sb("high", [S, B]), sb("low", [S, B])
        if E == 64:
            ebias = sb("ebias", [S, E])
            biased, masked, left = sb("biased", [S, 2, E]), sb("masked", [S, 2, E]), sb("left", [S, 2, E])
            best = sb("best", [S, 2, GROUPS, 8])
            gscore = sb("gscore", [S, 2, GROUPS])
            best8 = sb("best8", [S, 2, TOP])
            taken = sb("taken", [S, 2, E])
            passed, started = sem("passed"), sem("started")
            weight = sb("choice_weight", [S, 2, E])
            row1 = sb("row1", [128, E])
            late = sb("late", [S, 2, E])
            key = sb("key", [S, 2, E])
            key8 = sb("key8", [S, 2, TOP])
            match = sb("match", [S, 2, TOP, E])
            rows_now = ctx.enter_context(nc.sbuf_tensor(name + "_rows_now", [S, 2, TOP], I32))
            token_now = ctx.enter_context(nc.sbuf_tensor(name + "_token_now", [S, 2], I32))
            token_f = sb("token_f", [S, 2])
            rows_ready, sent, tokens_ready = sem("rows_ready"), sem("sent"), sem("tokens_ready")
            rows_free = sem("rows_free")
        banks, xb = Banks(k, 0, 7), Banks(k, 7, 1).plan(["xT"])
        banks.plan(["l", "c"]).done(TURNS)
        totals = Banks(k, 0, 1).plan(["n"])
        steps = {8: LN_STEPS + RANK_STEPS + 7, 64: LN_STEPS + RANK_STEPS + 30}[E]
        chain = Chain(sem("dve_step"), steps)
        with nc.Block() as block:
            @block.sync
            def _(sp):
                sp.dma_start(gate[:], w["gate"].rearrange("(c p) n -> p c n", p=128)).then_inc(loaded, 16)
                if E == 64:
                    sp.dma_start(ebias[:], w["ebias"].partition_broadcast(S)).then_inc(loaded, 16)
                sp.wait_ge(constants, 1)
                sp.dma_start(dispatch.token.rearrange("(p n) o -> p (n o)", n=128), no_token[:])\
                  .then_inc(table_clear, 16)
                rows_of = dispatch.xn.rearrange("(b s) d -> s b d", s=S)
                with sp.Fori(0, TURNS) as i:
                    sp.wait_ge(ln.xn_ready, i * 2 + 2)
                    sp.dma_start(rows_of[:, bass.ds(i * 2, 2), :], ln.xn[:]).then_inc(stored, 16)
                sp.wait_ge(stored, TURNS * 16)
                sp.wait_ge(table_clear, 16)

            LOADED = 16 if E == 8 else 32

            @block.gpsimd
            def _(pool):
                pool.memset(no_token[:], NO_TOKEN).then_inc(constants, 1)
                pool.wait_ge(constants, 1)
                if E == 8:
                    pool.iota(starts[:], pattern=[[128, FULL]], base=0, channel_multiplier=0,
                              allow_small_or_imprecise_dtypes=True).then_inc(constants, 1)
                    pool.wait_ge(constants, 2)
                    pool.iota(tile_no[:], pattern=[[1, TILES + 2]], base=-1, channel_multiplier=0,
                              allow_small_or_imprecise_dtypes=True).then_inc(constants, 1)
                    pool.wait_ge(constants, 3)
                else:
                    pool.iota(row1[:], pattern=[[2, E]], base=1, channel_multiplier=0,
                              allow_small_or_imprecise_dtypes=True).then_inc(constants, 1)
                    pool.wait_ge(constants, 2)
                    pool.iota(token_f[:], pattern=[[S, 2]], base=0, channel_multiplier=1,
                              allow_small_or_imprecise_dtypes=True).then_inc(constants, 1)
                    pool.wait_ge(constants, 3)
                layer_norm_rstd(pool, ln, 0)
                if E == 64:
                    pool.sem_inc(rows_free, 1)
                    pool.wait_ge(table_clear, 16)
                with pool.Fori(0, TURNS) as i:
                    layer_norm_rstd(pool, ln, i + 1)
                    if E == 64:
                        pool.wait_ge(rows_ready, i + 1)
                        pool.sem_inc(started, 1)
                        for u in range(2):
                            for n in range(TOP):
                                pool.indirect_dma_start(
                                    out=dispatch.token, in_=token_now[:, u:u + 1], in_offset=None,
                                    out_offset=bass.IndirectOffsetOnAxis(
                                        ap=rows_now[:, u, n:n + 1].bitcast(U32), axis=0),
                                    bounds_check=dispatch.rows - 1, oob_is_err=False).then_inc(sent, 16)
                        pool.wait_ge(sent, i * (2 * TOP * 16) + 2 * TOP * 16)
                        pool.sem_inc(rows_free, 1)

            @block.tensor
            def _(pe):
                pe.wait_ge(loaded, LOADED)
                turn_norm(pe, k, ln, xb, 0)
                with pe.Fori(0, TURNS) as i:
                    banks.wait_free(pe, "l", i)
                    xb.wait_moved(pe, i, "xT")
                    for u in range(2):
                        for c in range(KC):
                            last = pe.matmul(banks.at("l", S, 2, E)[:, u, :], xT[:, c, u, :], gate[:, c, :],
                                             start=(c == 0), stop=(c == KC - 1))
                    banks.fill_done(last, "l")
                    turn_norm(pe, k, ln, xb, i + 1)
                    taken_now = r.sel if E == 8 else taken
                    banks.wait_free(pe, "c", i)
                    pe.wait_ge(choices_ready, i + 1)
                    for u in range(2):
                        pe.matmul(banks.at("c", S, 2, E)[:, u, :], k.earlier[:], taken_now[:, u, :],
                                  start=True, stop=False)
                        last = pe.matmul(banks.at("c", S, 2, E)[:, u, :], k.ones[:], before[:, u, :],
                                         start=False, stop=True)
                    banks.fill_done(last, "c")
                if E == 8:
                    totals.wait_free(pe, "n", 0)
                    pe.wait_ge(choices_ready, TURNS + 1)
                    totals.fill_done(pe.matmul(totals.at("n", S, E), k.ones[:], before[:, 0, :],
                                               start=True, stop=True), "n")

            @block.scalar
            def _(act):
                def move_norm(t):
                    xb.wait_full(act, "xT", t)
                    act.activation(xT[:], xb.at("xT", 128, KC, 2, S), ACT.Copy)
                    xb.move_done(act.activation(xall[:, :, bass.ds(t * 2, 2), :], xb.at("xT", 128, KC, 2, S),
                                                ACT.Copy), "xT")

                move_norm(0)
                with act.Fori(0, TURNS) as i:
                    act.wait_ge(act_asked, i + 1)
                    act.activation(expd[:], logits[:], ACT.Exp if E == 8 else ACT.Sigmoid).then_inc(act_done, 1)
                    move_norm(i + 1)

            @block.vector
            def _(dve):
                first = Chain(sem("dve_first"), LN_STEPS)
                layer_norm(dve, ln, first, 0, 0, [X[:, u, :] for u in range(2)])
                dve.wait_ge(constants, 3)
                if E == 64:
                    dve.wait_ge(loaded, LOADED)
                first.link(dve, 0, dve.memset(before[:, 0, :], 0.0))
                with dve.Fori(0, TURNS) as i:
                    def link(ins):
                        chain.link(dve, i, ins)

                    if E == 8:
                        banks.wait_full(dve, "l", i)
                        banks.move_done(dve.tensor_copy(logits[:], banks.at("l", S, 2, E)), "l")
                        banks.wait_moved(dve, i, "l")
                        chosen_by_rank(link, dve, k, r, logits[:], 2)
                        dve.tensor_tensor(before[:, 1, :], before[:, 0, :], r.sel[:, 0, :], ALU.add)\
                           .then_inc(choices_ready, 1)
                        link(dve.tensor_reduce(top[:], logits[:], AX.X, ALU.max))
                        dve.tensor_tensor(logits[:], logits[:], top[:].unsqueeze(2).broadcast_to([S, 2, E]),
                                          ALU.subtract).then_inc(act_asked, 1)
                        layer_norm(dve, ln, chain, i + 1, i, [X[:, 2 * i + 2 + u, :] for u in range(2)], stored)
                        banks.wait_full(dve, "c", i)
                        banks.move_done(dve.tensor_copy(places[:, bass.ds(2 * i, 2), :], banks.at("c", S, 2, E)), "c")
                        chain.done(dve.tensor_copy(chosen[:, bass.ds(2 * i, 2), :], r.sel[:]))
                        link(dve.tensor_tensor(before[:, 0, :], before[:, 1, :], r.sel[:, 1, :], ALU.add))
                        dve.wait_ge(act_done, i + 1)
                        link(dve.tensor_tensor(expd[:], expd[:], r.sel[:], ALU.mult))
                        link(dve.tensor_reduce(total[:], expd[:], AX.X, ALU.add))
                        link(dve.reciprocal(total[:], total[:]))
                        link(dve.tensor_tensor(comb[:, bass.ds(2 * i, 2), :], expd[:],
                                               total[:].unsqueeze(2).broadcast_to([S, 2, E]), ALU.mult))
                    else:
                        banks.wait_full(dve, "l", i)
                        banks.move_done(dve.tensor_copy(logits[:], banks.at("l", S, 2, E)), "l")
                        banks.wait_moved(dve, i, "l")
                        dve.sem_inc(act_asked, 1)
                        layer_norm(dve, ln, chain, i + 1, i, [X[:, 2 * i + 2 + u, :] for u in range(2)],
                                   stored)
                        dve.wait_ge(act_done, i + 1)
                        wide = [S, 2, E]
                        link(dve.tensor_tensor(biased[:], expd[:], ebias[:].unsqueeze(1).broadcast_to(wide), ALU.add))
                        dve.sem_inc(passed, 1)
                        for u in range(2):
                            for g in range(GROUPS):
                                last = dve.max(best[:, u, g, :], biased[:, u, g * 8:(g + 1) * 8])
                        link(last)
                        link(dve.tensor_tensor(gscore[:], best[:, :, :, 0], best[:, :, :, 1], ALU.add))
                        chosen_by_rank(link, dve, k, r, gscore[:], 4)
                        link(dve.tensor_tensor(
                            masked[:].rearrange("p u (g e) -> p u g e", g=GROUPS),
                            biased[:].rearrange("p u (g e) -> p u g e", g=GROUPS),
                            r.sel[:].unsqueeze(3).broadcast_to([S, 2, GROUPS, 8]), ALU.mult))
                        link(dve.tensor_scalar(masked[:], masked[:], 0.0, None, ALU.add))
                        dve.sem_inc(passed, 1)
                        for u in range(2):
                            last = dve.max(best8[:, u, :], masked[:, u, :])
                        link(last)
                        dve.sem_inc(passed, 1)
                        for u in range(2):
                            last = dve.match_replace(left[:, u, :], best8[:, u, :], masked[:, u, :], -3.0e38)
                        link(last)
                        link(dve.tensor_scalar(taken[:], left[:], -1.0e38, None, ALU.is_lt))
                        dve.tensor_tensor(before[:, 1, :], before[:, 0, :], taken[:, 0, :], ALU.add)\
                           .then_inc(choices_ready, 1)
                        link(dve.tensor_tensor(expd[:], expd[:], taken[:], ALU.mult))
                        link(dve.tensor_reduce(total[:], expd[:], AX.X, ALU.add))
                        link(dve.tensor_scalar(total[:], total[:], 1e-20, None, ALU.add))
                        link(dve.reciprocal(total[:], total[:]))
                        link(dve.tensor_tensor(expd[:], expd[:], total[:].unsqueeze(2).broadcast_to(wide), ALU.mult))
                        banks.wait_full(dve, "c", i)
                        place = banks.at("c", S, 2, E)
                        link(dve.tensor_scalar(left[:], place, float(CAP), None, ALU.is_lt))
                        link(dve.tensor_scalar(late[:], place, float(CAP), DROPPED, ALU.is_ge, ALU.mult))
                        link(dve.tensor_scalar(masked[:], place, 128.0, -float(dispatch.rows - 1), ALU.is_ge, ALU.mult))
                        banks.move_done(dve.tensor_scalar(key[:], place, float(CAP - 1), 128.0, ALU.min, ALU.mult), "c")
                        banks.wait_moved(dve, i, "c")
                        link(dve.tensor_tensor(key[:], key[:], row1[0:S].unsqueeze(1).broadcast_to(wide), ALU.add))
                        link(dve.tensor_tensor(late[:], late[:], masked[:], ALU.add))
                        link(dve.tensor_tensor(key[:], key[:], late[:], ALU.add))
                        link(dve.tensor_tensor(key[:], key[:], taken[:], ALU.mult))
                        link(dve.tensor_tensor(before[:, 0, :], before[:, 1, :], taken[:, 1, :], ALU.add))
                        link(dve.scalar_tensor_tensor(weight[:], expd[:], FACTOR, left[:], ALU.mult, ALU.mult))
                        dve.sem_inc(passed, 1)
                        for u in range(2):
                            last = dve.max(key8[:, u, :], key[:, u, :])
                        link(last)
                        dve.wait_ge(rows_free, i + 1)
                        dve.tensor_scalar(rows_now[:], key8[:], -1.0, None, ALU.add).then_inc(tokens_ready, 1)
                        dve.wait_ge(tokens_ready, i + 1)
                        dve.tensor_scalar(token_now[:], token_f[:], 0.0, None, ALU.add).then_inc(rows_ready, 1)
                        dve.wait_ge(rows_ready, i + 1)
                        link(dve.tensor_scalar(token_f[:], token_f[:], float(2 * S), None, ALU.add))
                        full = [S, 2, TOP, E]
                        link(dve.tensor_tensor(match[:], key[:].unsqueeze(2).broadcast_to(full),
                                               key8[:].unsqueeze(3).broadcast_to(full), ALU.is_equal))
                        link(dve.tensor_tensor(match[:], match[:], weight[:].unsqueeze(2).broadcast_to(full), ALU.mult))
                        chain.done(dve.tensor_reduce(dispatch.weight[:, bass.ds(2 * i, 2), :], match[:], AX.X, ALU.add))
                        link(dve.tensor_scalar(best8[:], key8[:], DROPPED, -DROPPED, ALU.is_gt, ALU.mult))
                        link(dve.tensor_tensor(best8[:], best8[:], key8[:], ALU.add))
                        link(dve.tensor_scalar(dispatch.row[:, bass.ds(2 * i, 2), :], best8[:], -1.0, None, ALU.add))
                    chain.end()
                if E == 8:
                    last_steps = Chain(sem("last_step"), 0)

                    def then(ins):
                        last_steps.link(dve, 0, ins)

                    dve.sem_inc(choices_ready, 1)
                    totals.wait_full(dve, "n", 0)
                    totals.move_done(dve.tensor_copy(counts[:], totals.at("n", S, E)), "n")
                    totals.wait_moved(dve, 0, "n")
                    span, pair = [S, E, FULL], [S, E, E]
                    then(dve.tensor_tensor(spans[:], counts[:].unsqueeze(2).broadcast_to(span),
                                           starts[:].unsqueeze(1).broadcast_to(span), ALU.is_gt))
                    then(dve.tensor_reduce(tiles[:], spans[:], AX.X, ALU.add))
                    then(dve.tensor_tensor(firsts[:], k.ahead[:], tiles[:].unsqueeze(1).broadcast_to(pair), ALU.mult))
                    then(dve.tensor_reduce(first_tile[:], firsts[:], AX.X, ALU.add))
                    then(dve.tensor_tensor(ends[:], first_tile[:], tiles[:], ALU.add))
                    slot = [S, TILES + 2, E]
                    then(dve.tensor_tensor(passed_by[:], tile_no[:].unsqueeze(2).broadcast_to(slot),
                                           ends[:].unsqueeze(1).broadcast_to(slot), ALU.is_ge))
                    then(dve.tensor_reduce(expert_f[:], passed_by[:], AX.X, ALU.add))
                    then(dve.tensor_scalar(dispatch.expert[:], expert_f[:], float(E - 1), None, ALU.min))
                    then(dve.tensor_scalar(offset[:], first_tile[:], 128.0, 1.0, ALU.mult, ALU.add))
                    wide = [S, B, E]
                    then(dve.tensor_tensor(keys[:], places[:], offset[:].unsqueeze(1).broadcast_to(wide), ALU.add))
                    then(dve.tensor_tensor(keys[:], keys[:], chosen[:], ALU.mult))
                    then(dve.tensor_reduce(high[:], keys[:], AX.X, ALU.max))
                    then(dve.tensor_reduce(low[:], keys[:], AX.X, ALU.add))
                    then(dve.tensor_tensor(low[:], low[:], high[:], ALU.subtract))
                    for n, key_of in enumerate((high, low)):
                        then(dve.tensor_tensor(match[:], keys[:], key_of[:].unsqueeze(2).broadcast_to(wide),
                                               ALU.is_equal))
                        then(dve.tensor_tensor(match[:], match[:], comb[:], ALU.mult))
                        then(dve.tensor_reduce(dispatch.weight[:, :, n], match[:], AX.X, ALU.add))
                        then(dve.tensor_scalar(dispatch.send_row[:, :, n], key_of[:], -1.0, None, ALU.add))
                        then(dve.tensor_scalar(dispatch.row[:, :, n], key_of[:], 127.0, None, ALU.add))
        if E == 8:
            totals.done(1)
        xb.done(TURNS + 1)


def shared_expert(k, w, name, width, xall, beside=None):
    nc, X = k.nc, k.X
    IT = -(-width // 128)
    I = IT * 128
    NB = 4
    TURNS = B // NB
    with ExitStack() as ctx:
        def sb(n, shape):
            return ctx.enter_context(nc.sbuf_tensor(f"{name}_{n}", shape, F32))

        wg, wu, wd = sb("wg", [128, KC, I]), sb("wu", [128, KC, I]), sb("wd", [128, IT, D])
        gated, h = sb("gated", [128, IT, NB * S]), sb("h", [128, IT, NB * S])
        loaded = k.sem(f"{name}_loaded")
        names = [f"{a}{t}" for t in range(IT) for a in "gu"] + [f"y{n}" for n in range(NB // 2)]
        banks = Banks(k, 0, 8).plan(names)
        with nc.Block() as block:
            @block.sync
            def _(sp):
                sp.dma_start(wg[:], w["G"].rearrange("(c p) n -> p c n", p=128)).then_inc(loaded, 16)
                sp.dma_start(wu[:], w["U"].rearrange("(c p) n -> p c n", p=128)).then_inc(loaded, 16)
                sp.dma_start(wd[:], w["D"].rearrange("(t p) n -> p t n", p=128)).then_inc(loaded, 16)
                if beside is not None:
                    beside.sync(sp)

            @block.gpsimd
            def _(pool):
                if beside is not None:
                    beside.gpsimd(pool)

            @block.tensor
            def _(pe):
                pe.wait_ge(loaded, 48)
                with pe.Fori(0, TURNS) as j:
                    xs = [xall[:, c, bass.ds(j * NB, NB), :].rearrange("p b s -> p (b s)") for c in range(KC)]
                    for t in range(IT):
                        for nm, wt in (("g", wg), ("u", wu)):
                            banks.wait_free(pe, f"{nm}{t}", j)
                            for c in range(KC):
                                last = pe.matmul(banks.at(f"{nm}{t}", 128, NB * S), wt[:, c, t * 128:(t + 1) * 128],
                                                 xs[c], start=(c == 0), stop=(c == KC - 1))
                            banks.fill_done(last, f"{nm}{t}")
                    for n in range(NB // 2):
                        banks.wait_free(pe, f"y{n}", j, *[f"u{t}" for t in range(IT)])
                        for b in range(2):
                            for t in range(IT):
                                s0 = (2 * n + b) * S
                                last = pe.matmul(banks.at(f"y{n}", S, 2, D)[:, b, :], h[:, t, s0:s0 + S],
                                                 wd[:, t, :], start=(t == 0), stop=(t == IT - 1))
                        banks.fill_done(last, f"y{n}")

            @block.scalar
            def _(act):
                with act.Fori(0, TURNS) as j:
                    for t in range(IT):
                        banks.wait_full(act, f"g{t}", j)
                        banks.move_done(act.activation(gated[:, t, :], banks.at(f"g{t}", 128, NB * S), ACT.Silu),
                                        f"g{t}")

            @block.vector
            def _(dve):
                if beside is not None:
                    beside.vector_start(dve)
                with dve.Fori(0, TURNS) as j:
                    for t in range(IT):
                        banks.wait_moved(dve, j, f"g{t}")
                        banks.wait_full(dve, f"u{t}", j)
                        banks.move_done(dve.tensor_tensor(h[:, t, :], gated[:, t, :],
                                                          banks.at(f"u{t}", 128, NB * S), ALU.mult), f"u{t}")
                    if beside is not None:
                        beside.vector(dve, j)
                    for n in range(NB // 2):
                        banks.wait_full(dve, f"y{n}", j)
                        at = j * NB + 2 * n
                        banks.move_done(dve.tensor_tensor(X[:, bass.ds(at, 2), :], X[:, bass.ds(at, 2), :],
                                                          banks.at(f"y{n}", S, 2, D), ALU.add), f"y{n}")
        banks.done(TURNS)


class Sending:
    NB = 4

    def __init__(self, k, sb, name, dispatch, wgu, w, gu_loaded):
        self.dispatch, self.wgu, self.w, self.gu_loaded = dispatch, wgu, w, gu_loaded
        self.tokens = sb(name + "_tokens", [S, B], I32)
        self.rows_now, self.token_now = sb(name + "_rows_now", [S, self.NB, 2], I32), sb(name + "_token_now", [S, self.NB], I32)
        self.ready, self.sent, self.started = (k.sem(f"{name}_{n}") for n in ("ready", "sent", "started"))

    def sync(self, sp):
        for e in range(8):
            sp.dma_start(self.wgu[:, e, 0], self.w["G"][e].rearrange("(c p) n -> p c n", p=128))\
              .then_inc(self.gu_loaded, 16)
            sp.dma_start(self.wgu[:, e, 1], self.w["U"][e].rearrange("(c p) n -> p c n", p=128))\
              .then_inc(self.gu_loaded, 16)

    def gpsimd(self, pool):
        NB = self.NB
        d = self.dispatch
        pool.iota(self.tokens[:], pattern=[[S, B]], base=0, channel_multiplier=1).then_inc(self.ready, 1)
        pool.wait_ge(self.ready, 1)
        with pool.Fori(0, B // NB) as i:
            pool.tensor_copy(self.rows_now[:], d.send_row[:, bass.ds(i * NB, NB), :]).then_inc(self.ready, 1)
            pool.tensor_copy(self.token_now[:], self.tokens[:, bass.ds(i * NB, NB)]).then_inc(self.ready, 1)
            pool.wait_ge(self.ready, i * 2 + 3)
            pool.sem_inc(self.started, 1)
            for b in range(NB):
                for n in range(2):
                    pool.indirect_dma_start(
                        out=d.token, in_=self.token_now[:, b:b + 1], in_offset=None,
                        out_offset=bass.IndirectOffsetOnAxis(ap=self.rows_now[:, b, n:n + 1].bitcast(U32), axis=0),
                        bounds_check=d.rows - 1, oob_is_err=False).then_inc(self.sent, 16)
            pool.wait_ge(self.sent, i * (2 * NB * 16) + 2 * NB * 16)
            pool.sem_inc(self.started, 1)

    def vector_start(self, dve):
        pass

    def vector(self, dve, j):
        pass


def sorted_experts(k, w, name, dispatch, wgu, gu_loaded):
    nc = k.nc
    TURNS = TILES + 1
    assert TURNS % 2 == 0
    WIDTH = 704
    HALF = WIDTH // 2
    IT = -(-WIDTH // 128)
    with ExitStack() as ctx:
        def sb(n, shape, dt=F32):
            return ctx.enter_context(nc.sbuf_tensor(f"{name}_{n}", shape, dt))

        def sem(n):
            return k.sem(f"{name}_{n}")

        wd = sb("wd", [128, 8, IT, D])
        token_rows = sb("token_rows", [TILES + 2, 128], I32)
        token_f, token = sb("token_f", [TILES + 2, 128]), sb("token", [128, TILES + 2], I32)
        token_now = sb("token_now", [128, 2], I32)
        xg, xT = sb("xg", [128, 2, D]), sb("xT", [128, KC, 128])
        gated, h, hT = sb("gated", [128, 2, HALF]), sb("h", [128, IT * 128]), sb("hT", [128, IT, 128])
        y = sb("y", [128, 2, D])
        tokens_loaded, d_loaded, converted = sem("tokens_loaded"), sem("d_loaded"), sem("converted")
        cleared, token_ready, started = sem("cleared"), sem("token_ready"), sem("started")
        gathered = [sem(f"gathered{v}") for v in range(2)]
        y_stored = [sem(f"y_stored{v}") for v in range(2)]
        table = Banks(k, 7, 1).plan(["table"])
        table.done(1)
        banks = Banks(k, 0, 6).plan(["g0", "g1", "t0", "t1", "u0", "u1"])
        xb, yb = Banks(k, 6, 1).plan(["x"]), Banks(k, 7, 1).plan(["y"])
        with nc.Block() as block:
            @block.sync
            def _(sp):
                sp.dma_start(token_rows[:], dispatch.token.rearrange("(t p) o -> t (p o)", p=128))\
                  .then_inc(tokens_loaded, 16)
                for e in range(8):
                    sp.dma_start(wd[:, e], w["D"][e].rearrange("(t p) n -> p t n", p=128)).then_inc(d_loaded, 16)
                for v in range(2):
                    sp.sem_inc(y_stored[v], 16)
                y_rows = dispatch.y.rearrange("(j p) d -> p j d", p=128)
                with sp.Fori(0, TURNS // 2) as m:
                    for v in range(2):
                        yb.wait_moved(sp, 2 * m + v, "y")
                        sp.dma_start(y_rows[:, bass.ds(2 * m + v, 1), :], y[:, v:v + 1, :]).then_inc(y_stored[v], 16)
                for v in range(2):
                    sp.wait_ge(y_stored[v], (TURNS // 2) * 16 + 16)

            @block.gpsimd
            def _(pool):
                pool.memset(xg[:], 0.0).then_inc(cleared, 1)
                pool.memset(h[:], 0.0).then_inc(cleared, 1)
                pool.wait_ge(cleared, 2)
                pool.wait_ge(converted, 2)

                def gather(t, v):
                    xb.wait_full(pool, "x", t - 2)
                    pool.sem_inc(started, 1)
                    pool.tensor_copy(token_now[:, v:v + 1], token[:, bass.ds(t, 1)]).then_inc(token_ready, 1)
                    pool.wait_ge(token_ready, t + 1)
                    pool.sem_inc(started, 1)
                    pool.indirect_dma_start(
                        out=xg[:, v, :], out_offset=None, in_=dispatch.xn,
                        in_offset=bass.IndirectOffsetOnAxis(ap=token_now[:, v:v + 1].bitcast(U32), axis=0),
                        bounds_check=B * S - 1, oob_is_err=False).then_inc(gathered[v], 16)

                gather(0, 0)
                with pool.Fori(0, TURNS // 2) as m:
                    for v in range(2):
                        gather(2 * m + (v + 1), (v + 1) % 2)

            @block.tensor
            def _(pe):
                table.wait_free(pe, "table", 0)
                pe.wait_ge(converted, 1)
                table.fill_done(pe.transpose(table.at("table", 128, TILES + 2), token_f[:],
                                             k.ident[0:TILES + 2, 0:TILES + 2]), "table")

                def turn_x(t, v, gathers):
                    xb.wait_free(pe, "x", t)
                    pe.wait_ge(gathered[v], gathers * 16)
                    for c in range(KC):
                        last = pe.transpose(xb.at("x", 128, KC, 128)[:, c, :], xg[:, v, c * 128:(c + 1) * 128],
                                            k.ident[:])
                    xb.fill_done(last, "x")

                turn_x(0, 0, 1)
                pe.wait_ge(cleared, 2)
                pe.wait_ge(gu_loaded, 2 * 8 * 16)
                pe.wait_ge(d_loaded, 8 * 16)
                with pe.Fori(0, TURNS // 2) as m:
                    for v in range(2):
                        j = 2 * m + v
                        before = pe.value_load(dispatch.expert[0:1, bass.ds(j, 1)], min_val=0, max_val=7)
                        now = pe.value_load(dispatch.expert[0:1, bass.ds(j + 1, 1)], min_val=0, max_val=7)

                        def widen(a, what):
                            for s in range(2):
                                banks.wait_free(pe, f"{a}{s}", j)
                                if a == "g" and s == 0:
                                    xb.wait_moved(pe, j, "x")
                                for c in range(KC):
                                    last = pe.matmul(banks.at(f"{a}{s}", 128, HALF), xT[:, c, :],
                                                     wgu[:, bass.ds(now, 1), what, c, s * HALF:(s + 1) * HALF]
                                                     .rearrange("p o n -> p (o n)"),
                                                     start=(c == 0), stop=(c == KC - 1))
                                banks.fill_done(last, f"{a}{s}")

                        widen("g", 0)
                        for s, ts in enumerate((range(4), range(4, IT))):
                            banks.wait_free(pe, f"t{s}", j)
                            if s == 0:
                                banks.wait_moved(pe, j - 1, "u0", "u1")
                            for n, t in enumerate(ts):
                                last = pe.transpose(banks.at(f"t{s}", 128, len(ts), 128)[:, n, :],
                                                    h[:, t * 128:(t + 1) * 128], k.ident[:])
                            banks.fill_done(last, f"t{s}")
                        widen("u", 1)
                        turn_x(j + 1, (v + 1) % 2, m + (v + 1))
                        yb.wait_free(pe, "y", j)
                        banks.wait_moved(pe, j, "t0", "t1")
                        for t in range(IT):
                            last = pe.matmul(yb.at("y", 128, D), hT[:, t, :],
                                             wd[:, bass.ds(before, 1), t, :].rearrange("p o n -> p (o n)"),
                                             start=(t == 0), stop=(t == IT - 1))
                        yb.fill_done(last, "y")

            @block.scalar
            def _(act):
                def move_x(t):
                    xb.wait_full(act, "x", t)
                    xb.move_done(act.activation(xT[:], xb.at("x", 128, KC, 128), ACT.Copy), "x")

                move_x(0)
                with act.Fori(0, TURNS // 2) as m:
                    for v in range(2):
                        j = 2 * m + v
                        for s in range(2):
                            banks.wait_moved(act, j - 1, f"u{s}")
                            banks.wait_full(act, f"g{s}", j)
                            banks.move_done(act.activation(gated[:, s, :], banks.at(f"g{s}", 128, HALF), ACT.Silu),
                                            f"g{s}")
                        banks.wait_full(act, "t0", j)
                        banks.move_done(act.activation(hT[:, 0:4, :], banks.at("t0", 128, 4, 128), ACT.Copy), "t0")
                        move_x(j + 1)

            @block.vector
            def _(dve):
                dve.wait_ge(tokens_loaded, 16)
                dve.tensor_copy(token_f[:], token_rows[:]).then_inc(converted, 1)
                table.wait_full(dve, "table", 0)
                table.move_done(dve.tensor_copy(token[:], table.at("table", 128, TILES + 2)), "table")
                table.wait_moved(dve, 0, "table")
                dve.sem_inc(converted, 1)
                dve.wait_ge(cleared, 2)
                with dve.Fori(0, TURNS // 2) as m:
                    for v in range(2):
                        j = 2 * m + v
                        banks.wait_full(dve, "t1", j)
                        banks.move_done(dve.tensor_copy(hT[:, 4:IT, :], banks.at("t1", 128, IT - 4, 128)), "t1")
                        for s in range(2):
                            banks.wait_moved(dve, j, f"g{s}")
                            banks.wait_full(dve, f"u{s}", j)
                            banks.move_done(dve.tensor_tensor(h[:, s * HALF:(s + 1) * HALF], gated[:, s, :],
                                                              banks.at(f"u{s}", 128, HALF), ALU.mult), f"u{s}")
                        dve.wait_ge(y_stored[v], m * 16 + 16)
                        yb.wait_full(dve, "y", j)
                        yb.move_done(dve.tensor_copy(y[:, v, :], yb.at("y", 128, D)), "y")
        banks.done(TURNS)
        xb.done(TURNS + 1)
        yb.done(TURNS)


def gathered_experts(k, w, name, dispatch):
    nc = k.nc
    Q = 4
    E = 64
    TURNS = E // Q
    NW = 2 * KC * 128 + D
    with ExitStack() as ctx:
        def sb(n, shape, dt=F32):
            return ctx.enter_context(nc.sbuf_tensor(f"{name}_{n}", shape, dt))

        def sem(n):
            return k.sem(f"{name}_{n}")

        wt = sb("w", [128, Q, NW])
        token = sb("token", [128, E * 2], I32)
        token_now = sb("token_now", [128, Q, 2], I32)
        xg = sb("xg", [128, Q, 2, D])
        xT = sb("xT", [128, Q, KC, 256])
        gated, h = sb("gated", [128, Q, 256]), sb("h", [128, Q, 256])
        y = sb("y", [128, Q, 2, D])
        tokens_loaded, cleared, tokens_ready = sem("tokens_loaded"), sem("cleared"), sem("tokens_ready")
        w_loaded = [sem(f"w_loaded{q}") for q in range(Q)]
        gathered = [sem(f"gathered{q}") for q in range(Q)]
        y_stored = [sem(f"y_stored{q}") for q in range(Q)]
        silu_done, started = sem("silu_done"), sem("started")
        banks = Banks(k, 0, 8)
        names = [f"{a}{q}" for a in "xgy" for q in range(Q)]
        banks.plan(names)
        ident = k.ident
        y_rows = dispatch.y.rearrange("(p n) d -> p n d", p=128)
        with nc.Block() as block:
            @block.sync
            def _(sp):
                sp.dma_start(token[:], dispatch.token.rearrange("(p n) o -> p (n o)", p=128)).then_inc(tokens_loaded, 16)
                for q in range(Q):
                    sp.dma_start(wt[:, q], w["all"][q]).then_inc(w_loaded[q], 16)
                with sp.Fori(0, TURNS - 1) as i:
                    for q in range(Q):
                        banks.wait_full(sp, f"y{q}", i)
                        sp.dma_start(wt[:, q], w["all"][i * Q + (Q + q)]).then_inc(w_loaded[q], 16)

            @block.gpsimd
            def _(pool):
                pool.memset(xg[:], 0.0).then_inc(cleared, 1)
                pool.wait_ge(cleared, 1)
                pool.wait_ge(tokens_loaded, 16)
                with pool.Fori(0, TURNS) as i:
                    for q in range(Q):
                        banks.wait_full(pool, f"x{q}", i - 1)
                    pool.sem_inc(started, 1)
                    pool.tensor_copy(token_now[:].rearrange("p q h -> p (q h)"), token[:, bass.ds(i * (2 * Q), 2 * Q)])\
                        .then_inc(tokens_ready, 1)
                    pool.wait_ge(tokens_ready, i + 1)
                    pool.sem_inc(started, 1)
                    for q in range(Q):
                        for half in range(2):
                            pool.indirect_dma_start(
                                out=xg[:, q, half, :], out_offset=None, in_=dispatch.xn,
                                in_offset=bass.IndirectOffsetOnAxis(ap=token_now[:, q, half:half + 1].bitcast(U32), axis=0),
                                bounds_check=B * S - 1, oob_is_err=False).then_inc(gathered[q], 16)

            @block.tensor
            def _(pe):
                with pe.Fori(0, TURNS) as i:
                    for q in range(Q):
                        banks.wait_free(pe, f"x{q}", i)
                        pe.wait_ge(gathered[q], i * 32 + 32)
                        for c in range(KC):
                            for half in range(2):
                                last = pe.transpose(banks.at(f"x{q}", 128, KC, 2, 128)[:, c, half, :],
                                                    xg[:, q, half, c * 128:(c + 1) * 128], ident[:])
                        banks.fill_done(last, f"x{q}")
                    for q in range(Q):
                        banks.wait_free(pe, f"g{q}", i, f"x{q}")
                        pe.wait_ge(w_loaded[q], i * 16 + 16)
                        for m in range(2):
                            for c in range(KC):
                                at = (m * KC + c) * 128
                                last = pe.matmul(banks.at(f"g{q}", 128, 2, 256)[:, m, :], wt[:, q, at:at + 128],
                                                 xT[:, q, c, :], start=(c == 0), stop=(c == KC - 1))
                        banks.fill_done(last, f"g{q}")
                    for q in range(Q):
                        banks.wait_free(pe, f"y{q}", i, f"g{q}")
                        for half in range(2):
                            last = pe.matmul(banks.at(f"y{q}", 128, 2, D)[:, half, :],
                                             h[:, q, half * 128:(half + 1) * 128], wt[:, q, NW - D:NW],
                                             start=True, stop=True)
                        banks.fill_done(last, f"y{q}")

            @block.scalar
            def _(act):
                for q in range(Q):
                    act.sem_inc(y_stored[q], 16)
                with act.Fori(0, TURNS) as i:
                    for q in range(Q):
                        banks.wait_full(act, f"x{q}", i)
                        banks.move_done(act.activation(xT[:, q], banks.at(f"x{q}", 128, KC, 256), ACT.Copy), f"x{q}")
                    for q in range(Q):
                        banks.wait_full(act, f"g{q}", i)
                        act.activation(gated[:, q, :], banks.at(f"g{q}", 128, 2, 256)[:, 0, :], ACT.Silu)\
                           .then_inc(silu_done, 1)
                    for q in range(Q):
                        banks.wait_moved(act, i, f"y{q}")
                        act.dma_start(y_rows[:, bass.ds(i * (2 * Q) + 2 * q, 2), :], y[:, q]).then_inc(y_stored[q], 16)
                for q in range(Q):
                    act.wait_ge(y_stored[q], TURNS * 16 + 16)

            @block.vector
            def _(dve):
                with dve.Fori(0, TURNS) as i:
                    for q in range(Q):
                        dve.wait_ge(silu_done, i * Q + (q + 1))
                        banks.move_done(dve.tensor_tensor(h[:, q, :], gated[:, q, :],
                                                          banks.at(f"g{q}", 128, 2, 256)[:, 1, :], ALU.mult), f"g{q}")
                    for q in range(Q):
                        dve.wait_ge(y_stored[q], i * 16 + 16)
                        banks.wait_full(dve, f"y{q}", i)
                        banks.move_done(dve.tensor_copy(y[:, q], banks.at(f"y{q}", 128, 2, D)), f"y{q}")
        banks.done(TURNS)


class Combining:
    def __init__(self, k, sb, name, dispatch):
        self.k, self.dispatch = k, dispatch
        self.top = dispatch.top
        self.batches = 16 // self.top
        self.turns = B // self.batches
        self.credit = (self.batches - 1) * self.top + 1
        self.rows = sb(name + "_rows", [S, self.batches, self.top], I32)
        self.y = sb(name + "_y", [S, self.batches, self.top, D], F32)
        self.fetched = [k.sem(f"{name}_fetched{u}") for u in range(self.batches)]
        self.rows_ready, self.added, self.started = (k.sem(f"{name}_{n}") for n in ("rows_ready", "added", "started"))

    def sync(self, sp):
        pass

    def gpsimd(self, pool):
        d, NU, TOP = self.dispatch, self.batches, self.top
        with pool.Fori(0, self.turns) as i:
            for u in range(NU):
                pool.wait_ge(self.added, i * (NU * TOP) + (u * TOP + 1))
                pool.sem_inc(self.started, 1)
                pool.tensor_copy(self.rows[:, u], d.row[:, i * NU + u, :]).then_inc(self.rows_ready, 1)
                pool.wait_ge(self.rows_ready, i * NU + (u + 1))
                pool.sem_inc(self.started, 1)
                for n in range(TOP):
                    pool.indirect_dma_start(
                        out=self.y[:, u, n, :], out_offset=None, in_=d.y,
                        in_offset=bass.IndirectOffsetOnAxis(ap=self.rows[:, u, n:n + 1].bitcast(U32), axis=0),
                        bounds_check=d.y_rows - 1, oob_is_err=False).then_inc(self.fetched[u], 16)

    def vector_start(self, dve):
        dve.sem_inc(self.added, self.credit)

    def add(self, dve, i):
        X, d, NU, TOP = self.k.X, self.dispatch, self.batches, self.top
        for u in range(NU):
            dve.wait_ge(self.fetched[u], i * (TOP * 16) + TOP * 16)
            at = i * NU + u
            for n in range(TOP):
                dve.scalar_tensor_tensor(X[:, at, :], self.y[:, u, n, :], d.weight[:, at, n:n + 1],
                                         X[:, at, :], ALU.mult, ALU.add).then_inc(self.added, 1)
                dve.wait_ge(self.added, i * (NU * TOP) + (u * TOP + n + 1 + self.credit))

    def vector(self, dve, j):
        for v in range(4 // self.batches):
            self.add(dve, j * (4 // self.batches) + v)


def combine(k, combining):
    with k.nc.Block() as block:
        @block.gpsimd
        def _(pool):
            combining.gpsimd(pool)

        @block.vector
        def _(dve):
            combining.vector_start(dve)
            with dve.Fori(0, combining.turns) as i:
                combining.add(dve, i)


def layer0_mixture(k, gate, shared, routed):
    nc = k.nc
    with ExitStack() as stage:
        def sb(n, shape, dt=F32):
            return stage.enter_context(nc.sbuf_tensor(n, shape, dt))

        d = Dispatch(k, sb, "c", (TILES + 2) * 128, 2, (TILES + 1) * 128)
        d.send_row = sb("c_send_row", [S, B, 2], I32)
        d.expert = sb("c_expert", [S, TILES + 2], I32)
        gu_loaded = k.sem("c_gu_loaded")
        with ExitStack() as with_x:
            wgu = with_x.enter_context(nc.sbuf_tensor("c_wgu", [128, 8, 2, KC, 704], F32))
            with nc.sbuf_tensor("c_xall", [128, KC, B + 2, S], F32) as xall:
                route(k, gate, "c_gate", 8, xall, d)
                with ExitStack() as small:
                    def sb2(n, shape, dt=F32):
                        return small.enter_context(nc.sbuf_tensor(n, shape, dt))

                    shared_expert(k, shared, "c_shared", 352, xall,
                                  Sending(k, sb2, "c_sending", d, wgu, routed, gu_loaded))
            sorted_experts(k, routed, "c_routed", d, wgu, gu_loaded)
        combine(k, Combining(k, sb, "c_combine", d))


def layer1_mixture(k, gate, shared, routed):
    nc = k.nc
    with ExitStack() as stage:
        def sb(n, shape, dt=F32):
            return stage.enter_context(nc.sbuf_tensor(n, shape, dt))

        d = Dispatch(k, sb, "f", 64 * 256, 8, 64 * 256)
        xall = sb("f_xall", [128, KC, B + 2, S])
        route(k, gate, "f_gate", 64, xall, d)
        gathered_experts(k, routed, "f_experts", d)
        shared_expert(k, shared, "f_shared", 256, xall, Combining(k, sb, "f_combine", d))


def decoder(nc, w, x, ctx_T, out):
    with ExitStack() as ctx:
        def sem(name):
            return ctx.enter_context(nc.semaphore(name))

        k = Shared(nc, sem)
        k.X = ctx.enter_context(nc.sbuf_tensor("X", [S, B + 2, D], F32))
        k.ident = ctx.enter_context(nc.sbuf_tensor("ident", [128, 128], F32))
        k.causal = ctx.enter_context(nc.sbuf_tensor("causal", [S, S], F32))
        k.PS = ctx.enter_context(nc.psum_tensor("PS", [128, 8, 512], F32))
        k.filled, k.moved = [sem(f"bank{b}_filled") for b in range(8)], [sem(f"bank{b}_moved") for b in range(8)]
        k.uses = [0] * 8
        k.keep = ctx.enter_context(nc.sbuf_tensor("keep", [S, S], F32))
        k.earlier = ctx.enter_context(nc.sbuf_tensor("earlier", [S, S], F32))
        k.ones = ctx.enter_context(nc.sbuf_tensor("ones", [S, S], F32))
        k.ahead = ctx.enter_context(nc.sbuf_tensor("ahead", [S, 8, 8], F32))
        k.one_rows = ctx.enter_context(nc.sbuf_tensor("one_rows", [128, 8], F32))
        k.quarter_rows = ctx.enter_context(nc.sbuf_tensor("quarter_rows", [128, 8], F32))
        k.half = ctx.enter_context(nc.sbuf_tensor("minus_half", [S, 2], F32))
        x_loaded, made, stored = sem("x_loaded"), sem("constants_made"), sem("stored")

        with nc.Block() as block:
            @block.sync
            def _(sp):
                sp.dma_start(k.X[:, 0:B], x.rearrange("b s d -> s b d")).then_inc(x_loaded, 16)
                sp.wait_ge(x_loaded, 16)

            @block.gpsimd
            def _(pool):
                for moved in k.moved:
                    pool.sem_inc(moved, 1)
                pool.memset(k.X[:, B:B + 2], 0.0).then_inc(made, 1)
                pool.memset(k.half[:], -0.5).then_inc(made, 1)
                pool.memset(k.ident[:], 0.0).then_inc(made, 1)
                pool.memset(k.causal[:], 3.0e38).then_inc(made, 1)
                for t in (k.keep, k.earlier, k.ones, k.ahead):
                    pool.memset(t[:], 1.0).then_inc(made, 1)
                pool.wait_ge(made, 8)
                pool.memset(k.one_rows[:], 1.0).then_inc(made, 1)
                pool.memset(k.quarter_rows[:], 16 ** -0.5).then_inc(made, 1)
                pool.wait_ge(made, 10)
                for n, t in enumerate((k.one_rows, k.quarter_rows)):
                    pool.affine_select(out=t[:], in_=t[:], compare_op=ALU.is_ge, fill=0.0,
                                       base=0, pattern=[[-16, 8]], channel_multiplier=1).then_inc(made, 1)
                    pool.wait_ge(made, 11 + 2 * n)
                    pool.affine_select(out=t[:], in_=t[:], compare_op=ALU.is_ge, fill=0.0,
                                       base=15, pattern=[[16, 8]], channel_multiplier=-1).then_inc(made, 1)
                pool.affine_select(out=k.keep[:], in_=k.keep[:], compare_op=ALU.is_ge, fill=0.0,
                                   base=0, pattern=[[1, S]], channel_multiplier=-1).then_inc(made, 1)
                pool.affine_select(out=k.earlier[:], in_=k.earlier[:], compare_op=ALU.is_gt, fill=0.0,
                                   base=0, pattern=[[1, S]], channel_multiplier=-1).then_inc(made, 1)
                pool.affine_select(out=k.ahead[:], in_=k.ahead[:], compare_op=ALU.is_gt, fill=0.0,
                                   base=0, pattern=[[1, 8], [-1, 8]], channel_multiplier=0).then_inc(made, 1)
                pool.affine_select(out=k.ident[:], in_=k.ident[:], compare_op=ALU.not_equal, fill=1.0,
                                   base=0, pattern=[[-1, 128]], channel_multiplier=1).then_inc(made, 1)
                pool.affine_select(out=k.causal[:], in_=k.causal[:], compare_op=ALU.is_ge, fill=MASKED,
                                   base=0, pattern=[[-1, S]], channel_multiplier=1).then_inc(made, 1)
                pool.wait_ge(made, 19)

        k.ctx_T = ctx_T
        self_attention(k, w["L0_attn"])
        if LAST_STAGE >= 2:
            cross_attention(k, w["L0_xattn"], "b", 16, 16 ** -0.5)
        if LAST_STAGE >= 3:
            layer0_mixture(k, w["L0_gate"], w["L0_shared"], w["L0_experts"])
        if LAST_STAGE >= 4:
            linear_attention(k, w["L1_attn"])
        if LAST_STAGE >= 5:
            cross_attention(k, w["L1_xattn"], "e", 64, 64 ** -0.5)

        if LAST_STAGE >= 6:
            layer1_mixture(k, w["L1_gate"], w["L1_shared"], w["L1_experts"])

        with nc.Block() as block:
            @block.sync
            def _(sp):
                sp.dma_start(out.rearrange("b s d -> s b d"), k.X[:, 0:B]).then_inc(stored, 16)
                sp.wait_ge(stored, 16)


def kernel(**inputs):
    import numpy as np
    import concourse.bacc as bacc
    from concourse.bass_utils import run_bass_kernel_spmd

    nc = bacc.Bacc("TRN2", target_bir_lowering=False, num_devices=1)
    arrays, w = {}, {}

    def give(name, a):
        a = np.ascontiguousarray(a)
        arrays["in_" + name] = a
        return nc.dram_tensor("in_" + name, a.shape, mybir.dt.from_np(a.dtype), kind="ExternalInput").ap()

    def heads_last(a):
        return np.transpose(a, (1, 0, 2)).reshape(a.shape[1], -1)

    def rows(a):
        return a.reshape(-1, 128).T

    I = {n: np.asarray(a) for n, a in inputs.items()}
    x = give("x", I["x"])
    ctx_T = give("ctx_T", np.pad(np.transpose(I["ctx_512"], (0, 2, 1)), ((0, 0), (0, 0), (0, 2))))
    w["L0_attn"] = dict(
        Wq=give("a_Wq", heads_last(I["L0_attn_Wq"])), Wk=give("a_Wk", heads_last(I["L0_attn_Wk"])),
        Wv=give("a_Wv", heads_last(I["L0_attn_Wv"])), Wo=give("a_Wo", I["L0_attn_Wo"].reshape(H * 64, D)),
        bq=give("a_bq", rows(I["L0_attn_bq"])), bk=give("a_bk", rows(I["L0_attn_bk"])),
        bv=give("a_bv", I["L0_attn_bv"].reshape(-1)), bo=give("a_bo", I["L0_attn_bo"]))
    w["L0_xattn"] = dict(
        Wq=give("b_Wq", I["L0_xattn_Wq"].T), Wk=give("b_Wk", I["L0_xattn_Wkv"][0:D].T),
        Wv=give("b_Wv", I["L0_xattn_Wkv"][D:2 * D].T), Wo=give("b_Wo", I["L0_xattn_Wo"].T), bo=None)
    w["L1_xattn"] = dict(
        bo=give("e_bo", I["L1_xattn_bo"]),
        **{n: give("e_" + n, I["L1_xattn_" + n]) for n in ("Wq", "Wk", "Wv", "Wo")})
    def columns(a, n):
        return np.pad(a, [(0, 0)] * (a.ndim - 1) + [(0, n - a.shape[-1])])

    def turned(a):
        return np.swapaxes(a, -1, -2)

    W1, b1 = I["L1_attn_W1"], I["L1_attn_b1"]
    w["L1_attn"] = dict(
        Wk=give("d_Wk", W1[:, 0:D]), Wq=give("d_Wq", W1[:, D:2 * D]),
        Wv=give("d_Wv", W1[:, 2 * D:]), Wo=give("d_Wo", I["L1_attn_W2"]),
        bk=give("d_bk", rows(b1[0:D])), bq=give("d_bq", rows(b1[D:2 * D])),
        bv=give("d_bv", b1[2 * D:]), bo=give("d_bo", I["L1_attn_b2"]))
    w["L0_gate"] = dict(gate=give("c_gate", I["L0_ffn_gate_w"]))
    w["L0_experts"] = dict(
        G=give("c_G", I["L0_ffn_Wg"]), U=give("c_U", I["L0_ffn_Wu"]),
        D=give("c_D", turned(columns(turned(I["L0_ffn_Wd"]), 768))))
    w["L0_shared"] = dict(
        G=give("c_SG", columns(I["L0_ffn_Sg"], 384)), U=give("c_SU", columns(I["L0_ffn_Su"], 384)),
        D=give("c_SD", turned(columns(turned(I["L0_ffn_Sd"]), 384))))
    w["L1_gate"] = dict(gate=give("f_gate", I["L1_ffn_gate_weight"].T), ebias=give("f_ebias", I["L1_ffn_e_bias"]))
    def in_rows(a):
        return np.swapaxes(a.reshape(a.shape[0], -1, 128, a.shape[-1]), 1, 2).reshape(a.shape[0], 128, -1)

    w["L1_experts"] = dict(all=give("f_W", np.concatenate(
        [in_rows(turned(I["L1_ffn_w1"])), in_rows(turned(I["L1_ffn_w3"])), in_rows(turned(I["L1_ffn_w2"]))], axis=-1)))
    w["L1_shared"] = dict(
        G=give("f_SG", I["L1_ffn_shared_gate"].T), U=give("f_SU", I["L1_ffn_shared_up"].T),
        D=give("f_SD", I["L1_ffn_shared_down"].T))
    out = nc.dram_tensor("out", (B, S, D), F32, kind="ExternalOutput").ap()
    decoder(nc, w, x, ctx_T, out)
    r = run_bass_kernel_spmd(nc, [arrays], core_ids=[0])
    return r.results[0]["out"]
```

```python
from contextlib import ExitStack

import concourse.bass as bass
from concourse import mybir

F32 = mybir.dt.float32
I32 = mybir.dt.int32
U32 = mybir.dt.uint32
ALU = mybir.AluOpType
ACT = mybir.ActivationFunctionType
AX = mybir.AxisListType

B, S, D = 32, 100, 256
KC = D // 128
H = 16
CTX, CTXD = 361, 128
EPS = 1e-5
MASKED = -100000.0


class Shared:

    def __init__(self, nc, sem):
        self.nc, self.sem = nc, sem


class Banks:

    def __init__(self, k, first, n):
        self.PS, self.first, self.n, self.uses = k.PS, first, n, k.uses
        self.filled, self.moved = k.filled[first:first + n], k.moved[first:first + n]

    def plan(self, names):
        self.bank = {name: n % self.n for n, name in enumerate(names)}
        self.order = {name: n // self.n for n, name in enumerate(names)}
        self.per = [len(range(b, len(names), self.n)) for b in range(self.n)]
        assert len(self.bank) == len(names)
        self.base = self.uses[self.first:self.first + self.n]
        return self

    def done(self, turns):
        for b in range(self.n):
            self.uses[self.first + b] += turns * self.per[b]

    def at(self, name, p, *shape):
        n = 1
        for q in shape:
            n *= q
        flat = self.PS[0:p, self.first + self.bank[name], 0:n]
        if len(shape) == 2:
            return flat.rearrange("p (a b) -> p a b", a=shape[0])
        if len(shape) == 3:
            return flat.rearrange("p (a b c) -> p a b c", a=shape[0], b=shape[1])
        return flat

    def before(self, name, i):
        b = self.bank[name]
        return i * self.per[b] + (self.base[b] + self.order[name])

    def wait_free(self, pe, name, i, *moved):
        last = {self.bank[name]: self.order[name]}
        for m in moved:
            b = self.bank[m]
            last[b] = max(last.get(b, 0), self.order[m] + 1)
        for b, n in last.items():
            pe.wait_ge(self.moved[b], i * self.per[b] + (self.base[b] + n + 1))

    def fill_done(self, ins, name):
        ins.then_inc(self.filled[self.bank[name]], 1)

    def wait_full(self, eng, name, i):
        eng.wait_ge(self.filled[self.bank[name]], self.before(name, i) + 1)

    def move_done(self, ins, name):
        ins.then_inc(self.moved[self.bank[name]], 1)

    def wait_moved(self, eng, i, *names):
        last = {}
        for m in names:
            last[self.bank[m]] = max(last.get(self.bank[m], 0), self.order[m])
        for b, n in last.items():
            eng.wait_ge(self.moved[b], i * self.per[b] + (self.base[b] + n + 2))


def layer_norm(dve, ln, step, t, i, xs, stored=None):
    for u, x in enumerate(xs):
        step.done(dve.bn_stats(ln.stats[:, u, :], x))
    step.wait(dve, i)
    dve.sem_inc(ln.passed, 1)
    for u in range(len(xs)):
        step.done(dve.bn_aggr(ln.mv[:, u, :], ln.stats[:, u, :]))
    step.wait(dve, i)
    dve.tensor_scalar(ln.var[:], ln.mv[:, :, 1], EPS, None, ALU.add).then_inc(ln.var_ready, 1)
    dve.wait_ge(ln.rstd_ready, t + 1)
    if stored is not None:
        dve.wait_ge(stored, t * 16)
    for u, x in enumerate(xs):
        dve.tensor_scalar(ln.xn[:, u, :], x, ln.mv[:, u, 0:1], ln.rstd[:, u:u + 1],
                          ALU.subtract, ALU.mult).then_inc(ln.xn_ready, 1)


LN_STEPS = 4


def layer_norm_rstd(pool, ln, t):
    pool.wait_ge(ln.var_ready, t + 1)
    pool.tensor_tensor(ln.rstd[:], ln.var[:], ln.half[:], ALU.pow).then_inc(ln.rstd_ready, 1)


class NormOfAll:

    GROUP = 17

    def __init__(self, k, sb, name):
        self.k, self.turns = k, (B + 2) // self.GROUP
        self.stats, self.mv = sb(name + "_stats", [S, self.GROUP, 6]), sb(name + "_mv", [S, self.GROUP, 2])
        self.mean, self.var = sb(name + "_mean", [S, B + 2]), sb(name + "_var", [S, B + 2])
        self.rstd, self.half = sb(name + "_rstd", [S, B + 2]), sb(name + "_half", [S, B + 2])
        self.xn = sb(name + "_xn", [S, 2, D])
        self.var_ready, self.rstd_ready = k.sem(name + "_var_ready"), k.sem(name + "_rstd_ready")
        self.xn_ready, self.passed = k.sem(name + "_xn_ready"), k.sem(name + "_wait_passed")
        self.step = Chain(k.sem(name + "_step"), 2 * self.GROUP + 2)

    def find(self, dve):
        X, step = self.k.X, self.step
        assert self.turns * self.GROUP == B + 2
        with dve.Fori(0, self.turns) as t:
            for n in range(self.GROUP):
                step.done(dve.bn_stats(self.stats[:, n, :], X[:, self.GROUP * t + n, :]))
            step.wait(dve, t)
            dve.sem_inc(self.passed, 1)
            for n in range(self.GROUP):
                step.done(dve.bn_aggr(self.mv[:, n, :], self.stats[:, n, :]))
            step.wait(dve, t)
            dve.sem_inc(self.passed, 1)
            group = bass.ds(self.GROUP * t, self.GROUP)
            step.done(dve.tensor_copy(self.mean[:, group], self.mv[:, :, 0]))
            step.done(dve.tensor_scalar(self.var[:, group], self.mv[:, :, 1], EPS, None, ALU.add))
            step.wait(dve, t)
        dve.sem_inc(self.var_ready, 1)
        dve.wait_ge(self.rstd_ready, 2)

    def root(self, pool):
        pool.memset(self.half[:], -0.5).then_inc(self.rstd_ready, 1)
        pool.wait_ge(self.rstd_ready, 1)
        pool.wait_ge(self.var_ready, 1)
        pool.tensor_tensor(self.rstd[:], self.var[:], self.half[:], ALU.pow).then_inc(self.rstd_ready, 1)

    def apply(self, dve, t, stored=None):
        if stored is not None:
            dve.wait_ge(stored, t * 16)
            dve.sem_inc(self.passed, 1)
        for u in range(2):
            at = 2 * t + u
            dve.tensor_scalar(self.xn[:, u, :], self.k.X[:, at, :], self.mean[:, bass.ds(at, 1)],
                              self.rstd[:, bass.ds(at, 1)], ALU.subtract, ALU.mult).then_inc(self.xn_ready, 1)


class Chain:

    def __init__(self, sem, per):
        self.sem, self.per, self.n = sem, per, 0

    def done(self, ins):
        self.n += 1
        ins.then_inc(self.sem, 1)

    def wait(self, eng, i):
        eng.wait_ge(self.sem, i * self.per + self.n)

    def link(self, eng, i, ins):
        self.done(ins)
        self.wait(eng, i)

    def end(self):
        assert self.n == self.per, (self.n, self.per)


class Norm:

    def __init__(self, sb, sem, name, half):
        self.half = half
        self.stats, self.mv = sb(name + "_stats", [S, 2, 6]), sb(name + "_mv", [S, 2, 2])
        self.var, self.rstd = sb(name + "_var", [S, 2]), sb(name + "_rstd", [S, 2])
        self.xn = sb(name + "_xn", [S, 2, D])
        self.var_ready, self.rstd_ready = sem(name + "_var_ready"), sem(name + "_rstd_ready")
        self.xn_ready, self.passed = sem(name + "_xn_ready"), sem(name + "_wait_passed")


def turn_norm(pe, k, ln, xb, t):
    xb.wait_free(pe, "xT", t)
    pe.wait_ge(ln.xn_ready, t * 2 + 2)
    for c in range(KC):
        for u in range(2):
            last = pe.transpose(xb.at("xT", 128, KC, 2, S)[:, c, u, :],
                                ln.xn[:, u, c * 128:(c + 1) * 128], k.ident[0:S, 0:S])
    xb.fill_done(last, "xT")


def self_attention(k, w):
    nc, X = k.nc, k.X
    A = 64
    T = H * A // 128
    TURNS = B // 2
    GH = 4
    G = H // GH
    with ExitStack() as ctx:
        def sb(name, shape):
            return ctx.enter_context(nc.sbuf_tensor(name, shape, F32))

        sem = k.sem
        wq, wk, wv = (sb(n, [128, KC, H * A]) for n in ("a_wq", "a_wk", "a_wv"))
        wo = sb("a_wo", [128, T, D])
        bq, bk = sb("a_bq", [128, T]), sb("a_bk", [128, T])
        bv, bo = sb("a_bv", [S, H, A]), sb("a_bo", [S, D])
        ln = Norm(sb, sem, "a", k.half)
        xT = sb("a_xT", [128, KC, 2, S])
        qT = sb("a_qT", [128, T, 2 * S])
        kT = sb("a_kT", [128, T, 2, 2 * S])
        v = sb("a_v", [S, 2, H, A + 1])
        sm = sb("a_sm", [S, 2, G, GH, S])
        mx = sb("a_mx", [S, 2, G, GH])
        pT = sb("a_pT", [S, 2, G, GH, S])
        den = sb("a_den", [S, 2, G, GH])
        o = sb("a_o", [S, 2, H * A])
        oT = sb("a_oT", [128, 2, T, S])
        loaded, prepared = sem("a_loaded"), sem("a_prepared")
        shifted, exped, bq_scaled = sem("a_shifted"), sem("a_exped"), sem("a_bq_scaled")
        chain = Chain(sem("a_dve_step"), LN_STEPS + 2 + 4 * G)
        banks, xb = Banks(k, 0, 7), Banks(k, 7, 1).plan(["xT"])
        names = ([f"q{j}" for j in range(T // 2)] + [f"k{j}" for j in range(T // 2)]
                 + [f"v{u}{c}" for u in range(2) for c in range(2)]
                 + [f"s{u}{g}" for u in range(2) for g in range(G)])
        for u in range(2):
            for g in range(G):
                names.append(f"p{u}{g}")
                if g:
                    names.append(f"o{u}{g - 1}")
            names.append(f"o{u}{G - 1}")
        names += [f"t{u}{c}" for u in range(2) for c in range(2)] + ["y0", "y1"]
        banks.plan(names)
        bank = banks.at

        with nc.Block() as block:
            @block.sync
            def _(sp):
                for t, src in ((wq, w["Wq"]), (wk, w["Wk"]), (wv, w["Wv"])):
                    sp.dma_start(t[:], src.rearrange("(c p) n -> p c n", p=128)).then_inc(loaded, 16)
                sp.dma_start(wo[:], w["Wo"].rearrange("(t p) n -> p t n", p=128)).then_inc(loaded, 16)
                for t, src in ((bq, w["bq"]), (bk, w["bk"])):
                    sp.dma_start(t[:], src).then_inc(loaded, 16)
                sp.dma_start(bv[:].rearrange("p h a -> p (h a)"), w["bv"].partition_broadcast(S)).then_inc(loaded, 16)
                sp.dma_start(bo[:], w["bo"].partition_broadcast(S)).then_inc(loaded, 16)
                sp.dma_start(X[:, 2:B], k.x[2:B].rearrange("b s d -> s b d")).then_inc(k.x_rest_loaded, 16)
                sp.wait_ge(k.x_rest_loaded, 16)

            LOADED = 8 * 16

            @block.gpsimd
            def _(pool):
                pool.memset(v[:, :, :, A:A + 1], 1.0).then_inc(prepared, 1)
                pool.wait_ge(prepared, 1)
                pool.memset(kT[:], 0.0).then_inc(prepared, 1)
                layer_norm_rstd(pool, ln, 0)
                with pool.Fori(0, TURNS) as i:
                    layer_norm_rstd(pool, ln, i + 1)

            @block.tensor
            def _(pe):
                pe.wait_ge(loaded, LOADED)
                pe.wait_ge(prepared, 2)
                turn_norm(pe, k, ln, xb, 0)
                with pe.Fori(0, TURNS) as i:
                    xb.wait_moved(pe, i, "xT")
                    for nm, wt in (("q", wq), ("k", wk)):
                        for j in range(T // 2):
                            name = f"{nm}{j}"
                            banks.wait_free(pe, name, i)
                            for t in range(2):
                                for c in range(KC):
                                    m = (2 * j + t) * 128
                                    last = pe.matmul(bank(name, 128, 2, 2 * S)[:, t, :], wt[:, c, m:m + 128],
                                                     xT[:, c].rearrange("p u s -> p (u s)"),
                                                     start=(c == 0), stop=(c == KC - 1))
                            banks.fill_done(last, name)
                    for u in range(2):
                        for half in range(2):
                            name = f"v{u}{half}"
                            banks.wait_free(pe, name, i)
                            for c in range(KC):
                                last = pe.matmul(bank(name, S, 512), xT[:, c, u, :],
                                                 wv[:, c, half * 512:(half + 1) * 512],
                                                 start=(c == 0), stop=(c == KC - 1))
                            banks.fill_done(last, name)
                    for u in range(2):
                        for g in range(G):
                            banks.wait_free(pe, f"s{u}{g}", i, f"q{g}", f"k{g}")
                            for t in range(GH // 2):
                                cols = slice(u * S, (u + 1) * S)
                                last = pe.matmul(bank(f"s{u}{g}", S, GH, S)[:, 2 * t:2 * t + 2, :],
                                                 qT[:, 2 * g + t, cols], kT[:, 2 * g + t, :, cols],
                                                 start=True, stop=True)
                            banks.fill_done(last, f"s{u}{g}")

                    def turn_probs(u, g):
                        name = f"p{u}{g}"
                        banks.wait_free(pe, name, i)
                        pe.wait_ge(exped, i * (2 * G) + (u * G + g + 1))
                        for n in range(GH):
                            last = pe.transpose(bank(name, S, GH, S)[:, n, :], sm[:, u, g, n, :],
                                                k.ident[0:S, 0:S])
                        banks.fill_done(last, name)

                    def weigh(u, g):
                        name = f"o{u}{g}"
                        banks.wait_free(pe, name, i, f"v{u}{g // 2}", f"p{u}{g}")
                        for n in range(GH):
                            last = pe.matmul(bank(name, S, GH, A + 1)[:, n, :], pT[:, u, g, n, :],
                                             v[:, u, g * GH + n, :], start=True, stop=True)
                        banks.fill_done(last, name)

                    for u in range(2):
                        for g in range(G):
                            turn_probs(u, g)
                            if g:
                                weigh(u, g - 1)
                        weigh(u, G - 1)
                    for u in range(2):
                        for half in range(2):
                            name = f"t{u}{half}"
                            banks.wait_free(pe, name, i, f"o{u}{2 * half}", f"o{u}{2 * half + 1}")
                            for t in range(4):
                                m = (half * 4 + t) * 128
                                last = pe.transpose(bank(name, 128, 4, S)[:, t, :], o[:, u, m:m + 128],
                                                    k.ident[0:S, 0:S])
                            banks.fill_done(last, name)
                    turn_norm(pe, k, ln, xb, i + 1)
                    for u in range(2):
                        name = f"y{u}"
                        banks.wait_free(pe, name, i, f"t{u}0", f"t{u}1")
                        for t in range(T):
                            last = pe.matmul(bank(name, S, D), oT[:, u, t, :], wo[:, t, :],
                                             start=(t == 0), stop=(t == T - 1))
                        banks.fill_done(last, name)

            @block.scalar
            def _(act):
                act.wait_ge(loaded, LOADED)
                act.wait_ge(prepared, 2)

                def move_norm(t):
                    xb.wait_full(act, "xT", t)
                    xb.move_done(act.activation(xT[:], xb.at("xT", 128, KC, 2, S), ACT.Copy), "xT")

                move_norm(0)
                with act.Fori(0, TURNS) as i:
                    for j in range(T // 2):
                        name = f"k{j}"
                        banks.wait_full(act, name, i)
                        for t in range(2):
                            for r in range(2):
                                rows = slice(r * A, (r + 1) * A)
                                last = act.activation(kT[rows, 2 * j + t, r, :], bank(name, 128, 2, 2 * S)[rows, t, :],
                                                      ACT.Identity, bias=bk[rows, 2 * j + t:2 * j + t + 1])
                        banks.move_done(last, name)
                    for u in range(2):
                        for g in range(G):
                            act.wait_ge(shifted, i * (2 * G) + (u * G + g + 1))
                            act.activation(sm[:, u, g], sm[:, u, g], ACT.Exp).then_inc(exped, 1)
                            banks.wait_full(act, f"p{u}{g}", i)
                            banks.move_done(act.activation(pT[:, u, g], bank(f"p{u}{g}", S, GH, S), ACT.Copy),
                                            f"p{u}{g}")
                    for u in range(2):
                        for half in range(2):
                            name = f"t{u}{half}"
                            banks.wait_full(act, name, i)
                            banks.move_done(act.activation(oT[:, u, half * 4:half * 4 + 4, :],
                                                           bank(name, 128, 4, S), ACT.Copy), name)
                    move_norm(i + 1)

            @block.vector
            def _(dve):
                dve.wait_ge(loaded, LOADED)
                dve.tensor_scalar(bq[:], bq[:], 0.125, None, ALU.mult).then_inc(bq_scaled, 1)
                dve.wait_ge(bq_scaled, 1)
                first = Chain(sem("a_dve_first"), LN_STEPS)
                layer_norm(dve, ln, first, 0, 0, [X[:, u, :] for u in range(2)])
                with dve.Fori(0, TURNS) as i:
                    for u in range(2):
                        chain.done(dve.tensor_tensor(X[:, 2 * i + u, :], X[:, 2 * i + u, :], bo[:], ALU.add))
                    for j in range(T // 2):
                        name = f"q{j}"
                        banks.wait_full(dve, name, i)
                        last = dve.scalar_tensor_tensor(
                            qT[:, 2 * j:2 * j + 2, :], bank(name, 128, 2, 2 * S), 0.125,
                            bq[:, 2 * j:2 * j + 2].unsqueeze(2).broadcast_to([128, 2, 2 * S]), ALU.mult, ALU.add)
                        banks.move_done(last, name)
                    for u in range(2):
                        for half in range(2):
                            name = f"v{u}{half}"
                            banks.wait_full(dve, name, i)
                            h = slice(half * 8, half * 8 + 8)
                            banks.move_done(dve.tensor_tensor(v[:, u, h, 0:A], bank(name, S, 8, A), bv[:, h, :],
                                                              ALU.add), name)
                    for u in range(2):
                        for g in range(G):
                            name = f"s{u}{g}"
                            banks.wait_full(dve, name, i)
                            banks.move_done(dve.tensor_tensor(
                                sm[:, u, g], bank(name, S, GH, S),
                                k.causal[:].unsqueeze(1).broadcast_to([S, GH, S]), ALU.min), name)
                            banks.wait_moved(dve, i, name)
                            chain.link(dve, i, dve.tensor_reduce(mx[:, u, g], sm[:, u, g], AX.X, ALU.max))
                            dve.tensor_tensor(sm[:, u, g], sm[:, u, g],
                                              mx[:, u, g].unsqueeze(2).broadcast_to([S, GH, S]),
                                              ALU.subtract).then_inc(shifted, 1)
                    dve.wait_ge(k.x_rest_loaded, 16)
                    layer_norm(dve, ln, chain, i + 1, i, [X[:, 2 * i + 2 + u, :] for u in range(2)])
                    for u in range(2):
                        for g in range(G):
                            name = f"o{u}{g}"
                            banks.wait_full(dve, name, i)
                            ps = bank(name, S, GH, A + 1)
                            chain.link(dve, i, dve.reciprocal(den[:, u, g], ps[:, :, A]))
                            banks.move_done(dve.tensor_tensor(
                                o[:, u, g * GH * A:(g + 1) * GH * A].rearrange("p (n a) -> p n a", a=A),
                                ps[:, :, 0:A], den[:, u, g].unsqueeze(2).broadcast_to([S, GH, A]), ALU.mult), name)
                    for u in range(2):
                        name = f"y{u}"
                        banks.wait_full(dve, name, i)
                        banks.move_done(dve.tensor_tensor(X[:, 2 * i + u, :], X[:, 2 * i + u, :],
                                                          bank(name, S, D), ALU.add), name)
                    chain.end()
        banks.done(TURNS)
        xb.done(TURNS + 1)


def cross_attention(k, w, name, A, scale):
    nc, X = k.nc, k.X
    HT = 128 // A
    T = H // HT
    TURNS = B // 2
    KEYS, CH = 121, 3
    HG = 4 if A == 64 else H
    VB = min(H * A, 512)
    NP, NT = 6, 4
    with ExitStack() as ctx:
        def sb(n, shape):
            return ctx.enter_context(nc.sbuf_tensor(f"{name}_{n}", shape, F32))

        def sem(n):
            return k.sem(f"{name}_{n}")

        FOLD = A == 64
        if FOLD:
            wqT, wkT = sb("wqT", [128, T, D]), sb("wkT", [128, T, 128])
            wqk = sb("wqk", [128, KC, H, 128])
        else:
            wq, wk = sb("wq", [128, KC, T * 128]), sb("wk", [128, T * 128])
        wv, wo = sb("wv", [128, H * A]), sb("wo", [128, T, D])
        bo = sb("bo", [S, D])
        ln = Norm(lambda n, shape: ctx.enter_context(nc.sbuf_tensor(n, shape, F32)), k.sem, name, k.half)
        xT = sb("xT", [128, KC, 2, S])
        cT = sb("cT", [128, 2, KEYS * CH])
        qT = sb("qT", [128, T, HT, 2 * S])
        if not FOLD:
            kT = sb("kT", [128, 2, T, CTX])
        v = sb("v", [KEYS, 2, CH, H, A + 1])
        nmx = sb("nmx", [S, 2, H])
        p = sb("p", [S, NP, KEYS * CH])
        pT = sb("pT", [KEYS, NT, CH, S])
        den = sb("den", [S, 2, H])
        o = sb("o", [S, 2, H, A])
        oT = sb("oT", [128, 2, T, S])
        loaded, prepared, ctx_loaded = sem("loaded"), sem("prepared"), sem("ctx_loaded")
        max_ready = sem("max_ready")

        heads = [(u, h) for u in range(2) for h in range(H)]
        steps = []
        for m in range(0, 2 * H + 6, 2):
            steps += [("s", *heads[n]) for n in (m, m + 1) if n < 2 * H]
            steps += [("p", *heads[n]) for n in (m - 4, m - 3) if 0 <= n < 2 * H]
            for n in (m - 6, m - 5):
                if 0 <= n:
                    steps.append(("o", *heads[n]))
            if m - 6 == H + 4:
                steps += [("t", 0, c) for c in range(0, T, 4)]
            if m - 6 == H + 8:
                steps.append(("y", 0, 0))
        steps += [("x", 0, 0)] + [("t", 1, c) for c in range(0, T, 4)] + [("y", 1, 0)]

        QS = H // 2 if FOLD else T // 2
        folds = [(c, g) for c in range(KC) for g in range(H // 4)] if FOLD else []
        folding = Banks(k, 0, 5).plan([f"w{c}{g}" for c, g in folds])
        folding.done(1)
        banks = Banks(k, 0, 5)
        banks.plan([f"q{j}" for j in range(QS)]
                   + ([] if FOLD else [f"k{u}{t}" for u in range(2) for t in range(T)])
                   + [f"v{u}{c}{n}" for u in range(2) for c in range(CH) for n in range(H * A // VB)]
                   + [f"{a}{u}.{h}" for a, u, h in steps if a in "spty"])
        ob = Banks(k, 5, 2).plan([f"o{u}.{g}" for u in range(2) for g in range(H // HG)])
        xb = Banks(k, 7, 1).plan(["xT"])
        bank = banks.at
        on_act = [n for n in range(2 * H) if n % 2]
        chain = Chain(sem("dve_step"), LN_STEPS + 2 * H // HG + (2 if w["bo"] is not None else 0))

        with nc.Block() as block:
            @block.sync
            def _(sp):
                if FOLD:
                    sp.dma_start(wqT[:], w["WqT"].rearrange("(t p) n -> p t n", p=128)).then_inc(loaded, 16)
                    sp.dma_start(wkT[:], w["WkT"].rearrange("(t p) n -> p t n", p=128)).then_inc(loaded, 16)
                else:
                    sp.dma_start(wq[:], w["Wq"].rearrange("(c p) n -> p c n", p=128)).then_inc(loaded, 16)
                    sp.dma_start(wk[:], w["Wk"]).then_inc(loaded, 16)
                sp.dma_start(wv[:], w["Wv"]).then_inc(loaded, 16)
                sp.dma_start(wo[:], w["Wo"].rearrange("(t p) n -> p t n", p=128)).then_inc(loaded, 16)
                if w["bo"] is not None:
                    sp.dma_start(bo[:], w["bo"].partition_broadcast(S)).then_inc(loaded, 16)
                sp.dma_start(cT[:], k.ctx_T[0:2].rearrange("b p n -> p b n")).then_inc(ctx_loaded, 16)
                with sp.Fori(0, TURNS - 1) as i:
                    banks.wait_full(sp, f"s1.{H - 1}" if FOLD else f"v1{CH - 1}{H * A // VB - 1}", i)
                    sp.dma_start(cT[:], k.ctx_T[bass.ds(2 * i + 2, 2)].rearrange("b p n -> p b n"))\
                      .then_inc(ctx_loaded, 16)

            LOADED = 64 if w["bo"] is None else 80

            PREPARED = 2 if FOLD else 3

            @block.gpsimd
            def _(pool):
                pool.memset(v[:, :, :, :, A:A + 1], 1.0).then_inc(prepared, 1)
                pool.wait_ge(prepared, 1)
                pool.memset(p[:, :, CTX:KEYS * CH], 0.0).then_inc(prepared, 1)
                pool.wait_ge(prepared, 2)
                if not FOLD:
                    pool.memset(qT[:], 0.0).then_inc(prepared, 1)
                layer_norm_rstd(pool, ln, 0)
                with pool.Fori(0, TURNS) as i:
                    layer_norm_rstd(pool, ln, i + 1)

            @block.tensor
            def _(pe):
                pe.wait_ge(loaded, LOADED)
                pe.wait_ge(prepared, PREPARED)
                for c, g in folds:
                    folding.wait_free(pe, f"w{c}{g}", 0)
                    for n in range(4):
                        t, row = g // HT * 4 + n, g % HT * A
                        last = pe.matmul(folding.at(f"w{c}{g}", 128, 4, 128)[:, n, :],
                                         wqT[row:row + A, t, c * 128:(c + 1) * 128], wkT[row:row + A, t, :],
                                         start=True, stop=True)
                    folding.fill_done(last, f"w{c}{g}")
                turn_norm(pe, k, ln, xb, 0)
                if FOLD:
                    folding.wait_moved(pe, 0, *[f"w{c}{g}" for c, g in folds])
                with pe.Fori(0, TURNS) as i:
                    xb.wait_moved(pe, i, "xT")
                    for j in range(QS):
                        banks.wait_free(pe, f"q{j}", i)
                        for t in range(2):
                            for c in range(KC):
                                m = (2 * j + t) * 128
                                weights = wqk[:, c, 2 * j + t, :] if FOLD else wq[:, c, m:m + 128]
                                last = pe.matmul(bank(f"q{j}", 128, 2, 2 * S)[:, t, :], weights,
                                                 xT[:, c].rearrange("p u s -> p (u s)"),
                                                 start=(c == 0), stop=(c == KC - 1))
                        banks.fill_done(last, f"q{j}")
                    pe.wait_ge(ctx_loaded, i * 16 + 16)
                    for u in range(2):
                        for t in range(0 if FOLD else T):
                            banks.wait_free(pe, f"k{u}{t}", i)
                            last = pe.matmul(bank(f"k{u}{t}", 128, CTX), wk[:, t * 128:(t + 1) * 128],
                                             cT[:, u, 0:CTX], start=True, stop=True)
                            banks.fill_done(last, f"k{u}{t}")
                    for u in range(2):
                        for c in range(CH):
                            for n in range(H * A // VB):
                                banks.wait_free(pe, f"v{u}{c}{n}", i)
                                last = pe.matmul(bank(f"v{u}{c}{n}", KEYS, VB), cT[:, u, c * KEYS:(c + 1) * KEYS],
                                                 wv[:, n * VB:(n + 1) * VB], start=True, stop=True)
                                banks.fill_done(last, f"v{u}{c}{n}")
                    for kind, u, h in steps:
                        name, n = f"{kind}{u}.{h}", u * H + h
                        if kind == "s":
                            made = [f"q{h // 2}"] if FOLD else [f"q{h // HT // 2}", f"k{u}{h // HT}"]
                            banks.wait_free(pe, name, i, *made)
                            banks.fill_done(pe.matmul(
                                bank(name, S, CTX), qT[:, h // HT, h % HT, u * S:(u + 1) * S],
                                cT[:, u, 0:CTX] if FOLD else kT[:, u, h // HT, :], start=True, stop=True), name)
                        elif kind == "p":
                            banks.wait_free(pe, name, i, f"s{u}.{h}")
                            for c in range(CH):
                                last = pe.transpose(bank(name, KEYS, CH, S)[:, c, :],
                                                    p[:, n % NP, c * KEYS:(c + 1) * KEYS], k.ident[0:S, 0:S])
                            banks.fill_done(last, name)
                        elif kind == "o":
                            g = h // HG
                            if h % HG == 0:
                                ob.wait_free(pe, f"o{u}.{g}", i)
                            vs = [f"v{u}{c}{h * A // VB}" for c in range(CH)] if h % HG == 0 else []
                            banks.wait_moved(pe, i, f"p{u}.{h}", *vs)
                            for c in range(CH):
                                last = pe.matmul(ob.at(f"o{u}.{g}", S, HG, A + 1)[:, h % HG, :],
                                                 pT[:, n % NT, c, :], v[:, u, c, h, :],
                                                 start=(c == 0), stop=(c == CH - 1))
                            if h % HG == HG - 1:
                                ob.fill_done(last, f"o{u}.{g}")
                        elif kind == "x":
                            turn_norm(pe, k, ln, xb, i + 1)
                        elif kind == "t":
                            banks.wait_free(pe, name, i)
                            gs = sorted({(h + t) * (128 // A) // HG for t in range(min(4, T))})
                            ob.wait_moved(pe, i, *[f"o{u}.{g}" for g in gs])
                            for t in range(min(4, T)):
                                last = pe.transpose(bank(name, 128, min(4, T), S)[:, t, :],
                                                    o[:, u].rearrange("p h a -> p (h a)")[:, (h + t) * 128:(h + t + 1) * 128],
                                                    k.ident[0:S, 0:S])
                            banks.fill_done(last, name)
                        elif kind == "y":
                            banks.wait_free(pe, name, i, *[f"t{u}.{c}" for c in range(0, T, 4)])
                            for t in range(T):
                                last = pe.matmul(bank(name, S, D), oT[:, u, t, :], wo[:, t, :],
                                                 start=(t == 0), stop=(t == T - 1))
                            banks.fill_done(last, name)

            @block.scalar
            def _(act):
                def move_norm(t):
                    xb.wait_full(act, "xT", t)
                    xb.move_done(act.activation(xT[:], xb.at("xT", 128, KC, 2, S), ACT.Copy), "xT")

                def move(name, i, out, src):
                    banks.wait_full(act, name, i)
                    banks.move_done(act.activation(out, src, ACT.Copy), name)

                for c, g in folds:
                    folding.wait_full(act, f"w{c}{g}", 0)
                    to = wqk[:, c].rearrange("p (t r) n -> p t r n", r=HT)[:, g // HT * 4:g // HT * 4 + 4, g % HT, :]
                    folding.move_done(act.activation(to, folding.at(f"w{c}{g}", 128, 4, 128), ACT.Copy, scale=scale),
                                      f"w{c}{g}")
                move_norm(0)
                act.wait_ge(prepared, PREPARED)
                with act.Fori(0, TURNS) as i:
                    if FOLD:
                        for j in range(QS):
                            move(f"q{j}", i, qT[:, j], bank(f"q{j}", 128, 2, 2 * S))
                    for u in range(2):
                        for t in range(0, 0 if FOLD else T, 2):
                            move(f"k{u}{t}", i, kT[:, u, t, :], bank(f"k{u}{t}", 128, CTX))
                    for kind, u, h in steps:
                        name, n = f"{kind}{u}.{h}", u * H + h
                        if kind == "s":
                            act.wait_ge(max_ready, i * (2 * H) + (n + 1))
                            banks.move_done(act.activation(p[:, n % NP, 0:CTX], bank(name, S, CTX), ACT.Exp,
                                                           bias=nmx[:, u, h:h + 1]), name)
                        elif kind == "p" and n in on_act:
                            move(name, i, pT[:, n % NT], bank(name, KEYS, CH, S))
                        elif kind == "t":
                            move(name, i, oT[:, u, h:h + min(4, T), :], bank(name, 128, min(4, T), S))
                        elif kind == "x":
                            move_norm(i + 1)

            @block.vector
            def _(dve):
                first = Chain(sem("dve_first"), LN_STEPS)
                layer_norm(dve, ln, first, 0, 0, [X[:, u, :] for u in range(2)])
                if w["bo"] is not None:
                    dve.wait_ge(loaded, LOADED)
                dve.wait_ge(prepared, PREPARED)
                with dve.Fori(0, TURNS) as i:
                    if w["bo"] is not None:
                        for u in range(2):
                            chain.done(dve.tensor_tensor(X[:, 2 * i + u, :], X[:, 2 * i + u, :], bo[:], ALU.add))
                    if A == 16:
                        banks.wait_full(dve, "q0", i)
                        for t in range(T):
                            last = dve.tensor_tensor(
                                qT[:, t], bank("q0", 128, 2, 2 * S)[:, t, :].unsqueeze(1).broadcast_to([128, HT, 2 * S]),
                                k.quarter_rows[:].unsqueeze(2).broadcast_to([128, HT, 2 * S]), ALU.mult)
                        banks.move_done(last, "q0")
                    for u in range(2):
                        for t in range(1, 0 if FOLD else T, 2):
                            banks.wait_full(dve, f"k{u}{t}", i)
                            banks.move_done(dve.tensor_copy(kT[:, u, t, :], bank(f"k{u}{t}", 128, CTX)), f"k{u}{t}")
                    for u in range(2):
                        for c in range(CH):
                            for n in range(H * A // VB):
                                name = f"v{u}{c}{n}"
                                banks.wait_full(dve, name, i)
                                hs = slice(n * VB // A, (n + 1) * VB // A)
                                banks.move_done(dve.tensor_copy(v[:, u, c, hs, 0:A],
                                                                bank(name, KEYS, VB // A, A)), name)
                    for kind, u, h in steps:
                        name, n = f"{kind}{u}.{h}", u * H + h
                        if kind == "s":
                            banks.wait_full(dve, name, i)
                            dve.tensor_reduce(nmx[:, u, h:h + 1], bank(name, S, CTX), AX.X, ALU.max,
                                              negate=True).then_inc(max_ready, 1)
                        elif kind == "p" and n not in on_act:
                            banks.wait_full(dve, name, i)
                            banks.move_done(dve.tensor_copy(pT[:, n % NT], bank(name, KEYS, CH, S)), name)
                        elif kind == "o" and h % HG == HG - 1:
                            g = h // HG
                            ob.wait_full(dve, f"o{u}.{g}", i)
                            ps = ob.at(f"o{u}.{g}", S, HG, A + 1)
                            hs = slice(g * HG, (g + 1) * HG)
                            chain.link(dve, i, dve.reciprocal(den[:, u, hs], ps[:, :, A]))
                            ob.move_done(dve.tensor_tensor(
                                o[:, u, hs, :], ps[:, :, 0:A], den[:, u, hs].unsqueeze(2).broadcast_to([S, HG, A]),
                                ALU.mult), f"o{u}.{g}")
                        elif kind == "t" and u == 0 and h == 0:
                            layer_norm(dve, ln, chain, i + 1, i, [X[:, 2 * i + 2 + b, :] for b in range(2)])
                        elif kind == "y":
                            banks.wait_full(dve, name, i)
                            banks.move_done(dve.tensor_tensor(X[:, 2 * i + u, :], X[:, 2 * i + u, :],
                                                              bank(name, S, D), ALU.add), name)
                    chain.end()
        banks.done(TURNS)
        ob.done(TURNS)
        xb.done(TURNS + 1)


def linear_attention(k, w):
    nc, X = k.nc, k.X
    A, HT, GH = 16, 8, 4
    T = H // HT
    TURNS = B // 2
    with ExitStack() as ctx:
        def sb(n, shape):
            return ctx.enter_context(nc.sbuf_tensor(n, shape, F32))

        sem = k.sem
        wq, wk = sb("d_wq", [128, KC, T * 128]), sb("d_wk", [128, KC, T * 128])
        wv, wo = sb("d_wv", [128, KC, D]), sb("d_wo", [128, KC, D])
        bq, bk = sb("d_bq", [128, T]), sb("d_bk", [128, T])
        bv, bo = sb("d_bv", [S, D]), sb("d_bo", [S, D])
        ln = Norm(sb, sem, "d", k.half)
        xT = sb("d_xT", [128, KC, 2, S])
        qT, kT = sb("d_qT", [128, T, HT, 2 * S]), sb("d_kT", [128, T, 2 * S])
        v = sb("d_v", [S, 2, D])
        sT = sb("d_sT", [S, 2, H, S])
        o = sb("d_o", [S, 2, D])
        oT = sb("d_oT", [128, 2, KC, S])
        loaded = sem("d_loaded")
        chain = Chain(sem("d_dve_step"), LN_STEPS + 2)
        banks, xb = Banks(k, 0, 7), Banks(k, 7, 1).plan(["xT"])
        banks.plan(["q0", "k0", "v0", "v1"] + [f"s{u}{r}" for u in range(2) for r in range(H // GH)]
                   + ["o0", "o1", "t0", "t1", "y0", "y1"])
        bank = banks.at
        with nc.Block() as block:
            @block.sync
            def _(sp):
                for t, src in ((wq, w["Wq"]), (wk, w["Wk"]), (wv, w["Wv"]), (wo, w["Wo"])):
                    sp.dma_start(t[:], src.rearrange("(c p) n -> p c n", p=128)).then_inc(loaded, 16)
                for t, src in ((bq, w["bq"]), (bk, w["bk"])):
                    sp.dma_start(t[:], src).then_inc(loaded, 16)
                for t, src in ((bv, w["bv"]), (bo, w["bo"])):
                    sp.dma_start(t[:], src.partition_broadcast(S)).then_inc(loaded, 16)

            LOADED = 8 * 16

            @block.gpsimd
            def _(pool):
                layer_norm_rstd(pool, ln, 0)
                with pool.Fori(0, TURNS) as i:
                    layer_norm_rstd(pool, ln, i + 1)

            @block.tensor
            def _(pe):
                pe.wait_ge(loaded, LOADED)
                turn_norm(pe, k, ln, xb, 0)
                with pe.Fori(0, TURNS) as i:
                    xb.wait_moved(pe, i, "xT")
                    for nm, wt in (("q", wq), ("k", wk)):
                        for j in range(T // 2):
                            banks.wait_free(pe, f"{nm}{j}", i)
                            for t in range(2):
                                for c in range(KC):
                                    m = (2 * j + t) * 128
                                    last = pe.matmul(bank(f"{nm}{j}", 128, 2, 2 * S)[:, t, :], wt[:, c, m:m + 128],
                                                     xT[:, c].rearrange("p u s -> p (u s)"),
                                                     start=(c == 0), stop=(c == KC - 1))
                            banks.fill_done(last, f"{nm}{j}")
                    for u in range(2):
                        banks.wait_free(pe, f"v{u}", i)
                        for c in range(KC):
                            last = pe.matmul(bank(f"v{u}", S, D), xT[:, c, u, :], wv[:, c, :],
                                             start=(c == 0), stop=(c == KC - 1))
                        banks.fill_done(last, f"v{u}")
                    for u in range(2):
                        for r in range(H // GH):
                            banks.wait_free(pe, f"s{u}{r}", i, "q0", "k0")
                            t, h = r * GH // HT, r * GH % HT
                            cols = slice(u * S, (u + 1) * S)
                            banks.fill_done(pe.matmul(bank(f"s{u}{r}", S, GH, S), kT[:, t, cols],
                                                      qT[:, t, h:h + GH, cols], start=True, stop=True), f"s{u}{r}")
                    turn_norm(pe, k, ln, xb, i + 1)
                    for u in range(2):
                        banks.wait_free(pe, f"o{u}", i, f"v{u}", *[f"s{u}{r}" for r in range(H // GH)])
                        for h in range(H):
                            last = pe.matmul(bank(f"o{u}", S, H, A)[:, h, :], sT[:, u, h, :],
                                             v[:, u, h * A:(h + 1) * A], start=True, stop=True)
                        banks.fill_done(last, f"o{u}")
                    for u in range(2):
                        banks.wait_free(pe, f"t{u}", i, f"o{u}")
                        for t in range(KC):
                            last = pe.transpose(bank(f"t{u}", 128, KC, S)[:, t, :], o[:, u, t * 128:(t + 1) * 128],
                                                k.ident[0:S, 0:S])
                        banks.fill_done(last, f"t{u}")
                    for u in range(2):
                        banks.wait_free(pe, f"y{u}", i, f"t{u}")
                        for t in range(KC):
                            last = pe.matmul(bank(f"y{u}", S, D), oT[:, u, t, :], wo[:, t, :],
                                             start=(t == 0), stop=(t == KC - 1))
                        banks.fill_done(last, f"y{u}")

            @block.scalar
            def _(act):
                act.wait_ge(loaded, LOADED)

                def move_norm(t):
                    xb.wait_full(act, "xT", t)
                    xb.move_done(act.activation(xT[:], xb.at("xT", 128, KC, 2, S), ACT.Copy), "xT")

                move_norm(0)
                with act.Fori(0, TURNS) as i:
                    for j in range(T // 2):
                        banks.wait_full(act, f"k{j}", i)
                        for t in range(2):
                            last = act.activation(kT[:, 2 * j + t, :], bank(f"k{j}", 128, 2, 2 * S)[:, t, :],
                                                  ACT.Identity, bias=bk[:, 2 * j + t:2 * j + t + 1])
                        banks.move_done(last, f"k{j}")
                    move_norm(i + 1)
                    for u in range(2):
                        banks.wait_full(act, f"o{u}", i)
                        banks.move_done(act.activation(o[:, u, :], bank(f"o{u}", S, D), ACT.Copy), f"o{u}")
                    for u in range(2):
                        banks.wait_full(act, f"t{u}", i)
                        banks.move_done(act.activation(oT[:, u], bank(f"t{u}", 128, KC, S), ACT.Copy), f"t{u}")

            @block.vector
            def _(dve):
                dve.wait_ge(loaded, LOADED)
                first = Chain(sem("d_dve_first"), LN_STEPS)
                layer_norm(dve, ln, first, 0, 0, [X[:, u, :] for u in range(2)])
                with dve.Fori(0, TURNS) as i:
                    for u in range(2):
                        chain.done(dve.tensor_tensor(X[:, 2 * i + u, :], X[:, 2 * i + u, :], bo[:], ALU.add))
                    for j in range(T // 2):
                        banks.wait_full(dve, f"q{j}", i)
                        for t in range(2):
                            last = dve.scalar_tensor_tensor(
                                qT[:, t], bank(f"q{j}", 128, 2, 2 * S)[:, t, :].unsqueeze(1).broadcast_to([128, HT, 2 * S]),
                                bq[:, t:t + 1], k.one_rows[:].unsqueeze(2).broadcast_to([128, HT, 2 * S]),
                                ALU.add, ALU.mult)
                        banks.move_done(last, f"q{j}")
                    for u in range(2):
                        banks.wait_full(dve, f"v{u}", i)
                        banks.move_done(dve.tensor_tensor(v[:, u, :], bank(f"v{u}", S, D), bv[:], ALU.add), f"v{u}")
                    layer_norm(dve, ln, chain, i + 1, i, [X[:, 2 * i + 2 + u, :] for u in range(2)])
                    for u in range(2):
                        for r in range(H // GH):
                            banks.wait_full(dve, f"s{u}{r}", i)
                            banks.move_done(dve.tensor_tensor(
                                sT[:, u, r * GH:(r + 1) * GH], bank(f"s{u}{r}", S, GH, S),
                                k.keep[:].unsqueeze(1).broadcast_to([S, GH, S]), ALU.mult), f"s{u}{r}")
                    for u in range(2):
                        banks.wait_full(dve, f"y{u}", i)
                        banks.move_done(dve.tensor_tensor(X[:, 2 * i + u, :], X[:, 2 * i + u, :],
                                                          bank(f"y{u}", S, D), ALU.add), f"y{u}")
                    chain.end()
        banks.done(TURNS)
        xb.done(TURNS + 1)


class Ranking:

    def __init__(self, sb):
        self.above, self.equal = sb("above", [S, 2, 8, 8]), sb("equal", [S, 2, 8, 8])
        self.rank, self.sel = sb("rank", [S, 2, 8]), sb("sel", [S, 2, 8])


def chosen_by_rank(link, dve, k, r, score, count):
    wide = [S, 2, 8, 8]
    mine = score.unsqueeze(3).broadcast_to(wide)
    other = score.unsqueeze(2).broadcast_to(wide)
    link(dve.tensor_tensor(r.above[:], other, mine, ALU.is_gt))
    link(dve.tensor_tensor(r.equal[:], other, mine, ALU.is_equal))
    link(dve.tensor_tensor(r.equal[:], r.equal[:], k.ahead[:].unsqueeze(1).broadcast_to(wide), ALU.mult))
    link(dve.tensor_tensor(r.above[:], r.above[:], r.equal[:], ALU.add))
    link(dve.tensor_reduce(r.rank[:], r.above[:], AX.X, ALU.add))
    link(dve.tensor_scalar(r.sel[:], r.rank[:], float(count), None, ALU.is_lt))


RANK_STEPS = 6


class Dispatch:

    def __init__(self, k, name, places, x_rows):
        self.places, self.x_rows = places, x_rows
        self.xn = k.nc.dram_tensor(name + "_xn_rows", (B * S, D), F32).ap()
        self.table = k.nc.dram_tensor(name + "_table", (places, 2), I32).ap()


TILES = 2 * B * S // 128 + 7
SLOTS = TILES + 3
NO_TOKEN = 1 << 20
DROPPED = 32768.0


def route(k, w, name, E, xall, dispatch, shared=None):
    nc, X = k.nc, k.X
    TURNS = B // 2
    GROUPS, TOP, CAP, FACTOR = 8, 8, 256, 2.5
    with ExitStack() as ctx:
        def sb(n, shape):
            return ctx.enter_context(nc.sbuf_tensor(f"{name}_{n}", shape, F32))

        def sem(n):
            return k.sem(f"{name}_{n}")

        gate = sb("gate", [128, KC, E])
        ln = NormOfAll(k, lambda n, shape: ctx.enter_context(nc.sbuf_tensor(n, shape, F32)), name)
        xT = sb("xT", [128, KC, 2, S])
        logits = sb("logits", [S, 2, E])
        r = Ranking(sb)
        top, total = sb("top", [S, 2]), sb("total", [S, 2])
        expd = sb("expd", [S, 2, E])
        loaded, act_asked, act_done = sem("loaded"), sem("act_asked"), sem("act_done")
        before = sb("before", [S, 2, E])
        choices_ready = sem("choices_ready")
        constants, table_clear, stored = sem("constants"), sem("table_clear"), sem("xn_stored")
        table_parts = dispatch.places // 128
        no_token = ctx.enter_context(nc.sbuf_tensor(name + "_no_token", [table_parts, 128, 2], I32))
        if shared is not None:
            IT = shared["G"].shape[-1] // 128
            wg, wu, wd = sb("wg", [128, KC, IT * 128]), sb("wu", [128, KC, IT * 128]), sb("wd", [128, IT, D])
            gated, h = sb("gated", [128, IT, 2 * S]), sb("h", [128, IT, 2 * S])
        if E == 8:
            places, chosen, comb = (sb(n, [S, B, E]) for n in ("places", "chosen", "comb"))
            keys, match = sb("keys", [S, B, E]), sb("match", [S, B, E])
            FULL = B * S // 128
            starts, spans = sb("starts", [S, FULL]), sb("spans", [S, E, FULL])
            counts, tiles, first_tile = sb("counts", [S, E]), sb("tiles", [S, E]), sb("first_tile", [S, E])
            firsts, ends, offset = sb("firsts", [S, E, E]), sb("ends", [S, E]), sb("offset", [S, E])
            tile_no, passed_by = sb("tile_no", [S, TILES + 2]), sb("passed_by", [S, TILES + 2, E])
            expert_f = sb("expert_f", [S, TILES + 2])
            high, low = sb("high", [S, B]), sb("low", [S, B])
        if E == 64:
            ebias = sb("ebias", [S, E])
            biased, masked, left = sb("biased", [S, 2, E]), sb("masked", [S, 2, E]), sb("left", [S, 2, E])
            best = sb("best", [S, 2, GROUPS, 8])
            gscore = sb("gscore", [S, 2, GROUPS])
            best8 = sb("best8", [S, 2, TOP])
            taken = sb("taken", [S, 2, E])
            passed, started = sem("passed"), sem("started")
            weight = sb("choice_weight", [S, 2, E])
            row1 = sb("row1", [128, E])
            late = sb("late", [S, 2, E])
            key = sb("key", [S, 2, E])
            key8 = sb("key8", [S, 2, TOP])
            match = sb("match", [S, 2, TOP, E])
            rows_now = ctx.enter_context(nc.sbuf_tensor(name + "_rows_now", [S, 2, TOP], I32))
            entries = sb("entries", [S, 2, TOP, 2])
            token_f = sb("token_f", [S, 2])
            rows_ready, sent = sem("rows_ready"), sem("sent")
            rows_free = sem("rows_free")
        banks, xb = Banks(k, 0, 7), Banks(k, 7, 1).plan(["xT"])
        widened = [f"{a}{t}" for t in range(IT) for a in "gu"] if shared is not None else []
        banks.plan(["l", "c"] + widened + (["y"] if shared is not None else [])).done(TURNS)
        totals = Banks(k, 0, 1).plan(["n"])
        steps = {8: RANK_STEPS + 7, 64: RANK_STEPS + 29}[E]
        chain = Chain(sem("dve_step"), steps)
        with nc.Block() as block:
            @block.sync
            def _(sp):
                sp.dma_start(gate[:], w["gate"].rearrange("(c p) n -> p c n", p=128)).then_inc(loaded, 16)
                if E == 64:
                    sp.dma_start(ebias[:], w["ebias"].partition_broadcast(S)).then_inc(loaded, 16)
                if shared is not None:
                    for t, src in ((wg, shared["G"]), (wu, shared["U"]), (wd, shared["D"])):
                        sp.dma_start(t[:], src.rearrange("(c p) n -> p c n", p=128)).then_inc(loaded, 16)
                sp.wait_ge(constants, 1)
                sp.dma_start(dispatch.table.rearrange("(p n) o -> p n o", n=128), no_token[:])\
                  .then_inc(table_clear, 16)
                rows_of = dispatch.xn.rearrange("(b s) d -> s b d", s=S)
                with sp.Fori(0, TURNS) as i:
                    sp.wait_ge(ln.xn_ready, i * 2 + 2)
                    sp.dma_start(rows_of[:, bass.ds(i * 2, 2), :], ln.xn[:]).then_inc(stored, 16)
                sp.wait_ge(stored, TURNS * 16)
                sp.wait_ge(table_clear, 16)

            LOADED = 16 if E == 8 else 80

            @block.gpsimd
            def _(pool):
                pool.memset(no_token[:], NO_TOKEN).then_inc(constants, 1)
                pool.wait_ge(constants, 1)
                if E == 8:
                    pool.iota(starts[:], pattern=[[128, FULL]], base=0, channel_multiplier=0,
                              allow_small_or_imprecise_dtypes=True).then_inc(constants, 1)
                    pool.wait_ge(constants, 2)
                    pool.iota(tile_no[:], pattern=[[1, TILES + 2]], base=-1, channel_multiplier=0,
                              allow_small_or_imprecise_dtypes=True).then_inc(constants, 1)
                    pool.wait_ge(constants, 3)
                else:
                    pool.iota(row1[:], pattern=[[2, E]], base=1, channel_multiplier=0,
                              allow_small_or_imprecise_dtypes=True).then_inc(constants, 1)
                    pool.wait_ge(constants, 2)
                    pool.iota(token_f[:], pattern=[[S, 2]], base=0, channel_multiplier=1,
                              allow_small_or_imprecise_dtypes=True).then_inc(constants, 1)
                    pool.wait_ge(constants, 3)
                ln.root(pool)
                if E == 64:
                    pool.sem_inc(rows_free, 1)
                    pool.wait_ge(table_clear, 16)
                    with pool.Fori(0, TURNS) as i:
                        pool.wait_ge(rows_ready, i + 1)
                        pool.sem_inc(started, 1)
                        for u in range(2):
                            for n in range(TOP):
                                pool.indirect_dma_start(
                                    out=dispatch.table, in_=entries[:, u, n, :].bitcast(I32), in_offset=None,
                                    out_offset=bass.IndirectOffsetOnAxis(
                                        ap=rows_now[:, u, n:n + 1].bitcast(U32), axis=0),
                                    bounds_check=dispatch.places - 1, oob_is_err=False).then_inc(sent, 16)
                        pool.wait_ge(sent, i * (2 * TOP * 16) + 2 * TOP * 16)
                        pool.sem_inc(rows_free, 1)

            @block.tensor
            def _(pe):
                pe.wait_ge(loaded, LOADED)
                turn_norm(pe, k, ln, xb, 0)
                with pe.Fori(0, TURNS) as i:
                    banks.wait_free(pe, "l", i)
                    xb.wait_moved(pe, i, "xT")
                    for u in range(2):
                        for c in range(KC):
                            last = pe.matmul(banks.at("l", S, 2, E)[:, u, :], xT[:, c, u, :], gate[:, c, :],
                                             start=(c == 0), stop=(c == KC - 1))
                    banks.fill_done(last, "l")
                    for n, nm in enumerate(widened):
                        banks.wait_free(pe, nm, i)
                        for c in range(KC):
                            last = pe.matmul(banks.at(nm, 128, 2 * S),
                                             (wg, wu)[n % 2][:, c, n // 2 * 128:(n // 2 + 1) * 128],
                                             xT[:, c].rearrange("p u s -> p (u s)"),
                                             start=(c == 0), stop=(c == KC - 1))
                        banks.fill_done(last, nm)
                    turn_norm(pe, k, ln, xb, i + 1)
                    taken_now = r.sel if E == 8 else taken
                    banks.wait_free(pe, "c", i)
                    pe.wait_ge(choices_ready, i + 1)
                    for u in range(2):
                        pe.matmul(banks.at("c", S, 2, E)[:, u, :], k.earlier[:], taken_now[:, u, :],
                                  start=True, stop=False)
                        last = pe.matmul(banks.at("c", S, 2, E)[:, u, :], k.ones[:], before[:, u, :],
                                         start=False, stop=True)
                    banks.fill_done(last, "c")
                    if shared is not None:
                        banks.wait_free(pe, "y", i, *[f"u{t}" for t in range(IT)])
                        for u in range(2):
                            for t in range(IT):
                                last = pe.matmul(banks.at("y", S, 2, D)[:, u, :], h[:, t, u * S:(u + 1) * S],
                                                 wd[:, t, :], start=(t == 0), stop=(t == IT - 1))
                        banks.fill_done(last, "y")
                if E == 8:
                    totals.wait_free(pe, "n", 0)
                    pe.wait_ge(choices_ready, TURNS + 1)
                    totals.fill_done(pe.matmul(totals.at("n", S, E), k.ones[:], before[:, 0, :],
                                               start=True, stop=True), "n")

            @block.scalar
            def _(act):
                def move_norm(t):
                    xb.wait_full(act, "xT", t)
                    last = act.activation(xT[:], xb.at("xT", 128, KC, 2, S), ACT.Copy)
                    if xall is not None:
                        last = act.activation(xall[:, :, bass.ds(t * 2, 2), :], xb.at("xT", 128, KC, 2, S), ACT.Copy)
                    xb.move_done(last, "xT")

                move_norm(0)
                with act.Fori(0, TURNS) as i:
                    act.wait_ge(act_asked, i + 1)
                    act.activation(expd[:], logits[:], ACT.Exp if E == 8 else ACT.Sigmoid).then_inc(act_done, 1)
                    for nm in widened[0::2]:
                        banks.wait_moved(act, i - 1, "u" + nm[1:])
                        banks.wait_full(act, nm, i)
                        banks.move_done(act.activation(gated[:, int(nm[1:]), :], banks.at(nm, 128, 2 * S), ACT.Silu), nm)
                    move_norm(i + 1)

            @block.vector
            def _(dve):
                first = Chain(sem("dve_first"), 1)
                ln.find(dve)
                ln.apply(dve, 0)
                dve.wait_ge(constants, 3)
                if E == 64:
                    dve.wait_ge(loaded, LOADED)
                first.link(dve, 0, dve.memset(before[:, 0, :], 0.0))
                with dve.Fori(0, TURNS) as i:
                    def link(ins):
                        chain.link(dve, i, ins)

                    if E == 8:
                        banks.wait_full(dve, "l", i)
                        banks.move_done(dve.tensor_copy(logits[:], banks.at("l", S, 2, E)), "l")
                        banks.wait_moved(dve, i, "l")
                        chosen_by_rank(link, dve, k, r, logits[:], 2)
                        dve.tensor_tensor(before[:, 1, :], before[:, 0, :], r.sel[:, 0, :], ALU.add)\
                           .then_inc(choices_ready, 1)
                        link(dve.tensor_reduce(top[:], logits[:], AX.X, ALU.max))
                        dve.tensor_tensor(logits[:], logits[:], top[:].unsqueeze(2).broadcast_to([S, 2, E]),
                                          ALU.subtract).then_inc(act_asked, 1)
                        ln.apply(dve, i + 1, stored)
                        banks.wait_full(dve, "c", i)
                        banks.move_done(dve.tensor_copy(places[:, bass.ds(2 * i, 2), :], banks.at("c", S, 2, E)), "c")
                        chain.done(dve.tensor_copy(chosen[:, bass.ds(2 * i, 2), :], r.sel[:]))
                        link(dve.tensor_tensor(before[:, 0, :], before[:, 1, :], r.sel[:, 1, :], ALU.add))
                        dve.wait_ge(act_done, i + 1)
                        link(dve.tensor_tensor(expd[:], expd[:], r.sel[:], ALU.mult))
                        link(dve.tensor_reduce(total[:], expd[:], AX.X, ALU.add))
                        link(dve.reciprocal(total[:], total[:]))
                        link(dve.tensor_tensor(comb[:, bass.ds(2 * i, 2), :], expd[:],
                                               total[:].unsqueeze(2).broadcast_to([S, 2, E]), ALU.mult))
                    else:
                        banks.wait_full(dve, "l", i)
                        banks.move_done(dve.tensor_copy(logits[:], banks.at("l", S, 2, E)), "l")
                        banks.wait_moved(dve, i, "l")
                        dve.sem_inc(act_asked, 1)
                        ln.apply(dve, i + 1, stored)
                        dve.wait_ge(act_done, i + 1)
                        wide = [S, 2, E]
                        link(dve.tensor_tensor(biased[:], expd[:], ebias[:].unsqueeze(1).broadcast_to(wide), ALU.add))
                        dve.sem_inc(passed, 1)
                        for u in range(2):
                            for g in range(GROUPS):
                                last = dve.max(best[:, u, g, :], biased[:, u, g * 8:(g + 1) * 8])
                        link(last)
                        link(dve.tensor_tensor(gscore[:], best[:, :, :, 0], best[:, :, :, 1], ALU.add))
                        chosen_by_rank(link, dve, k, r, gscore[:], 4)
                        link(dve.tensor_tensor(
                            masked[:].rearrange("p u (g e) -> p u g e", g=GROUPS),
                            biased[:].rearrange("p u (g e) -> p u g e", g=GROUPS),
                            r.sel[:].unsqueeze(3).broadcast_to([S, 2, GROUPS, 8]), ALU.mult))
                        link(dve.tensor_scalar(masked[:], masked[:], 0.0, None, ALU.add))
                        dve.sem_inc(passed, 1)
                        for u in range(2):
                            last = dve.max(best8[:, u, :], masked[:, u, :])
                        link(last)
                        dve.sem_inc(passed, 1)
                        for u in range(2):
                            last = dve.match_replace(left[:, u, :], best8[:, u, :], masked[:, u, :], -3.0e38)
                        link(last)
                        link(dve.tensor_scalar(taken[:], left[:], -1.0e38, None, ALU.is_lt))
                        dve.tensor_tensor(before[:, 1, :], before[:, 0, :], taken[:, 0, :], ALU.add)\
                           .then_inc(choices_ready, 1)
                        link(dve.tensor_tensor(expd[:], expd[:], taken[:], ALU.mult))
                        link(dve.tensor_reduce(total[:], expd[:], AX.X, ALU.add))
                        link(dve.tensor_scalar(total[:], total[:], 1e-20, None, ALU.add))
                        link(dve.reciprocal(total[:], total[:]))
                        link(dve.tensor_tensor(expd[:], expd[:], total[:].unsqueeze(2).broadcast_to(wide), ALU.mult))
                        banks.wait_full(dve, "c", i)
                        place = banks.at("c", S, 2, E)
                        link(dve.tensor_scalar(left[:], place, float(CAP), None, ALU.is_lt))
                        link(dve.tensor_scalar(late[:], place, float(CAP), DROPPED, ALU.is_ge, ALU.mult))
                        link(dve.tensor_scalar(masked[:], place, 128.0, -float(dispatch.places - 1), ALU.is_ge, ALU.mult))
                        banks.move_done(dve.tensor_scalar(key[:], place, float(CAP - 1), 128.0, ALU.min, ALU.mult), "c")
                        banks.wait_moved(dve, i, "c")
                        link(dve.tensor_tensor(key[:], key[:], row1[0:S].unsqueeze(1).broadcast_to(wide), ALU.add))
                        link(dve.tensor_tensor(late[:], late[:], masked[:], ALU.add))
                        link(dve.tensor_tensor(key[:], key[:], late[:], ALU.add))
                        link(dve.tensor_tensor(key[:], key[:], taken[:], ALU.mult))
                        link(dve.tensor_tensor(before[:, 0, :], before[:, 1, :], taken[:, 1, :], ALU.add))
                        link(dve.scalar_tensor_tensor(weight[:], expd[:], FACTOR, left[:], ALU.mult, ALU.mult))
                        dve.sem_inc(passed, 1)
                        for u in range(2):
                            last = dve.max(key8[:, u, :], key[:, u, :])
                        link(last)
                        full = [S, 2, TOP, E]
                        link(dve.tensor_tensor(match[:], key[:].unsqueeze(2).broadcast_to(full),
                                               key8[:].unsqueeze(3).broadcast_to(full), ALU.is_equal))
                        link(dve.tensor_tensor(match[:], match[:], weight[:].unsqueeze(2).broadcast_to(full), ALU.mult))
                        for t in range(IT):
                            banks.wait_moved(dve, i, f"g{t}")
                            banks.wait_full(dve, f"u{t}", i)
                            banks.move_done(dve.tensor_tensor(h[:, t, :], gated[:, t, :], banks.at(f"u{t}", 128, 2 * S),
                                                              ALU.mult), f"u{t}")
                        dve.wait_ge(rows_free, i + 1)
                        chain.done(dve.tensor_reduce(entries[:, :, :, 1], match[:], AX.X, ALU.add))
                        chain.done(dve.tensor_scalar(rows_now[:], key8[:], -1.0, None, ALU.add))
                        link(dve.tensor_scalar(entries[:].bitcast(I32)[:, :, :, 0],
                                               token_f[:].unsqueeze(2).broadcast_to([S, 2, TOP]), 0.0, None, ALU.add))
                        dve.sem_inc(rows_ready, 1)
                        banks.wait_full(dve, "y", i)
                        pair = bass.ds(2 * i, 2)
                        banks.move_done(dve.tensor_tensor(X[:, pair, :], X[:, pair, :], banks.at("y", S, 2, D),
                                                          ALU.add), "y")
                        link(dve.tensor_scalar(token_f[:], token_f[:], float(2 * S), None, ALU.add))
                    chain.end()
                if E == 8:
                    last_steps = Chain(sem("last_step"), 0)

                    def then(ins):
                        last_steps.link(dve, 0, ins)

                    dve.sem_inc(choices_ready, 1)
                    totals.wait_full(dve, "n", 0)
                    totals.move_done(dve.tensor_copy(counts[:], totals.at("n", S, E)), "n")
                    totals.wait_moved(dve, 0, "n")
                    span, pair = [S, E, FULL], [S, E, E]
                    then(dve.tensor_tensor(spans[:], counts[:].unsqueeze(2).broadcast_to(span),
                                           starts[:].unsqueeze(1).broadcast_to(span), ALU.is_gt))
                    then(dve.tensor_reduce(tiles[:], spans[:], AX.X, ALU.add))
                    then(dve.tensor_tensor(firsts[:], k.ahead[:], tiles[:].unsqueeze(1).broadcast_to(pair), ALU.mult))
                    then(dve.tensor_reduce(first_tile[:], firsts[:], AX.X, ALU.add))
                    then(dve.tensor_tensor(ends[:], first_tile[:], tiles[:], ALU.add))
                    slot = [S, TILES + 2, E]
                    then(dve.tensor_tensor(passed_by[:], tile_no[:].unsqueeze(2).broadcast_to(slot),
                                           ends[:].unsqueeze(1).broadcast_to(slot), ALU.is_ge))
                    then(dve.tensor_reduce(expert_f[:], passed_by[:], AX.X, ALU.add))
                    then(dve.tensor_scalar(dispatch.expert[:], expert_f[:], float(E - 1), None, ALU.min))
                    then(dve.tensor_scalar(offset[:], first_tile[:], 128.0, 1.0, ALU.mult, ALU.add))
                    wide = [S, B, E]
                    then(dve.tensor_tensor(keys[:], places[:], offset[:].unsqueeze(1).broadcast_to(wide), ALU.add))
                    then(dve.tensor_tensor(keys[:], keys[:], chosen[:], ALU.mult))
                    then(dve.tensor_reduce(high[:], keys[:], AX.X, ALU.max))
                    then(dve.tensor_reduce(low[:], keys[:], AX.X, ALU.add))
                    then(dve.tensor_tensor(low[:], low[:], high[:], ALU.subtract))
                    for n, key_of in enumerate((high, low)):
                        then(dve.tensor_tensor(match[:], keys[:], key_of[:].unsqueeze(2).broadcast_to(wide),
                                               ALU.is_equal))
                        then(dve.tensor_tensor(match[:], match[:], comb[:], ALU.mult))
                        then(dve.tensor_reduce(dispatch.entries[:, :, n, 1], match[:], AX.X, ALU.add))
                        then(dve.tensor_scalar(dispatch.send_row[:, :, n], key_of[:], -1.0, None, ALU.add))
        if E == 8:
            totals.done(1)
        xb.done(TURNS + 1)


def shared_expert(k, w, name, width, xall, beside=None):
    nc, X = k.nc, k.X
    IT = -(-width // 128)
    I = IT * 128
    NB = 4
    TURNS = B // NB
    with ExitStack() as ctx:
        def sb(n, shape):
            return ctx.enter_context(nc.sbuf_tensor(f"{name}_{n}", shape, F32))

        wg, wu, wd = sb("wg", [128, KC, I]), sb("wu", [128, KC, I]), sb("wd", [128, IT, D])
        gated, h = sb("gated", [128, IT, NB * S]), sb("h", [128, IT, NB * S])
        loaded = k.sem(f"{name}_loaded")
        names = [f"{a}{t}" for t in range(IT) for a in "gu"] + [f"y{n}" for n in range(NB // 2)]
        banks = Banks(k, 0, 8).plan(names)
        with nc.Block() as block:
            @block.sync
            def _(sp):
                sp.dma_start(wg[:], w["G"].rearrange("(c p) n -> p c n", p=128)).then_inc(loaded, 16)
                sp.dma_start(wu[:], w["U"].rearrange("(c p) n -> p c n", p=128)).then_inc(loaded, 16)
                sp.dma_start(wd[:], w["D"].rearrange("(t p) n -> p t n", p=128)).then_inc(loaded, 16)
                if beside is not None:
                    beside.sync(sp)

            @block.gpsimd
            def _(pool):
                if beside is not None:
                    beside.gpsimd(pool)

            @block.tensor
            def _(pe):
                pe.wait_ge(loaded, 48)
                with pe.Fori(0, TURNS) as j:
                    xs = [xall[:, c, bass.ds(j * NB, NB), :].rearrange("p b s -> p (b s)") for c in range(KC)]
                    for t in range(IT):
                        for nm, wt in (("g", wg), ("u", wu)):
                            banks.wait_free(pe, f"{nm}{t}", j)
                            for c in range(KC):
                                last = pe.matmul(banks.at(f"{nm}{t}", 128, NB * S), wt[:, c, t * 128:(t + 1) * 128],
                                                 xs[c], start=(c == 0), stop=(c == KC - 1))
                            banks.fill_done(last, f"{nm}{t}")
                    for n in range(NB // 2):
                        banks.wait_free(pe, f"y{n}", j, *[f"u{t}" for t in range(IT)])
                        for b in range(2):
                            for t in range(IT):
                                s0 = (2 * n + b) * S
                                last = pe.matmul(banks.at(f"y{n}", S, 2, D)[:, b, :], h[:, t, s0:s0 + S],
                                                 wd[:, t, :], start=(t == 0), stop=(t == IT - 1))
                        banks.fill_done(last, f"y{n}")

            @block.scalar
            def _(act):
                with act.Fori(0, TURNS) as j:
                    for t in range(IT):
                        banks.wait_full(act, f"g{t}", j)
                        banks.move_done(act.activation(gated[:, t, :], banks.at(f"g{t}", 128, NB * S), ACT.Silu),
                                        f"g{t}")

            @block.vector
            def _(dve):
                with dve.Fori(0, TURNS) as j:
                    for t in range(IT):
                        banks.wait_moved(dve, j, f"g{t}")
                        banks.wait_full(dve, f"u{t}", j)
                        banks.move_done(dve.tensor_tensor(h[:, t, :], gated[:, t, :],
                                                          banks.at(f"u{t}", 128, NB * S), ALU.mult), f"u{t}")
                    for n in range(NB // 2):
                        banks.wait_full(dve, f"y{n}", j)
                        at = j * NB + 2 * n
                        banks.move_done(dve.tensor_tensor(X[:, bass.ds(at, 2), :], X[:, bass.ds(at, 2), :],
                                                          banks.at(f"y{n}", S, 2, D), ALU.add), f"y{n}")
        banks.done(TURNS)


class Sending:
    NB = 4

    def __init__(self, k, sb, name, dispatch, wgu, w, gu_loaded):
        self.dispatch, self.wgu, self.w, self.gu_loaded = dispatch, wgu, w, gu_loaded
        self.rows_now = sb(name + "_rows_now", [S, self.NB, 2], I32)
        self.entries_now = sb(name + "_entries_now", [S, self.NB, 2, 2], F32)
        self.ready, self.sent, self.started = (k.sem(f"{name}_{n}") for n in ("ready", "sent", "started"))

    def sync(self, sp):
        for e in range(8):
            sp.dma_start(self.wgu[:, e, 0], self.w["G"][e].rearrange("(c p) n -> p c n", p=128))\
              .then_inc(self.gu_loaded, 16)
            sp.dma_start(self.wgu[:, e, 1], self.w["U"][e].rearrange("(c p) n -> p c n", p=128))\
              .then_inc(self.gu_loaded, 16)

    def gpsimd(self, pool):
        NB = self.NB
        d = self.dispatch
        for n in range(2):
            pool.iota(d.entries[:].bitcast(I32)[:, :, n, 0], pattern=[[S, B]], base=0, channel_multiplier=1)\
                .then_inc(self.ready, 1)
            pool.wait_ge(self.ready, n + 1)
        with pool.Fori(0, B // NB) as i:
            pool.tensor_copy(self.rows_now[:], d.send_row[:, bass.ds(i * NB, NB), :]).then_inc(self.ready, 1)
            pool.tensor_copy(self.entries_now[:].bitcast(I32), d.entries[:].bitcast(I32)[:, bass.ds(i * NB, NB)])\
                .then_inc(self.ready, 1)
            pool.wait_ge(self.ready, i * 2 + 4)
            pool.sem_inc(self.started, 1)
            for b in range(NB):
                for n in range(2):
                    pool.indirect_dma_start(
                        out=d.table, in_=self.entries_now[:, b, n, :].bitcast(I32), in_offset=None,
                        out_offset=bass.IndirectOffsetOnAxis(ap=self.rows_now[:, b, n:n + 1].bitcast(U32), axis=0),
                        bounds_check=d.places - 1, oob_is_err=False).then_inc(self.sent, 16)
            pool.wait_ge(self.sent, i * (2 * NB * 16) + 2 * NB * 16)
            pool.sem_inc(self.started, 1)


def sorted_experts(k, w, name, dispatch, wgu, gu_loaded):
    nc, X = k.nc, k.X
    TURNS = TILES + 1
    assert TURNS % 2 == 0
    WIDTH = 704
    HALF = WIDTH // 2
    IT = -(-WIDTH // 128)
    with ExitStack() as ctx:
        def sb(n, shape, dt=F32):
            return ctx.enter_context(nc.sbuf_tensor(f"{name}_{n}", shape, dt))

        def sem(n):
            return k.sem(f"{name}_{n}")

        wd = sb("wd", [128, 8, IT, D])
        table_rows = sb("table_rows", [SLOTS, 128, 2], I32)
        token_f, weight_f = sb("token_f", [SLOTS, 128]), sb("weight_f", [SLOTS, 128])
        token, weight = sb("token", [128, SLOTS + 1], I32), sb("weight", [128, SLOTS + 1])
        token_now, y_token_now = sb("token_now", [128, 2], I32), sb("y_token_now", [128, 2], I32)
        xg, xT = sb("xg", [128, 2, D]), sb("xT", [128, KC, 128])
        gated, h, hT = sb("gated", [128, 2, HALF]), sb("h", [128, IT * 128]), sb("hT", [128, IT, 128])
        y = sb("y", [128, 2, D])
        tokens_loaded, d_loaded, converted = sem("tokens_loaded"), sem("d_loaded"), sem("converted")
        cleared, token_ready, started = sem("cleared"), sem("token_ready"), sem("started")
        gathered = [sem(f"gathered{v}") for v in range(2)]
        added, y_free, x_moved = [sem(f"added{v}") for v in range(2)], sem("y_free"), sem("x_moved")
        table = Banks(k, 7, 1).plan(["table"])
        table.done(1)
        banks = Banks(k, 0, 6).plan(["g0", "g1", "t0", "t1", "u0", "u1"])
        xb, yb = Banks(k, 6, 1).plan(["x"]), Banks(k, 7, 1).plan(["y"])
        with nc.Block() as block:
            @block.sync
            def _(sp):
                sp.dma_start(table_rows[:], dispatch.table.rearrange("(t p) o -> t p o", p=128))\
                  .then_inc(tokens_loaded, 16)
                sp.wait_ge(token_ready, 3)
                for e in range(8):
                    sp.dma_start(wd[:, e], w["D"][e].rearrange("(t p) n -> p t n", p=128)).then_inc(d_loaded, 16)
                x_rows = dispatch.x_rows.rearrange("(b s) d -> s b d", s=S)
                sp.dma_start(x_rows, X[:, 0:B]).then_inc(x_moved, 16)
                sp.wait_ge(x_moved, 16)
                sp.wait_ge(y_free, TURNS + 2)
                sp.dma_start(X[:, 0:B], x_rows).then_inc(x_moved, 16)
                sp.wait_ge(x_moved, 32)

            @block.gpsimd
            def _(pool):
                pool.memset(xg[:], 0.0).then_inc(cleared, 1)
                pool.memset(h[:], 0.0).then_inc(cleared, 1)
                pool.memset(token[:, 0:1], NO_TOKEN).then_inc(cleared, 1)
                pool.memset(weight[:, 0:1], 0.0).then_inc(cleared, 1)
                pool.wait_ge(cleared, 4)
                pool.wait_ge(converted, 3)
                pool.sem_inc(y_free, 2)

                def gather(t, v, adds):
                    xb.wait_full(pool, "x", t - 2)
                    pool.sem_inc(started, 1)
                    pool.tensor_copy(token_now[:, v:v + 1], token[:, bass.ds(t + 1, 1)]).then_inc(token_ready, 1)
                    pool.wait_ge(token_ready, adds + t + 1)
                    pool.sem_inc(started, 1)
                    pool.indirect_dma_start(
                        out=xg[:, v, :], out_offset=None, in_=dispatch.xn,
                        in_offset=bass.IndirectOffsetOnAxis(ap=token_now[:, v:v + 1].bitcast(U32), axis=0),
                        bounds_check=B * S - 1, oob_is_err=False).then_inc(gathered[v], 16)

                for v in range(2):
                    gather(v, v, 0)
                with pool.Fori(0, TURNS // 2) as m:
                    for v in range(2):
                        j = 2 * m + v
                        pool.tensor_copy(y_token_now[:, v:v + 1], token[:, bass.ds(j, 1)]).then_inc(token_ready, 1)
                        gather(j + 2, v, j + 1)
                        yb.wait_moved(pool, j, "y")
                        pool.wait_ge(x_moved, 16)
                        pool.sem_inc(started, 1)
                        pool.indirect_dma_start(
                            out=dispatch.x_rows, in_=y[:, v, :], in_offset=None,
                            out_offset=bass.IndirectOffsetOnAxis(ap=y_token_now[:, v:v + 1].bitcast(U32), axis=0),
                            bounds_check=B * S - 1, oob_is_err=False, compute_op=ALU.add).then_inc(added[v], 16)
                        pool.wait_ge(added[v], m * 16 + 16)
                        pool.sem_inc(y_free, 1)
                for v in range(2):
                    pool.wait_ge(gathered[v], (TURNS // 2 + 1) * 16)

            @block.tensor
            def _(pe):
                table.wait_free(pe, "table", 0)
                pe.wait_ge(converted, 2)
                for n, rows in enumerate((token_f, weight_f)):
                    last = pe.transpose(table.at("table", 128, 2, SLOTS)[:, n, :], rows[:],
                                        k.ident[0:SLOTS, 0:SLOTS])
                table.fill_done(last, "table")

                def turn_x(t, v, gathers):
                    xb.wait_free(pe, "x", t)
                    pe.wait_ge(gathered[v], gathers * 16)
                    for c in range(KC):
                        last = pe.transpose(xb.at("x", 128, KC, 128)[:, c, :], xg[:, v, c * 128:(c + 1) * 128],
                                            k.ident[:])
                    xb.fill_done(last, "x")

                turn_x(0, 0, 1)
                pe.wait_ge(cleared, 4)
                pe.wait_ge(gu_loaded, 2 * 8 * 16)
                with pe.Fori(0, TURNS // 2) as m:
                    for v in range(2):
                        j = 2 * m + v
                        before = pe.value_load(dispatch.expert[0:1, bass.ds(j, 1)], min_val=0, max_val=7)
                        now = pe.value_load(dispatch.expert[0:1, bass.ds(j + 1, 1)], min_val=0, max_val=7)

                        def widen(a, what):
                            for s in range(2):
                                banks.wait_free(pe, f"{a}{s}", j)
                                if a == "g" and s == 0:
                                    xb.wait_moved(pe, j, "x")
                                for c in range(KC):
                                    last = pe.matmul(banks.at(f"{a}{s}", 128, HALF), xT[:, c, :],
                                                     wgu[:, bass.ds(now, 1), what, c, s * HALF:(s + 1) * HALF]
                                                     .rearrange("p o n -> p (o n)"),
                                                     start=(c == 0), stop=(c == KC - 1))
                                banks.fill_done(last, f"{a}{s}")

                        widen("g", 0)
                        for s, ts in enumerate((range(4), range(4, IT))):
                            banks.wait_free(pe, f"t{s}", j)
                            if s == 0:
                                banks.wait_moved(pe, j - 1, "u0", "u1")
                            for n, t in enumerate(ts):
                                last = pe.transpose(banks.at(f"t{s}", 128, len(ts), 128)[:, n, :],
                                                    h[:, t * 128:(t + 1) * 128], k.ident[:])
                            banks.fill_done(last, f"t{s}")
                        widen("u", 1)
                        turn_x(j + 1, (v + 1) % 2, m + (v + 1))
                        yb.wait_free(pe, "y", j)
                        banks.wait_moved(pe, j, "t0", "t1")
                        pe.wait_ge(d_loaded, 8 * 16)
                        for t in range(IT):
                            last = pe.matmul(yb.at("y", 128, D), hT[:, t, :],
                                             wd[:, bass.ds(before, 1), t, :].rearrange("p o n -> p (o n)"),
                                             start=(t == 0), stop=(t == IT - 1))
                        yb.fill_done(last, "y")

            @block.scalar
            def _(act):
                def move_x(t):
                    xb.wait_full(act, "x", t)
                    xb.move_done(act.activation(xT[:], xb.at("x", 128, KC, 128), ACT.Copy), "x")

                move_x(0)
                with act.Fori(0, TURNS // 2) as m:
                    for v in range(2):
                        j = 2 * m + v
                        for s in range(2):
                            banks.wait_moved(act, j - 1, f"u{s}")
                            banks.wait_full(act, f"g{s}", j)
                            banks.move_done(act.activation(gated[:, s, :], banks.at(f"g{s}", 128, HALF), ACT.Silu),
                                            f"g{s}")
                        banks.wait_full(act, "t0", j)
                        banks.move_done(act.activation(hT[:, 0:4, :], banks.at("t0", 128, 4, 128), ACT.Copy), "t0")
                        move_x(j + 1)

            @block.vector
            def _(dve):
                dve.wait_ge(tokens_loaded, 16)
                dve.tensor_copy(token_f[:], table_rows[:, :, 0]).then_inc(converted, 1)
                dve.tensor_copy(weight_f[:], table_rows[:].bitcast(F32)[:, :, 1]).then_inc(converted, 1)
                table.wait_full(dve, "table", 0)
                dve.wait_ge(cleared, 4)
                turned = table.at("table", 128, 2, SLOTS)
                dve.tensor_copy(token[:, 1:], turned[:, 0, :]).then_inc(converted, 1)
                table.move_done(dve.tensor_copy(weight[:, 1:], turned[:, 1, :]), "table")
                table.wait_moved(dve, 0, "table")
                with dve.Fori(0, TURNS // 2) as m:
                    for v in range(2):
                        j = 2 * m + v
                        banks.wait_full(dve, "t1", j)
                        banks.move_done(dve.tensor_copy(hT[:, 4:IT, :], banks.at("t1", 128, IT - 4, 128)), "t1")
                        for s in range(2):
                            banks.wait_moved(dve, j, f"g{s}")
                            banks.wait_full(dve, f"u{s}", j)
                            banks.move_done(dve.tensor_tensor(h[:, s * HALF:(s + 1) * HALF], gated[:, s, :],
                                                              banks.at(f"u{s}", 128, HALF), ALU.mult), f"u{s}")
                        dve.wait_ge(y_free, j + 1)
                        yb.wait_full(dve, "y", j)
                        yb.move_done(dve.tensor_scalar(y[:, v, :], yb.at("y", 128, D), weight[:, bass.ds(j, 1)],
                                                       None, ALU.mult), "y")
        banks.done(TURNS)
        xb.done(TURNS + 1)
        yb.done(TURNS)


def gathered_experts(k, w, name, dispatch):
    nc, X = k.nc, k.X
    Q = 4
    E = 64
    TURNS = E // Q
    NW = 2 * KC * 128 + D
    with ExitStack() as ctx:
        def sb(n, shape, dt=F32):
            return ctx.enter_context(nc.sbuf_tensor(f"{name}_{n}", shape, dt))

        def sem(n):
            return k.sem(f"{name}_{n}")

        wt = sb("w", [128, Q, NW])
        table = sb("table", [128, E * 2, 2], I32)
        token_now, y_token_now = sb("token_now", [128, Q, 2], I32), sb("y_token_now", [128, Q, 2], I32)
        xg = sb("xg", [128, Q, 2, D])
        xT = sb("xT", [128, Q, KC, 256])
        gated, h = sb("gated", [128, Q, 256]), sb("h", [128, Q, 256])
        y = sb("y", [128, Q, 2, D])
        tokens_loaded, cleared, tokens_ready = sem("tokens_loaded"), sem("cleared"), sem("tokens_ready")
        w_loaded = [sem(f"w_loaded{q}") for q in range(Q)]
        gathered = [sem(f"gathered{q}") for q in range(Q)]
        added, y_free, x_stored = [sem(f"added{q}") for q in range(Q)], sem("y_free"), sem("x_stored")
        silu_done, started = sem("silu_done"), sem("started")
        banks = Banks(k, 0, 8)
        names = [f"{a}{q}" for a in "xgy" for q in range(Q)]
        banks.plan(names)
        ident = k.ident
        with nc.Block() as block:
            @block.sync
            def _(sp):
                sp.dma_start(table[:], dispatch.table.rearrange("(p n) o -> p n o", p=128)).then_inc(tokens_loaded, 16)
                for q in range(Q):
                    sp.dma_start(wt[:, q], w["all"][q]).then_inc(w_loaded[q], 16)
                sp.wait_ge(tokens_ready, Q)
                sp.dma_start(dispatch.x_rows.rearrange("(b s) d -> s b d", s=S), X[:, 0:B]).then_inc(x_stored, 16)
                sp.wait_ge(x_stored, 16)
                with sp.Fori(0, TURNS - 1) as i:
                    for q in range(Q):
                        banks.wait_full(sp, f"y{q}", i)
                        sp.dma_start(wt[:, q], w["all"][i * Q + (Q + q)]).then_inc(w_loaded[q], 16)

            @block.gpsimd
            def _(pool):
                pool.memset(xg[:], 0.0).then_inc(cleared, 1)
                pool.wait_ge(cleared, 1)
                pool.wait_ge(tokens_loaded, 16)
                pool.sem_inc(y_free, Q)

                def take_tokens(i, q, to, count):
                    pool.tensor_copy(to[:, q, :], table[:, bass.ds(i * (2 * Q) + 2 * q, 2), 0]).then_inc(tokens_ready, 1)
                    pool.wait_ge(tokens_ready, count)
                    pool.sem_inc(started, 1)

                def gather(q):
                    for half in range(2):
                        pool.indirect_dma_start(
                            out=xg[:, q, half, :], out_offset=None, in_=dispatch.xn,
                            in_offset=bass.IndirectOffsetOnAxis(ap=token_now[:, q, half:half + 1].bitcast(U32), axis=0),
                            bounds_check=B * S - 1, oob_is_err=False).then_inc(gathered[q], 16)

                def add(i, q):
                    banks.wait_moved(pool, i, f"y{q}")
                    pool.sem_inc(started, 1)
                    for half in range(2):
                        pool.indirect_dma_start(
                            out=dispatch.x_rows, in_=y[:, q, half, :], in_offset=None,
                            out_offset=bass.IndirectOffsetOnAxis(ap=y_token_now[:, q, half:half + 1].bitcast(U32), axis=0),
                            bounds_check=B * S - 1, oob_is_err=False, compute_op=ALU.add).then_inc(added[q], 16)

                def add_done(i, q):
                    pool.wait_ge(added[q], i * 32 + 32)
                    pool.sem_inc(y_free, 1)

                def turn(i, adds):
                    for q in range(Q):
                        if adds:
                            take_tokens(i - 1, q, y_token_now, i * (2 * Q) + (2 * q + 1))
                            add(i - 1, q)
                        banks.wait_full(pool, f"x{q}", i)
                        pool.sem_inc(started, 1)
                        take_tokens(i + 1, q, token_now, i * (2 * Q) + (2 * q + 2) if adds else Q + q + 1)
                        gather(q)
                        if adds:
                            add_done(i - 1, q)
                            pool.sem_inc(started, 1)

                for q in range(Q):
                    take_tokens(0, q, token_now, q + 1)
                    gather(q)
                turn(0, adds=False)
                pool.wait_ge(x_stored, 16)
                with pool.Fori(1, TURNS - 1) as i:
                    turn(i, adds=True)
                for n, i in enumerate((TURNS - 2, TURNS - 1)):
                    for q in range(Q):
                        take_tokens(i, q, y_token_now, (TURNS - 1) * (2 * Q) + n * Q + q + 1)
                        add(i, q)
                        add_done(i, q)

            @block.tensor
            def _(pe):
                with pe.Fori(0, TURNS) as i:
                    for q in range(Q):
                        banks.wait_free(pe, f"x{q}", i)
                        pe.wait_ge(gathered[q], i * 32 + 32)
                        for c in range(KC):
                            for half in range(2):
                                last = pe.transpose(banks.at(f"x{q}", 128, KC, 2, 128)[:, c, half, :],
                                                    xg[:, q, half, c * 128:(c + 1) * 128], ident[:])
                        banks.fill_done(last, f"x{q}")
                    for q in range(Q):
                        banks.wait_free(pe, f"g{q}", i, f"x{q}")
                        pe.wait_ge(w_loaded[q], i * 16 + 16)
                        for m in range(2):
                            for c in range(KC):
                                at = (m * KC + c) * 128
                                last = pe.matmul(banks.at(f"g{q}", 128, 2, 256)[:, m, :], wt[:, q, at:at + 128],
                                                 xT[:, q, c, :], start=(c == 0), stop=(c == KC - 1))
                        banks.fill_done(last, f"g{q}")
                    for q in range(Q):
                        banks.wait_free(pe, f"y{q}", i, f"g{q}")
                        for half in range(2):
                            last = pe.matmul(banks.at(f"y{q}", 128, 2, D)[:, half, :],
                                             h[:, q, half * 128:(half + 1) * 128], wt[:, q, NW - D:NW],
                                             start=True, stop=True)
                        banks.fill_done(last, f"y{q}")

            @block.scalar
            def _(act):
                with act.Fori(0, TURNS) as i:
                    for q in range(Q):
                        banks.wait_full(act, f"x{q}", i)
                        banks.move_done(act.activation(xT[:, q], banks.at(f"x{q}", 128, KC, 256), ACT.Copy), f"x{q}")
                    for q in range(Q):
                        banks.wait_full(act, f"g{q}", i)
                        act.activation(gated[:, q, :], banks.at(f"g{q}", 128, 2, 256)[:, 0, :], ACT.Silu)\
                           .then_inc(silu_done, 1)

            @block.vector
            def _(dve):
                dve.wait_ge(tokens_loaded, 16)
                with dve.Fori(0, TURNS) as i:
                    for q in range(Q):
                        dve.wait_ge(silu_done, i * Q + (q + 1))
                        banks.move_done(dve.tensor_tensor(h[:, q, :], gated[:, q, :],
                                                          banks.at(f"g{q}", 128, 2, 256)[:, 1, :], ALU.mult), f"g{q}")
                    for q in range(Q):
                        dve.wait_ge(y_free, i * Q + (q + 1))
                        banks.wait_full(dve, f"y{q}", i)
                        for half in range(2):
                            last = dve.tensor_scalar(
                                y[:, q, half, :], banks.at(f"y{q}", 128, 2, D)[:, half, :],
                                table[:].bitcast(F32)[:, bass.ds(i * (2 * Q) + (2 * q + half), 1), 1], None, ALU.mult)
                        banks.move_done(last, f"y{q}")
        banks.done(TURNS)


def layer0_mixture(k, gate, shared, routed):
    nc = k.nc
    with ExitStack() as stage:
        def sb(n, shape, dt=F32):
            return stage.enter_context(nc.sbuf_tensor(n, shape, dt))

        d = Dispatch(k, "c", SLOTS * 128, nc.dram_tensor("c_x_rows", (B * S, D), F32).ap())
        d.entries = sb("c_entries", [S, B, 2, 2])
        d.send_row = sb("c_send_row", [S, B, 2], I32)
        d.expert = sb("c_expert", [S, TILES + 2], I32)
        gu_loaded = k.sem("c_gu_loaded")
        with ExitStack() as with_x:
            wgu = with_x.enter_context(nc.sbuf_tensor("c_wgu", [128, 8, 2, KC, 704], F32))
            with nc.sbuf_tensor("c_xall", [128, KC, B + 2, S], F32) as xall:
                route(k, gate, "c_gate", 8, xall, d)
                with ExitStack() as small:
                    def sb2(n, shape, dt=F32):
                        return small.enter_context(nc.sbuf_tensor(n, shape, dt))

                    shared_expert(k, shared, "c_shared", 352, xall,
                                  Sending(k, sb2, "c_sending", d, wgu, routed, gu_loaded))
            sorted_experts(k, routed, "c_routed", d, wgu, gu_loaded)


def layer1_mixture(k, gate, shared, routed, out):
    d = Dispatch(k, "f", 64 * 256, out.rearrange("b s d -> (b s) d"))
    route(k, gate, "f_gate", 64, None, d, shared)
    gathered_experts(k, routed, "f_experts", d)


def decoder(nc, w, x, ctx_T, out):
    with ExitStack() as ctx:
        def sem(name):
            return ctx.enter_context(nc.semaphore(name))

        k = Shared(nc, sem)
        k.X = ctx.enter_context(nc.sbuf_tensor("X", [S, B + 2, D], F32))
        k.ident = ctx.enter_context(nc.sbuf_tensor("ident", [128, 128], F32))
        k.causal = ctx.enter_context(nc.sbuf_tensor("causal", [S, S], F32))
        k.PS = ctx.enter_context(nc.psum_tensor("PS", [128, 8, 512], F32))
        k.filled, k.moved = [sem(f"bank{b}_filled") for b in range(8)], [sem(f"bank{b}_moved") for b in range(8)]
        k.uses = [0] * 8
        k.keep = ctx.enter_context(nc.sbuf_tensor("keep", [S, S], F32))
        k.earlier = ctx.enter_context(nc.sbuf_tensor("earlier", [S, S], F32))
        k.ones = ctx.enter_context(nc.sbuf_tensor("ones", [S, S], F32))
        k.ahead = ctx.enter_context(nc.sbuf_tensor("ahead", [S, 8, 8], F32))
        k.one_rows = ctx.enter_context(nc.sbuf_tensor("one_rows", [128, 8], F32))
        k.quarter_rows = ctx.enter_context(nc.sbuf_tensor("quarter_rows", [128, 8], F32))
        k.half = ctx.enter_context(nc.sbuf_tensor("minus_half", [S, 2], F32))
        x_loaded, made = sem("x_loaded"), sem("constants_made")
        k.x, k.x_rest_loaded = x, sem("x_rest_loaded")

        with nc.Block() as block:
            @block.sync
            def _(sp):
                sp.dma_start(k.X[:, 0:2], k.x[0:2].rearrange("b s d -> s b d")).then_inc(x_loaded, 16)
                sp.wait_ge(x_loaded, 16)

            @block.gpsimd
            def _(pool):
                for moved in k.moved:
                    pool.sem_inc(moved, 1)
                pool.memset(k.X[:, B:B + 2], 0.0).then_inc(made, 1)
                pool.memset(k.half[:], -0.5).then_inc(made, 1)
                pool.memset(k.ident[:], 0.0).then_inc(made, 1)
                pool.memset(k.causal[:], 3.0e38).then_inc(made, 1)
                for t in (k.keep, k.earlier, k.ones, k.ahead):
                    pool.memset(t[:], 1.0).then_inc(made, 1)
                pool.wait_ge(made, 8)
                pool.memset(k.one_rows[:], 1.0).then_inc(made, 1)
                pool.memset(k.quarter_rows[:], 16 ** -0.5).then_inc(made, 1)
                pool.wait_ge(made, 10)
                for n, t in enumerate((k.one_rows, k.quarter_rows)):
                    pool.affine_select(out=t[:], in_=t[:], compare_op=ALU.is_ge, fill=0.0,
                                       base=0, pattern=[[-16, 8]], channel_multiplier=1).then_inc(made, 1)
                    pool.wait_ge(made, 11 + 2 * n)
                    pool.affine_select(out=t[:], in_=t[:], compare_op=ALU.is_ge, fill=0.0,
                                       base=15, pattern=[[16, 8]], channel_multiplier=-1).then_inc(made, 1)
                pool.affine_select(out=k.keep[:], in_=k.keep[:], compare_op=ALU.is_ge, fill=0.0,
                                   base=0, pattern=[[1, S]], channel_multiplier=-1).then_inc(made, 1)
                pool.affine_select(out=k.earlier[:], in_=k.earlier[:], compare_op=ALU.is_gt, fill=0.0,
                                   base=0, pattern=[[1, S]], channel_multiplier=-1).then_inc(made, 1)
                pool.affine_select(out=k.ahead[:], in_=k.ahead[:], compare_op=ALU.is_gt, fill=0.0,
                                   base=0, pattern=[[1, 8], [-1, 8]], channel_multiplier=0).then_inc(made, 1)
                pool.affine_select(out=k.ident[:], in_=k.ident[:], compare_op=ALU.not_equal, fill=1.0,
                                   base=0, pattern=[[-1, 128]], channel_multiplier=1).then_inc(made, 1)
                pool.affine_select(out=k.causal[:], in_=k.causal[:], compare_op=ALU.is_ge, fill=MASKED,
                                   base=0, pattern=[[-1, S]], channel_multiplier=1).then_inc(made, 1)
                pool.wait_ge(made, 19)

        k.ctx_T = ctx_T
        self_attention(k, w["L0_attn"])
        cross_attention(k, w["L0_xattn"], "b", 16, 16 ** -0.5)
        layer0_mixture(k, w["L0_gate"], w["L0_shared"], w["L0_experts"])
        linear_attention(k, w["L1_attn"])
        cross_attention(k, w["L1_xattn"], "e", 64, 64 ** -0.5)
        layer1_mixture(k, w["L1_gate"], w["L1_shared"], w["L1_experts"], out)


def kernel(**inputs):
    import numpy as np
    import concourse.bacc as bacc
    from concourse.bass_utils import run_bass_kernel_spmd

    nc = bacc.Bacc("TRN2", target_bir_lowering=False, num_devices=1)
    arrays, w = {}, {}

    def give(name, a):
        a = np.ascontiguousarray(a)
        arrays["in_" + name] = a
        return nc.dram_tensor("in_" + name, a.shape, mybir.dt.from_np(a.dtype), kind="ExternalInput").ap()

    def heads_last(a):
        return np.transpose(a, (1, 0, 2)).reshape(a.shape[1], -1)

    def rows(a):
        return a.reshape(-1, 128).T

    I = {n: np.asarray(a) for n, a in inputs.items()}
    x = give("x", I["x"])
    ctx_T = give("ctx_T", np.pad(np.transpose(I["ctx_512"], (0, 2, 1)), ((0, 0), (0, 0), (0, 2))))
    w["L0_attn"] = dict(
        Wq=give("a_Wq", heads_last(I["L0_attn_Wq"])), Wk=give("a_Wk", heads_last(I["L0_attn_Wk"])),
        Wv=give("a_Wv", heads_last(I["L0_attn_Wv"])), Wo=give("a_Wo", I["L0_attn_Wo"].reshape(H * 64, D)),
        bq=give("a_bq", rows(I["L0_attn_bq"])), bk=give("a_bk", rows(I["L0_attn_bk"])),
        bv=give("a_bv", I["L0_attn_bv"].reshape(-1)), bo=give("a_bo", I["L0_attn_bo"]))
    w["L0_xattn"] = dict(
        Wq=give("b_Wq", I["L0_xattn_Wq"].T), Wk=give("b_Wk", I["L0_xattn_Wkv"][0:D].T),
        Wv=give("b_Wv", I["L0_xattn_Wkv"][D:2 * D].T), Wo=give("b_Wo", I["L0_xattn_Wo"].T), bo=None)
    w["L1_xattn"] = dict(
        bo=give("e_bo", I["L1_xattn_bo"]),
        WqT=give("e_WqT", I["L1_xattn_Wq"].T), WkT=give("e_WkT", I["L1_xattn_Wk"].T),
        Wv=give("e_Wv", I["L1_xattn_Wv"]), Wo=give("e_Wo", I["L1_xattn_Wo"]))
    def columns(a, n):
        return np.pad(a, [(0, 0)] * (a.ndim - 1) + [(0, n - a.shape[-1])])

    def turned(a):
        return np.swapaxes(a, -1, -2)

    W1, b1 = I["L1_attn_W1"], I["L1_attn_b1"]
    w["L1_attn"] = dict(
        Wk=give("d_Wk", W1[:, 0:D]), Wq=give("d_Wq", W1[:, D:2 * D]),
        Wv=give("d_Wv", W1[:, 2 * D:]), Wo=give("d_Wo", I["L1_attn_W2"]),
        bk=give("d_bk", rows(b1[0:D])), bq=give("d_bq", rows(b1[D:2 * D])),
        bv=give("d_bv", b1[2 * D:]), bo=give("d_bo", I["L1_attn_b2"]))
    w["L0_gate"] = dict(gate=give("c_gate", I["L0_ffn_gate_w"]))
    w["L0_experts"] = dict(
        G=give("c_G", I["L0_ffn_Wg"]), U=give("c_U", I["L0_ffn_Wu"]),
        D=give("c_D", turned(columns(turned(I["L0_ffn_Wd"]), 768))))
    w["L0_shared"] = dict(
        G=give("c_SG", columns(I["L0_ffn_Sg"], 384)), U=give("c_SU", columns(I["L0_ffn_Su"], 384)),
        D=give("c_SD", turned(columns(turned(I["L0_ffn_Sd"]), 384))))
    w["L1_gate"] = dict(gate=give("f_gate", I["L1_ffn_gate_weight"].T), ebias=give("f_ebias", I["L1_ffn_e_bias"]))

    def in_rows(a):
        return np.swapaxes(a.reshape(a.shape[0], -1, 128, a.shape[-1]), 1, 2).reshape(a.shape[0], 128, -1)

    w["L1_experts"] = dict(all=give("f_W", np.concatenate(
        [in_rows(turned(I["L1_ffn_w1"])), in_rows(turned(I["L1_ffn_w3"])), in_rows(turned(I["L1_ffn_w2"]))], axis=-1)))
    w["L1_shared"] = dict(
        G=give("f_SG", I["L1_ffn_shared_gate"].T), U=give("f_SU", I["L1_ffn_shared_up"].T),
        D=give("f_SD", I["L1_ffn_shared_down"].T))
    out = nc.dram_tensor("out", (B, S, D), F32, kind="ExternalOutput").ap()
    decoder(nc, w, x, ctx_T, out)
    r = run_bass_kernel_spmd(nc, [arrays], core_ids=[0])
    return r.results[0]["out"]
```
